# Optimizing a Trainium2 kernel written in Bass

```python
import numpy as np
import jax
import jax.numpy as jnp

def _softmax(x, axis=-1):
    return jax.nn.softmax(x, axis=axis)

def _gelu(x):
    return jax.nn.gelu(x, approximate=True)

def _silu(x):
    return jax.nn.silu(x)

def _sigmoid(x):
    return jax.nn.sigmoid(x)

def _layernorm(x, axis=-1, eps=1e-05):
    m = jnp.mean(x, axis=axis, keepdims=True)
    v = jnp.var(x, axis=axis, keepdims=True)
    return (x - m) / jnp.sqrt(v + eps)

def _scatter_add(tgt, idx, src, axis=0):
    return tgt.at[idx].add(src)

def _segment_sum(src, seg, n):
    return jax.ops.segment_sum(src, seg, n)
kernel_name = 'mk_seq_preln_d1_jaxref_r8_cea732'

def setup_inputs(seed: int=0):
    np.random.seed(seed)
    _w = jnp.asarray

    def _L0_attn_setup():
        import jax, jax.numpy as jnp
        import numpy as np
        DIM = 128
        H = 16
        HD = DIM // H
        R = 8
        QK = 32
        B = 4
        S = 128
        EPS = 1e-05

        def _lin(x, W, b):
            return x @ W.T + b

        def _ln(x, g, b):
            m = x.mean(-1, keepdims=True)
            v = ((x - m) ** 2).mean(-1, keepdims=True)
            return (x - m) / jnp.sqrt(v + EPS) * g + b
        key = jax.random.key(seed)
        ks = iter(jax.random.split(key, 32))

        def w(shape, fan):
            s = 1.0 / np.sqrt(fan)
            return jax.random.uniform(next(ks), shape, jnp.float32, -s, s)
        d = {}
        d['x'] = jax.random.normal(next(ks), (B, S, DIM), jnp.float32)
        d['Wq'] = w((DIM, DIM), DIM)
        d['bq'] = w((DIM,), DIM)
        d['Wk'] = w((DIM, DIM), DIM)
        d['bk'] = w((DIM,), DIM)
        d['Wv'] = w((HD * R, DIM), DIM)
        d['bv'] = w((HD * R,), DIM)
        d['Wqv'] = w((QK * H, DIM), DIM)
        d['bqv'] = w((QK * H,), DIM)
        d['Ws'] = w((1, HD + QK), HD + QK)
        d['bs'] = w((1,), HD + QK)
        d['Wf'] = w((DIM, DIM), DIM)
        d['bf'] = w((DIM,), DIM)
        d['Wr1'] = w((2 * DIM, DIM), DIM)
        d['br1'] = w((2 * DIM,), DIM)
        d['Wr2'] = w((DIM, 2 * DIM), 2 * DIM)
        d['br2'] = w((DIM,), 2 * DIM)
        d['g1'] = jnp.ones((DIM,), jnp.float32)
        d['b1'] = jnp.zeros((DIM,), jnp.float32)
        d['g2'] = jnp.ones((DIM,), jnp.float32)
        d['b2'] = jnp.zeros((DIM,), jnp.float32)
        return d
    _L0_attn_in = _L0_attn_setup()

    def _L0_ffn_setup():
        import jax, jax.numpy as jnp
        import numpy as np
        EMB = 128
        FF = 4 * EMB

        def _ternary(w):
            scale = jnp.maximum(jnp.mean(jnp.abs(w)), 1e-08)
            w_t = jnp.clip(jnp.round(w / scale), -1.0, 1.0)
            return w + jax.lax.stop_gradient(w_t - w)
        key = jax.random.key(seed)
        kx, k1, k2, kb1, kb2 = jax.random.split(key, 5)
        x = jax.random.normal(kx, (4, 256, EMB), dtype=jnp.float32)
        lim1 = 1.0 / np.sqrt(EMB)
        lim2 = 1.0 / np.sqrt(FF)
        W1 = jax.random.uniform(k1, (FF, EMB), jnp.float32, -lim1, lim1)
        b1 = jax.random.uniform(kb1, (FF,), jnp.float32, -lim1, lim1)
        W2 = jax.random.uniform(k2, (EMB, FF), jnp.float32, -lim2, lim2)
        b2 = jax.random.uniform(kb2, (EMB,), jnp.float32, -lim2, lim2)
        return {'x': x, 'W1': W1, 'b1': b1, 'W2': W2, 'b2': b2}
    _L0_ffn_in = _L0_ffn_setup()
    _d = {'L0_attn_x': _L0_attn_in['x'], 'L0_attn_Wq': _L0_attn_in['Wq'], 'L0_attn_bq': _L0_attn_in['bq'], 'L0_attn_Wk': _L0_attn_in['Wk'], 'L0_attn_bk': _L0_attn_in['bk'], 'L0_attn_Wv': _L0_attn_in['Wv'], 'L0_attn_bv': _L0_attn_in['bv'], 'L0_attn_Wqv': _L0_attn_in['Wqv'], 'L0_attn_bqv': _L0_attn_in['bqv'], 'L0_attn_Ws': _L0_attn_in['Ws'], 'L0_attn_bs': _L0_attn_in['bs'], 'L0_attn_Wf': _L0_attn_in['Wf'], 'L0_attn_bf': _L0_attn_in['bf'], 'L0_attn_Wr1': _L0_attn_in['Wr1'], 'L0_attn_br1': _L0_attn_in['br1'], 'L0_attn_Wr2': _L0_attn_in['Wr2'], 'L0_attn_br2': _L0_attn_in['br2'], 'L0_attn_g1': _L0_attn_in['g1'], 'L0_attn_b1': _L0_attn_in['b1'], 'L0_attn_g2': _L0_attn_in['g2'], 'L0_attn_b2': _L0_attn_in['b2'], 'L0_ffn_W1': _L0_ffn_in['W1'], 'L0_ffn_b1': _L0_ffn_in['b1'], 'L0_ffn_W2': _L0_ffn_in['W2'], 'L0_ffn_b2': _L0_ffn_in['b2']}
    _x0 = _d['L0_attn_x']
    _d['L0_attn_x'] = jax.random.normal(jax.random.fold_in(jax.random.key(seed), 1), (4, 1024, 128), dtype=_x0.dtype)
    del _x0
    return _d

def reference(L0_attn_x, L0_attn_Wq, L0_attn_bq, L0_attn_Wk, L0_attn_bk, L0_attn_Wv, L0_attn_bv, L0_attn_Wqv, L0_attn_bqv, L0_attn_Ws, L0_attn_bs, L0_attn_Wf, L0_attn_bf, L0_attn_Wr1, L0_attn_br1, L0_attn_Wr2, L0_attn_br2, L0_attn_g1, L0_attn_b1, L0_attn_g2, L0_attn_b2, L0_ffn_W1, L0_ffn_b1, L0_ffn_W2, L0_ffn_b2):

    def _L0_attn_ref(x, Wq, bq, Wk, bk, Wv, bv, Wqv, bqv, Ws, bs, Wf, bf, Wr1, br1, Wr2, br2, g1, b1, g2, b2):
        import jax, jax.numpy as jnp
        import numpy as np
        DIM = 128
        H = 16
        HD = DIM // H
        R = 8
        QK = 32
        B = 4
        S = 128
        EPS = 1e-05

        def _lin(x, W, b):
            return x @ W.T + b

        def _ln(x, g, b):
            m = x.mean(-1, keepdims=True)
            v = ((x - m) ** 2).mean(-1, keepdims=True)
            return (x - m) / jnp.sqrt(v + EPS) * g + b
        b, n, _ = x.shape
        res = x
        xn = _ln(x, g1, b1)
        q = _lin(xn, Wq, bq).reshape(b, n, H, HD) / np.sqrt(HD).astype(np.float32)
        k = _lin(xn, Wk, bk).reshape(b, n, H, HD)
        score = jax.nn.softmax(jnp.einsum('bihd,bjhd->bhij', q, k), axis=-1)
        v = _lin(xn, Wv, bv).reshape(b, n, R, HD)
        out = jnp.einsum('bhij,bjrd->bihrd', score, v)
        qv = _lin(xn, Wqv, bqv).reshape(b, n, H, 1, QK) / np.sqrt(QK).astype(np.float32)
        qv = jnp.broadcast_to(qv, (b, n, H, R, QK))
        comp = jnp.concatenate([qv, out], axis=-1) @ Ws.T + bs
        comp = jax.nn.softmax(comp, axis=3)
        out = (comp * out).sum(axis=3).reshape(b, n, DIM)
        out = res + _lin(out, Wf, bf)
        res2 = out
        on = _ln(out, g2, b2)
        ffn = _lin(jax.nn.relu(_lin(on, Wr1, br1)), Wr2, br2)
        return res2 + ffn

    def _L0_ffn_ref(x, W1, b1, W2, b2):
        import jax, jax.numpy as jnp
        import numpy as np
        EMB = 128
        FF = 4 * EMB

        def _ternary(w):
            scale = jnp.maximum(jnp.mean(jnp.abs(w)), 1e-08)
            w_t = jnp.clip(jnp.round(w / scale), -1.0, 1.0)
            return w + jax.lax.stop_gradient(w_t - w)
        h = jnp.einsum('bsd,fd->bsf', x, _ternary(W1)) + b1
        h = jax.nn.gelu(h, approximate=False)
        out = jnp.einsum('bsf,df->bsd', h, _ternary(W2)) + b2
        return out
    x = L0_attn_x
    x = x + _L0_attn_ref(_layernorm(x, axis=-1), L0_attn_Wq, L0_attn_bq, L0_attn_Wk, L0_attn_bk, L0_attn_Wv, L0_attn_bv, L0_attn_Wqv, L0_attn_bqv, L0_attn_Ws, L0_attn_bs, L0_attn_Wf, L0_attn_bf, L0_attn_Wr1, L0_attn_br1, L0_attn_Wr2, L0_attn_br2, L0_attn_g1, L0_attn_b1, L0_attn_g2, L0_attn_b2)
    x = x + _L0_ffn_ref(_layernorm(x, axis=-1), L0_ffn_W1, L0_ffn_b1, L0_ffn_W2, L0_ffn_b2)
    return x

_drawn_inputs = setup_inputs


def setup_inputs(seed=0):
    import zlib

    import numpy as np

    out = dict(_drawn_inputs(seed))
    spreads = {'L0_attn_g1': (1.0, 0.6),
     'L0_attn_b1': (0.0, 0.8),
     'L0_attn_g2': (1.0, 0.6),
     'L0_attn_b2': (0.0, 2.0)}
    factors = {'L0_attn_Wq': 8.0,
     'L0_attn_bq': 8.0,
     'L0_attn_Wk': 8.0,
     'L0_attn_bk': 200.0,
     'L0_attn_Wv': 8.0,
     'L0_attn_bv': 8.0,
     'L0_attn_Wqv': 200.0,
     'L0_attn_bqv': 200.0,
     'L0_attn_Ws': 8.0,
     'L0_attn_Wf': 6.46,
     'L0_attn_br1': 46.544,
     'L0_attn_br2': 25.056,
     'L0_ffn_b1': 8.0,
     'L0_ffn_b2': 200.0,
     'L0_attn_bf': 43.967,
     'L0_attn_Wr1': 5.945,
     'L0_attn_Wr2': 4.478}
    for name, (base, spread) in spreads.items():
        noise = np.random.default_rng([zlib.crc32(name.encode()), seed]).standard_normal(out[name].shape)
        drawn = base * np.exp(spread * noise) if base else spread * noise
        out[name] = jnp.asarray(drawn.astype(out[name].dtype))
    for name, factor in factors.items():
        out[name] = (out[name] * factor).astype(out[name].dtype)
    return out
```

```python
import numpy as np
import concourse.bass as bass
from concourse import mybir
from contextlib import ExitStack

FP32 = mybir.dt.float32
BF16 = mybir.dt.bfloat16
ALU = mybir.AluOpType
ACT = mybir.ActivationFunctionType
AX = mybir.AxisListType
ds = bass.ds

BATCH, SEQ, DIM = 4, 1024, 128
HEADS, HD, R, QK = 16, 8, 8, 32
HIDDEN, FF = 2 * DIM, 4 * DIM
P = 128
TB = SEQ // P
TILES = BATCH * TB
U = BATCH * HEADS
SLOTS = 4
GROUPS = U // SLOTS
GPB = HEADS // SLOTS
VW = R * HD
HALF = SEQ // 2
PARTS = 3
PROD_ROWS = PARTS * PARTS * HD
MAX_PARTS = 2
ROWS = PROD_ROWS + MAX_PARTS
EPS = 1e-5
DMA = 16

C_BQ, C_BK, C_G1, C_B1, C_G2, C_B2, C_BR1, C_FB1, C_BQV, N_COLS = 0, 1, 2, 3, 4, 5, 6, 8, 12, 16
R_BV, R_WS, R_BS, R_BF, R_BR2, R_FB2, N_ROWS = 0, 64, 104, 128, 256, 384, 512


def spread(ap, n):
    return ap.unsqueeze(2).to_broadcast([ap.shape[0], ap.shape[1], n])


def again(ap, n):
    return ap.unsqueeze(1).to_broadcast([ap.shape[0], n, ap.shape[1]])


class Resident:

    def __init__(self, nc, ctx):
        def sb(name, shape, dtype=FP32):
            return ctx.enter_context(nc.sbuf_tensor(name, shape, dtype))
        self.x = sb("x_all", [P, TILES, DIM])
        self.y = sb("y_all", [P, TILES, DIM])
        self.v = sb("v_all", [P, TILES, VW])
        self.qs = sb("qs_all", [P, TILES, HEADS])
        self.att = sb("att_all", [P, BATCH, GPB, TB, SLOTS * HD])
        self.identf = sb("identf", [P, P])
        self.identb = sb("identb", [P, P], BF16)
        self.colsT = sb("colsT", [P, N_COLS])
        self.rows = sb("rows", [P, N_ROWS])
        self.wfT = sb("wfT", [P, DIM])
        self.wr1T = sb("wr1T", [P, HIDDEN])
        self.wr2T = sb("wr2T", [P, HIDDEN // P, DIM])
        self.w1T = sb("w1T", [P, FF])
        self.w2T = sb("w2T", [P, FF // P, DIM])
        self.q_parts = nc.dram_tensor("q_parts", [PARTS, U, HD, SEQ], BF16, kind="Internal").ap()
        self.k_parts = nc.dram_tensor("k_parts", [PARTS, U, HD, SEQ], BF16, kind="Internal").ap()


def prepare(nc, res, a):
    ctx = ExitStack()
    with ctx:
        def sb(name, shape, dtype=FP32):
            return ctx.enter_context(nc.sbuf_tensor(name, shape, dtype))

        def sem(name):
            return ctx.enter_context(nc.semaphore(name))

        wq_n, wk_n, wf_n = sb("wq_n", [P, DIM]), sb("wk_n", [P, DIM]), sb("wf_n", [P, DIM])
        wv_n = sb("wv_n", [VW, DIM])
        wqv_n = sb("wqv_n", [P, QK * HEADS // P, DIM])
        wr1_n = sb("wr1_n", [P, HIDDEN // P, DIM])
        wr2_n = sb("wr2_n", [P, HIDDEN])
        w1_n = sb("w1_n", [P, FF // P, DIM])
        w2_n = sb("w2_n", [P, FF])
        cols_n = sb("cols_n", [N_COLS, P])
        ws_col = sb("ws_col", [P, 1])
        ones = sb("ones", [P, P])
        qkvT = sb("qkvT", [P, 3 * DIM + VW])
        proj = sb("proj", [P, P])
        sel = sb("sel", [P, SLOTS])
        sel_b = sb("sel_b", [P, HEADS])
        qs_bias = sb("qs_bias", [P, HEADS])
        absum = sb("absum", [P, 2])
        scale = sb("scale", [P, 2, 2])
        above = sb("above", [P, 2, FF])
        below = sb("below", [P, 2, FF])
        stats = sb("stats", [P, TB, 6])
        moments = sb("moments", [P, TB, 2])
        std = sb("std", [P, TB])
        rstd = sb("rstd", [P, TB])
        z = sb("z", [P, TB, DIM])
        xnT = sb("xnT", [P, SEQ])
        full = sb("full", [P, 2, SEQ])
        parts = sb("parts", [P, PARTS, 2, SEQ], BF16)
        bank = [ctx.enter_context(nc.psum_tensor(f"prep{n}", [P, 2, HALF], FP32)) for n in range(4)]

        x_in, weights_in, parts_out = sem("x_in"), sem("weights_in"), sem("parts_out")
        ident_ready, cleared, sel_ready = sem("ident_ready"), sem("cleared"), sem("sel_ready")
        w_turned, w_copied, cols_ready = sem("w_turned"), sem("w_copied"), sem("cols_ready")
        selb_ready, qsb_summed, proj_ready = sem("selb_ready"), sem("qsb_summed"), sem("proj_ready")
        qsb_ready = sem("qsb_ready")
        absum_ready, absum_total = sem("absum_ready"), sem("absum_total")
        scale_ready, tern_step = sem("scale_ready"), sem("tern_step")
        stats_ready, moments_ready, var_ready = sem("stats_ready"), sem("moments_ready"), sem("var_ready")
        std_ready, rstd_ready, y_ready, z_ready = sem("std_ready"), sem("rstd_ready"), sem("y_ready"), sem("z_ready")
        z_turned, xnT_ready, qk_done, v_done = sem("z_turned"), sem("xnT_ready"), sem("qk_done"), sem("v_done")
        full_ready, part1, rest1, part2, part3 = (sem("full_ready"), sem("part1_ready"), sem("rest1_ready"),
                                                  sem("part2_ready"), sem("part3_ready"))
        v_copied = sem("v_copied")
        stood = sem("stood")

        weights = [
            (wq_n[:, :], a["Wq"]), (wk_n[:, :], a["Wk"]), (wf_n[:, :], a["Wf"]), (wv_n[:, :], a["Wv"]),
            (wqv_n[:, :, :], a["Wqv"].rearrange("(k p) d -> p k d", p=P)),
            (wr1_n[:, :, :], a["Wr1"].rearrange("(k p) d -> p k d", p=P)), (wr2_n[:, :], a["Wr2"]),
            (w1_n[:, :, :], a["W1"].rearrange("(k p) d -> p k d", p=P)), (w2_n[:, :], a["W2"]),
        ]
        for at, name, n in ((C_BQ, "bq", 1), (C_BK, "bk", 1), (C_G1, "g1", 1), (C_B1, "b1", 1),
                            (C_G2, "g2", 1), (C_B2, "b2", 1), (C_BR1, "br1", HIDDEN // P),
                            (C_FB1, "fb1", FF // P), (C_BQV, "bqv", QK * HEADS // P)):
            weights.append((cols_n[at:at + n, :], a[name].rearrange("(n p) -> n p", p=P)))
        for at, name, n in ((R_BV, "bv", VW), (R_BS, "bs", 1), (R_BF, "bf", DIM), (R_BR2, "br2", DIM),
                            (R_FB2, "fb2", DIM)):
            weights.append((res.rows[:, at:at + n], a[name].partition_broadcast(P)))
        weights.append((res.rows[:, R_WS:R_WS + QK + HD], a["Ws"][0, :].partition_broadcast(P)))
        for n in range(P // QK):
            weights.append((ws_col[n * QK:(n + 1) * QK, :], a["Ws"][0, 0:QK].rearrange("(p n) -> p n", n=1)))

        block = ctx.enter_context(nc.Block())

        @block.sync
        def _(sp):
            for b in range(BATCH):
                sp.dma_start(res.x[:, b * TB:(b + 1) * TB, :],
                             a["x"][b].rearrange("(t p) d -> p t d", p=P)).then_inc(x_in, DMA)
                sp.wait_ge(x_in, DMA * (b + 1))
            with sp.Fori(0, BATCH) as b:
                sp.wait_ge(part3, 2 * b + 2)
                for n, dram in enumerate((res.q_parts, res.k_parts)):
                    for c in range(PARTS):
                        sp.dma_start(dram[c, ds(b * HEADS, HEADS)].rearrange("h d s -> (h d) s"),
                                     parts[:, c, n, :]).then_inc(parts_out, DMA)
            sp.wait_ge(parts_out, DMA * 2 * PARTS * BATCH)

        @block.gpsimd
        def _(pool):
            pool.memset(res.identf[:, :], 0.0).then_inc(cleared, 1)
            pool.memset(res.identb[:, :], 0.0).then_inc(cleared, 1)
            pool.memset(sel[:, :], 1.0).then_inc(cleared, 1)
            pool.memset(ones[:, :], 1.0).then_inc(cleared, 1)
            pool.memset(proj[:, :], 0.0).then_inc(cleared, 1)
            pool.wait_ge(cleared, 5)
            for ident in (res.identf, res.identb):
                pool.affine_select(out=ident[:, :], in_=ident[:, :], compare_op=ALU.not_equal, fill=1.0,
                                   base=0, pattern=[[-1, P]], channel_multiplier=1).then_inc(ident_ready, 1)
            pool.affine_select(out=sel[:, :], in_=sel[:, :], compare_op=ALU.is_ge, fill=0.0,
                               base=0, pattern=[[-QK, SLOTS]], channel_multiplier=1).then_inc(ident_ready, 1)
            pool.wait_ge(ident_ready, 3)
            pool.affine_select(out=sel[:, :], in_=sel[:, :], compare_op=ALU.is_ge, fill=0.0,
                               base=QK - 1, pattern=[[QK, SLOTS]], channel_multiplier=-1).then_inc(ident_ready, 1)
            pool.wait_ge(scale_ready, 2)
            for n, w in enumerate((res.w1T[:, :], res.w2T[:, :, :].rearrange("p k d -> p (k d)"))):
                pool.tensor_scalar(above[:, n, :], w, scale[:, n, 0:1], None, ALU.is_gt).then_inc(tern_step, 1)
                pool.tensor_scalar(below[:, n, :], w, scale[:, n, 1:2], None, ALU.is_lt).then_inc(tern_step, 1)
                pool.wait_ge(tern_step, 5 * n + 2)
                pool.tensor_tensor(above[:, n, :], above[:, n, :], below[:, n, :], ALU.subtract).then_inc(tern_step, 1)
                pool.wait_ge(tern_step, 5 * n + 3)
                pool.tensor_tensor(above[:, n, :], above[:, n, :], w, ALU.subtract).then_inc(tern_step, 1)
                pool.wait_ge(tern_step, 5 * n + 4)
                pool.tensor_tensor(w, w, above[:, n, :], ALU.add).then_inc(tern_step, 1)

        @block.scalar
        def _(act):
            for dst, src in weights:
                act.dma_start(dst, src).then_inc(weights_in, DMA)
            act.wait_ge(w_turned, 1)
            nc.scalar.activation(qkvT[:, :], bank[0][:, 0, 0:3 * DIM + VW], ACT.Copy).then_inc(w_copied, 1)
            act.wait_ge(w_turned, 2)
            nc.scalar.activation(res.wr1T[:, :], bank[0][:, 1, 0:HIDDEN], ACT.Copy).then_inc(w_copied, 1)
            nc.scalar.activation(res.wr2T[:, :, :].rearrange("p k d -> p (k d)"), bank[0][:, 1, HIDDEN:2 * HIDDEN],
                                 ACT.Copy).then_inc(w_copied, 1)
            act.wait_ge(w_turned, 3)
            nc.scalar.activation(res.w1T[:, :], bank[1][:, 0, :], ACT.Copy).then_inc(w_copied, 1)
            act.wait_ge(w_turned, 4)
            nc.scalar.activation(res.w2T[:, :, :].rearrange("p k d -> p (k d)"), bank[1][:, 1, :],
                                 ACT.Copy).then_inc(w_copied, 1)
            act.wait_ge(w_copied, 5)
            nc.scalar.activation(res.wfT[:, :], qkvT[:, 2 * DIM:3 * DIM], ACT.Copy).then_inc(w_copied, 1)
            with act.Fori(0, BATCH) as b:
                for n in range(2):
                    act.wait_ge(var_ready, 2 * b + n + 1)
                    nc.scalar.activation(std[:, :], moments[:, :, 1], ACT.Sqrt).then_inc(std_ready, 1)
                for h in range(2):
                    act.wait_ge(z_turned, 2 * b + h + 1)
                    nc.scalar.activation(xnT[:, h * HALF:(h + 1) * HALF], bank[0][:, h, :], ACT.Identity,
                                         bias=res.colsT[:, C_B1:C_B1 + 1],
                                         scale=res.colsT[:, C_G1:C_G1 + 1]).then_inc(xnT_ready, 1)
                act.wait_ge(parts_out, DMA * 2 * PARTS * b)
                for n in range(2):
                    act.wait_ge(full_ready, 2 * b + n + 1)
                    nc.scalar.activation(parts[:, 0, n, :], full[:, n, :], ACT.Copy).then_inc(part1, 1)
                for n in range(2):
                    act.wait_ge(rest1, 2 * b + n + 1)
                    nc.scalar.activation(parts[:, 1, n, :], full[:, n, :], ACT.Copy).then_inc(part2, 1)

        @block.tensor
        def _(pe):
            pe.wait_ge(ident_ready, 4)
            pe.wait_ge(weights_in, DMA * len(weights))
            for n, w in enumerate((wq_n, wk_n, wf_n)):
                nc.tensor.transpose(bank[0][:, 0, n * DIM:(n + 1) * DIM], w[:, :], res.identf[:, :])
            nc.tensor.transpose(bank[0][:, 0, 3 * DIM:3 * DIM + VW], wv_n[:, :],
                                res.identf[0:VW, 0:VW]).then_inc(w_turned, 1)
            for k in range(HIDDEN // P):
                nc.tensor.transpose(bank[0][:, 1, k * P:(k + 1) * P], wr1_n[:, k, :], res.identf[:, :])
            for k in range(HIDDEN // P):
                last = nc.tensor.transpose(bank[0][:, 1, HIDDEN + k * P:HIDDEN + (k + 1) * P],
                                           wr2_n[:, k * P:(k + 1) * P], res.identf[:, :])
            last.then_inc(w_turned, 1)
            for k in range(FF // P):
                last = nc.tensor.transpose(bank[1][:, 0, k * P:(k + 1) * P], w1_n[:, k, :], res.identf[:, :])
            last.then_inc(w_turned, 1)
            for k in range(FF // P):
                last = nc.tensor.transpose(bank[1][:, 1, k * P:(k + 1) * P], w2_n[:, k * P:(k + 1) * P],
                                           res.identf[:, :])
            last.then_inc(w_turned, 1)
            nc.tensor.transpose(bank[2][:, 0, 0:N_COLS], cols_n[:, :],
                                res.identf[0:N_COLS, 0:N_COLS]).then_inc(w_turned, 1)
            pe.wait_ge(sel_ready, 1)
            for k in range(QK * HEADS // P):
                last = nc.tensor.matmul(bank[2][:, 1, k * SLOTS:(k + 1) * SLOTS], wqv_n[:, k, :], sel[:, :],
                                        start=True, stop=True)
            last.then_inc(w_turned, 1)
            pe.wait_ge(selb_ready, 1)
            nc.tensor.matmul(bank[3][:, 0, 0:HEADS], ones[:, :], sel_b[:, :],
                             start=True, stop=True).then_inc(qsb_summed, 1)
            pe.wait_ge(absum_ready, 2)
            nc.tensor.matmul(bank[3][:, 1, 0:2], ones[:, :], absum[:, :],
                             start=True, stop=True).then_inc(absum_total, 1)
            pe.wait_ge(w_copied, 5)
            pe.wait_ge(proj_ready, 2)
            pe.wait_ge(qsb_ready, 1)
            pe.wait_ge(scale_ready, 1)
            with pe.Fori(0, BATCH) as b:
                pe.wait_ge(z_ready, b + 1)
                pe.wait_ge(xnT_ready, 2 * b)
                for t in range(TB):
                    h, c = t // 4, t % 4
                    last = nc.tensor.transpose(bank[0][:, h, c * P:(c + 1) * P], z[:, t, :], res.identf[:, :])
                    if c == 3:
                        last.then_inc(z_turned, 1)
                pe.wait_ge(xnT_ready, 2 * b + 2)
                pe.wait_ge(full_ready, 2 * b)
                for n in range(2):
                    for h in range(2):
                        last = nc.tensor.matmul(bank[1 + n][:, h, :], qkvT[:, n * DIM:(n + 1) * DIM],
                                                xnT[:, h * HALF:(h + 1) * HALF], start=True, stop=True)
                    last.then_inc(qk_done, 1)
                pe.wait_ge(v_copied, 2 * b)
                for t in range(TB):
                    last = nc.tensor.matmul(bank[3][:, t // 4, (t % 4) * P:(t % 4 + 1) * P],
                                            xnT[:, t * P:(t + 1) * P], proj[:, :], start=True, stop=True)
                last.then_inc(v_done, 1)

        @block.vector
        def _(dve):
            dve.wait_ge(weights_in, DMA * len(weights))
            dve.wait_ge(ident_ready, 4)
            nc.vector.tensor_scalar(sel[:, :], sel[:, :], ws_col[:, 0:1], None, ALU.mult).then_inc(sel_ready, 1)
            dve.wait_ge(w_turned, 5)
            nc.vector.tensor_copy(res.colsT[:, :], bank[2][:, 0, 0:N_COLS]).then_inc(cols_ready, 1)
            dve.wait_ge(w_turned, 6)
            dve.wait_ge(w_copied, 1)
            nc.vector.tensor_copy(proj[:, 0:VW], qkvT[:, 3 * DIM:3 * DIM + VW]).then_inc(proj_ready, 1)
            nc.vector.tensor_scalar(proj[:, VW:VW + HEADS], bank[2][:, 1, 0:HEADS], QK ** -0.5, None,
                                    ALU.mult).then_inc(proj_ready, 1)
            dve.wait_ge(cols_ready, 1)
            for k in range(QK * HEADS // P):
                last = nc.vector.tensor_scalar(sel_b[:, k * SLOTS:(k + 1) * SLOTS], sel[:, :],
                                               res.colsT[:, C_BQV + k:C_BQV + k + 1], None, ALU.mult)
            last.then_inc(selb_ready, 1)
            dve.wait_ge(qsb_summed, 1)
            nc.vector.tensor_scalar(qs_bias[:, :], bank[3][:, 0, 0:HEADS], QK ** -0.5,
                                    res.rows[:, R_BS:R_BS + 1], ALU.mult, ALU.add).then_inc(qsb_ready, 1)
            dve.wait_ge(w_copied, 5)
            for n, w in enumerate((res.w1T[:, :], res.w2T[:, :, :].rearrange("p k d -> p (k d)"))):
                nc.vector.tensor_reduce(absum[:, n:n + 1], w, AX.X, ALU.add,
                                        apply_absolute_value=True).then_inc(absum_ready, 1)
            dve.wait_ge(absum_total, 1)
            nc.vector.tensor_scalar(scale[:, :, 0], bank[3][:, 1, 0:2], 1.0 / (FF * DIM), 1e-8,
                                    ALU.mult, ALU.max).then_inc(scale_ready, 1)
            dve.wait_ge(scale_ready, 1)
            nc.vector.tensor_scalar(scale[:, :, 1], scale[:, :, 0], -0.5, None, ALU.mult).then_inc(qsb_ready, 1)
            dve.wait_ge(qsb_ready, 2)
            nc.vector.tensor_scalar(scale[:, :, 0], scale[:, :, 0], 0.5, None, ALU.mult).then_inc(scale_ready, 1)
            with dve.Fori(0, BATCH) as b:
                dve.wait_ge(x_in, DMA * b + DMA).then_inc(stood, 1)
                for n in range(2):
                    for t in range(TB):
                        src = res.x if n == 0 else res.y
                        nc.vector.bn_stats(stats[:, t, :], src[:, ds(b * TB + t, 1), :]
                                           .rearrange("p t d -> p (t d)")).then_inc(stats_ready, 1)
                    dve.wait_ge(stats_ready, 2 * TB * b + TB * n + TB).then_inc(stood, 1)
                    for t in range(TB):
                        nc.vector.bn_aggr(moments[:, t, :], stats[:, t, :]).then_inc(moments_ready, 1)
                    dve.wait_ge(moments_ready, 2 * TB * b + TB * (n + 1))
                    nc.vector.tensor_scalar(moments[:, :, 1], moments[:, :, 1], EPS, None,
                                            ALU.add).then_inc(var_ready, 1)
                    dve.wait_ge(std_ready, 2 * b + n + 1)
                    nc.vector.reciprocal(rstd[:, :], std[:, :]).then_inc(rstd_ready, 1)
                    dve.wait_ge(rstd_ready, 2 * b + n + 1)
                    if n == 1:
                        dve.wait_ge(z_turned, 2 * b)
                    for t in range(TB):
                        src, dst = ((res.x[:, ds(b * TB + t, 1), :], res.y[:, ds(b * TB + t, 1), :]) if n == 0
                                    else (res.y[:, ds(b * TB + t, 1), :], z[:, t:t + 1, :]))
                        last = nc.vector.tensor_scalar(dst, src, moments[:, t, 0:1], rstd[:, t:t + 1],
                                                       ALU.subtract, ALU.mult)
                    last.then_inc(y_ready if n == 0 else z_ready, 1)
                    if n == 0:
                        dve.wait_ge(y_ready, b + 1).then_inc(stood, 1)
                dve.wait_ge(qk_done, 2 * b + 1)
                nc.vector.tensor_scalar(full[:, 0, :], bank[1][:, :, :].rearrange("p h s -> p (h s)"),
                                        res.colsT[:, C_BQ:C_BQ + 1], HD ** -0.5,
                                        ALU.add, ALU.mult).then_inc(full_ready, 1)
                dve.wait_ge(qk_done, 2 * b + 2)
                nc.vector.tensor_scalar(full[:, 1, :], bank[2][:, :, :].rearrange("p h s -> p (h s)"),
                                        res.colsT[:, C_BK:C_BK + 1], None, ALU.add).then_inc(full_ready, 1)
                for n in range(2):
                    dve.wait_ge(part1, 2 * b + n + 1)
                    nc.vector.tensor_tensor(full[:, n, :], full[:, n, :], parts[:, 0, n, :],
                                            ALU.subtract).then_inc(rest1, 1)
                dve.wait_ge(v_done, b + 1)
                tiles = bank[3][:, :, :].rearrange("p h (c w) -> p (h c) w", w=P)
                nc.vector.tensor_tensor(res.v[:, ds(b * TB, TB), :], tiles[:, :, 0:VW],
                                        again(res.rows[:, R_BV:R_BV + VW], TB), ALU.add).then_inc(v_copied, 1)
                nc.vector.tensor_tensor(res.qs[:, ds(b * TB, TB), :], tiles[:, :, VW:VW + HEADS],
                                        again(qs_bias[:, :], TB), ALU.add).then_inc(v_copied, 1)
                for n in range(2):
                    dve.wait_ge(part2, 2 * b + n + 1)
                    nc.vector.tensor_tensor(parts[:, 2, n, :], full[:, n, :], parts[:, 1, n, :],
                                            ALU.subtract).then_inc(part3, 1)


def attention(nc, res):
    ctx = ExitStack()
    with ctx:
        def sb(name, shape, dtype=FP32):
            return ctx.enter_context(nc.sbuf_tensor(name, shape, dtype))

        def pb(name, shape):
            return ctx.enter_context(nc.psum_tensor(name, shape, FP32))

        def sem(name):
            return ctx.enter_context(nc.semaphore(name))

        q_op = [sb(f"q_op{s}", [ROWS, SEQ], BF16) for s in range(SLOTS)]
        k_op = [sb(f"k_op{s}", [P, SEQ], BF16) for s in range(SLOTS)]
        v_op = [sb(f"v_op{s}", [P, TB, VW]) for s in range(SLOTS)]
        prob = sb("prob", [P, TB, SEQ])
        pair = sb("pair", [P, TB // 2, SEQ])
        quad = sb("quad", [P, 2, SEQ])
        rowmax = sb("rowmax", [P, 2, TB, 2])
        negmax = sb("negmax", [P, TB])
        max_parts = sb("max_parts", [P, 2, MAX_PARTS, TB], BF16)
        max_rows = [sb(f"max_rows{n}", [MAX_PARTS * TB, P], BF16) for n in range(2)]
        onehot = sb("onehot", [P, SLOTS, 32])
        outT = [sb(f"outT{n}", [P, HALF]) for n in range(2)]
        denT = sb("denT", [P, HALF])
        mix_in = sb("mix_in", [P, 2, TB, SLOTS, VW])
        product = sb("product", [P, TB * SLOTS, R, HD])
        den = sb("den", [P, TB, SLOTS])
        rden = sb("rden", [P, TB, SLOTS])
        logit = sb("logit", [P, TB * SLOTS, R])
        top = sb("top", [P, TB * SLOTS])
        total = sb("total", [P, TB * SLOTS])

        col_bank = [pb(f"col_bank{n}", [P, HALF]) for n in range(2)]
        row_bank = [pb(f"row_bank{n}", [P, HALF]) for n in range(2)]
        out_bank = [pb(f"out_bank{n}", [P, HALF]) for n in range(2)]
        den_bank = pb("den_bank", [P, HALF])
        turn_bank = pb("turn_bank", [P, HALF])

        operands_in = [sem(f"operands_in{s}") for s in range(SLOTS)]
        max_in = [sem(f"max_in{s}") for s in range(SLOTS)]
        ones_set, onehot_set = sem("ones_set"), sem("onehot_set")
        col_scored, row_scored = sem("col_scored"), sem("row_scored")
        exp_done, max_done, pv_done = sem("exp_done"), sem("max_done"), sem("pv_done")
        negmax_ready, part1_ready, max_split = sem("negmax_ready"), sem("part1_ready"), sem("max_split")
        max_turned, max_rows_ready = sem("max_turned"), sem("max_rows_ready")
        pair_done, quad_done, den_done = sem("pair_done"), sem("quad_done"), sem("den_done")
        outT_ready, out_turned, mix_in_ready = sem("outT_ready"), sem("out_turned"), sem("mix_in_ready")
        denT_ready, den_turned, den_ready, rden_ready = (sem("denT_ready"), sem("den_turned"), sem("den_ready"),
                                                         sem("rden_ready"))
        logit_product, logit_sum, logit_scaled, logit_ready = (sem("logit_product"), sem("logit_sum"),
                                                               sem("logit_scaled"), sem("logit_ready"))
        top_ready, logit_shifted, mix_exp = sem("top_ready"), sem("logit_shifted"), sem("mix_exp")
        total_ready, rtotal_ready, norm_ready, weight_ready = (sem("total_ready"), sem("rtotal_ready"),
                                                               sem("norm_ready"), sem("weight_ready"))
        mixed, att_done = sem("mixed"), sem("att_done")
        stood = sem("stood_pool")

        LOADS = 2 * PARTS + 1
        halves = lambda t: t.rearrange("p (c h i) -> p c h i", c=TB // 2, h=2)

        block = ctx.enter_context(nc.Block())

        @block.sync
        def _(sp):
            def load(u, b, slot):
                for n in range(PARTS):
                    sp.dma_start(k_op[slot][n * PARTS * HD:(n + 1) * PARTS * HD, :],
                                 res.k_parts[:, ds(u, 1)].rearrange("c u d s -> (c u) d s")).then_inc(operands_in[slot], DMA)
                    sp.dma_start(q_op[slot][n * PARTS * HD:(n + 1) * PARTS * HD, :],
                                 res.q_parts[n, ds(u, 1)].to_broadcast([PARTS, HD, SEQ])).then_inc(operands_in[slot], DMA)
                sp.dma_start(v_op[slot][:, :, :], res.v[:, ds(b * TB, TB), :]).then_inc(operands_in[slot], DMA)

            def put_max(w, slot, parity):
                sp.wait_ge(max_rows_ready, w + 1)
                sp.dma_start(q_op[slot][PROD_ROWS:ROWS, :].rearrange("m (t i) -> m t i", t=TB),
                             max_rows[parity][:, :]).then_inc(max_in[slot], DMA)

            def group(G, first, last):
                for s in range(SLOTS):
                    u = G * SLOTS + s
                    if not (last and s >= 1):
                        if not (first and s == 0):
                            sp.wait_ge(pv_done, TB * u)
                        nxt = G if s < 1 else G + 1
                        load(nxt * SLOTS + (s + 3) % SLOTS, nxt // GPB, (s + 3) % SLOTS)
                    if not (last and s == SLOTS - 1):
                        put_max(u + 1, (s + 1) % SLOTS, (s + 1) % 2)

            sp.wait_ge(ones_set, SLOTS)
            for u in range(3):
                load(u, 0, u)
            put_max(0, 0, 0)
            group(0, True, False)
            with sp.Fori(1, GROUPS - 1) as G:
                group(G, False, False)
            group(GROUPS - 1, False, True)

        @block.tensor
        def _(pe):
            def row_scores(v, slot, t, known_free):
                for h in range(2):
                    if not known_free:
                        pe.wait_ge(max_done, 2 * TB * v + 2 * t + h - 1)
                    nc.tensor.matmul(row_bank[h][:, :], q_op[slot][0:PROD_ROWS, t * P:(t + 1) * P],
                                     k_op[slot][0:PROD_ROWS, h * HALF:(h + 1) * HALF],
                                     start=True, stop=True).then_inc(row_scored, 1)

            def turn_max(w, parity):
                pe.wait_ge(max_split, w + 1)
                pe.wait_ge(max_rows_ready, w)
                nc.tensor.matmul(turn_bank[0:MAX_PARTS * TB, 0:P],
                                 max_parts[:, parity, :, :].rearrange("p m t -> p (m t)"),
                                 res.identb[:, :], start=True, stop=True).then_inc(max_turned, 1)

            def col_scores(u, slot, t, known_free):
                for h in range(2):
                    if not known_free:
                        pe.wait_ge(exp_done, 2 * TB * u + 2 * t + h - 1)
                    nc.tensor.matmul(col_bank[h][:, :], k_op[slot][0:ROWS, t * P:(t + 1) * P],
                                     q_op[slot][0:ROWS, h * HALF:(h + 1) * HALF],
                                     start=True, stop=True).then_inc(col_scored, 1)

            def values(u, slot, t):
                pe.wait_ge(exp_done, 2 * TB * u + 2 * t + 2)
                for ih in range(2):
                    last = nc.tensor.matmul(out_bank[slot % 2][ih * VW:(ih + 1) * VW, :], v_op[slot][:, t, :],
                                            halves(prob[:, t, :])[:, :, ih, :], start=(t == 0), stop=(t == TB - 1))
                last.then_inc(pv_done, 1)

            def denominators(u, slot):
                pe.wait_ge(quad_done, 4 * u + 4)
                for ih in range(2):
                    for k in range(2):
                        q = 32 * (2 * ih + k)
                        last = nc.tensor.matmul(den_bank[q:q + 32, :], onehot[:, slot, :],
                                                halves(quad[:, k, :])[:, :, ih, :],
                                                start=(slot == 0), stop=(slot == SLOTS - 1))
                last.then_inc(den_done, 1)

            def turn_out(u, parity):
                pe.wait_ge(outT_ready, u + 1)
                for c in range(TB // 2):
                    last = nc.tensor.transpose(out_bank[parity][:, c * P:(c + 1) * P],
                                               outT[parity][:, c * P:(c + 1) * P], res.identf[:, :])
                last.then_inc(out_turned, 1)

            def turn_den(G):
                pe.wait_ge(denT_ready, G + 1)
                for c in range(TB // 2):
                    last = nc.tensor.transpose(turn_bank[:, c * P:(c + 1) * P], denT[:, c * P:(c + 1) * P],
                                               res.identf[:, :])
                last.then_inc(den_turned, 1)

            def group(G, first, last):
                for s in range(SLOTS):
                    u = G * SLOTS + s
                    before = not (first and s == 0)
                    ahead = not (last and s >= 2)
                    Gv, sv, sp_ = (G if s < 2 else G + 1), (s + 2) % SLOTS, (s - 1) % SLOTS
                    for t in range(TB):
                        if t == 0:
                            pe.wait_ge(max_in[s], DMA * (G + 1))
                        col_scores(u, s, t, not before and t == 0)
                        if ahead:
                            if t == 0:
                                pe.wait_ge(operands_in[sv], LOADS * DMA * (Gv + 1))
                            row_scores(u + 2, sv, t, False)
                        if t > 0:
                            if t == 1 and not (first and s < 2):
                                pe.wait_ge(mix_in_ready, u - 1)
                            values(u, s, t - 1)
                        elif before:
                            values(u - 1, sp_, TB - 1)
                        if t == 1 and not (last and s == SLOTS - 1):
                            if s == 1 and not first:
                                pe.wait_ge(den_ready, G)
                            turn_max(u + 1, (s + 1) % 2)
                        if t == 2 and before:
                            turn_out(u - 1, sp_ % 2)
                        if t == 4 and before:
                            if s == 1 and not first:
                                pe.wait_ge(denT_ready, G)
                            denominators(u - 1, sp_)
                        if t == 6 and s == 0 and not first:
                            pe.wait_ge(max_rows_ready, u + 2)
                            turn_den(G - 1)

            pe.wait_ge(operands_in[0], LOADS * DMA)
            for t in range(TB):
                row_scores(0, 0, t, t == 0)
            pe.wait_ge(operands_in[1], LOADS * DMA)
            for t in range(TB):
                row_scores(1, 1, t, False)
                if t == 3:
                    pe.wait_ge(max_split, 1)
                    nc.tensor.matmul(turn_bank[0:MAX_PARTS * TB, 0:P],
                                     max_parts[:, 0, :, :].rearrange("p m t -> p (m t)"),
                                     res.identb[:, :], start=True, stop=True).then_inc(max_turned, 1)
            pe.wait_ge(onehot_set, 2)
            group(0, True, False)
            with pe.Fori(1, GROUPS - 1) as G:
                group(G, False, False)
            group(GROUPS - 1, False, True)
            values(U - 1, SLOTS - 1, TB - 1)
            turn_out(U - 1, 1)
            denominators(U - 1, SLOTS - 1)
            turn_den(GROUPS - 1)

        @block.scalar
        def _(act):
            def take_out(u, parity):
                act.wait_ge(pv_done, TB * u + TB)
                nc.scalar.activation(outT[parity][:, :], out_bank[parity][:, :], ACT.Copy).then_inc(outT_ready, 1)

            def take_turned(u, G, slot):
                act.wait_ge(out_turned, u + 1)
                nc.scalar.activation(mix_in[:, ds(G % 2, 1), :, slot, :].rearrange("p g e w -> p (g e) w"),
                                     out_bank[slot % 2][:, :].rearrange("p (e w) -> p e w", w=VW),
                                     ACT.Copy).then_inc(mix_in_ready, 1)

            def take_den(G):
                act.wait_ge(den_done, SLOTS * G + SLOTS)
                nc.scalar.activation(denT[:, :], den_bank[:, :], ACT.Copy).then_inc(denT_ready, 1)

            def mix_exps(G):
                act.wait_ge(logit_shifted, G + 1)
                nc.scalar.activation(logit[:, :, :], logit[:, :, :], ACT.Exp).then_inc(mix_exp, 1)

            def group(G, first):
                for s in range(SLOTS):
                    u = G * SLOTS + s
                    before = not (first and s == 0)
                    for t in range(TB):
                        for h in range(2):
                            if h == 0 and before:
                                act.wait_ge(pv_done, TB * u - TB + t + 1)
                                act.wait_ge(pair_done, TB // 2 * u - TB // 2 + t // 2 + 1)
                            act.wait_ge(col_scored, 2 * TB * u + 2 * t + h + 1)
                            nc.scalar.activation(prob[:, t, h * HALF:(h + 1) * HALF], col_bank[h][:, :],
                                                 ACT.Exp).then_inc(exp_done, 1)
                        if t == 1 and before:
                            take_out(u - 1, (s - 1) % 2)
                        if t == 3 and before:
                            if s == 1 and not first:
                                act.wait_ge(att_done, G - 1)
                            take_turned(u - 1, G if s > 0 else G - 1, (s - 1) % SLOTS)
                        if t == 5 and s == 0 and not first:
                            take_den(G - 1)
                        if t == 7 and s == 2 and not first:
                            mix_exps(G - 1)

            group(0, True)
            with act.Fori(1, GROUPS) as G:
                group(G, False)
            take_out(U - 1, 1)
            take_turned(U - 1, GROUPS - 1, SLOTS - 1)
            take_den(GROUPS - 1)
            mix_exps(GROUPS - 1)

        @block.vector
        def _(dve):
            def row_max(v, parity, t):
                for h in range(2):
                    dve.wait_ge(row_scored, 2 * TB * v + 2 * t + h + 1)
                    nc.vector.tensor_reduce(rowmax[:, parity, t, h:h + 1], row_bank[h][:, :], AX.X,
                                            ALU.max).then_inc(max_done, 1)

            def split_max(w, parity):
                dve.wait_ge(max_done, 2 * TB * w + 2 * TB)
                nc.vector.tensor_reduce(negmax[:, :], rowmax[:, parity, :, :], AX.X, ALU.max,
                                        negate=True).then_inc(negmax_ready, 1)
                dve.wait_ge(negmax_ready, w + 1)
                nc.vector.tensor_copy(max_parts[:, parity, 0, :], negmax[:, :]).then_inc(part1_ready, 1)
                dve.wait_ge(part1_ready, w + 1)
                nc.vector.tensor_tensor(max_parts[:, parity, 1, :], negmax[:, :], max_parts[:, parity, 0, :],
                                        ALU.subtract).then_inc(max_split, 1)

            def take_rows(w, parity):
                dve.wait_ge(max_turned, w + 1)
                nc.vector.tensor_copy(max_rows[parity][:, :], turn_bank[0:MAX_PARTS * TB, 0:P]).then_inc(max_rows_ready, 1)

            def quads(u, k, h, known_free):
                dve.wait_ge(pair_done, TB // 2 * u + 2 * k + 2)
                if not known_free:
                    dve.wait_ge(den_done, u)
                part = slice(h * HALF, (h + 1) * HALF)
                nc.vector.tensor_tensor(quad[:, k, part], pair[:, 2 * k, part], pair[:, 2 * k + 1, part],
                                        ALU.add).then_inc(quad_done, 1)

            def mixing(G, b, g, step):
                E = TB * SLOTS
                flat = lambda x: x[:, :, :].rearrange("p e s -> p (e s)")
                if step == 0:
                    dve.wait_ge(den_turned, G + 1)
                    nc.vector.tensor_reduce(den[:, :, :], turn_bank[:, :].rearrange("p (e k s) -> p e s k", k=2, s=32)
                                            [:, :, 0:SLOTS, :], AX.X, ALU.add).then_inc(den_ready, 1)
                    dve.wait_ge(den_ready, G + 1)
                    nc.vector.reciprocal(flat(rden), flat(den)).then_inc(rden_ready, 1)
                elif step in (1, 2, 3, 4):
                    n, part = step - 1, slice((step - 1) * TB, step * TB)
                    dve.wait_ge(logit_product, G + 1)
                    nc.vector.tensor_reduce(logit[:, part, :], product[:, part, :, :], AX.X,
                                            ALU.add).then_inc(logit_sum, 1)
                elif step == 5:
                    dve.wait_ge(logit_sum, 4 * G + 4)
                    dve.wait_ge(rden_ready, G + 1)
                    nc.vector.tensor_tensor(logit[:, :, :], logit[:, :, :], spread(flat(rden), R),
                                            ALU.mult).then_inc(logit_scaled, 1)
                elif step == 6:
                    dve.wait_ge(logit_scaled, G + 1)
                    for e in range(1):
                        nc.vector.tensor_tensor(
                            logit[:, :, :].rearrange("p (e s) r -> p e s r", s=SLOTS),
                            logit[:, :, :].rearrange("p (e s) r -> p e s r", s=SLOTS),
                            res.qs[:, ds(b * TB, TB), ds(g * SLOTS, SLOTS)].unsqueeze(3)
                            .to_broadcast([P, TB, SLOTS, R]), ALU.add).then_inc(logit_ready, 1)
                elif step == 7:
                    dve.wait_ge(logit_ready, G + 1)
                    nc.vector.tensor_reduce(top[:, :], logit[:, :, :], AX.X, ALU.max).then_inc(top_ready, 1)
                elif step == 8:
                    dve.wait_ge(top_ready, G + 1)
                    nc.vector.tensor_tensor(logit[:, :, :], logit[:, :, :], spread(top[:, :], R),
                                            ALU.subtract).then_inc(logit_shifted, 1)
                elif step == 9:
                    dve.wait_ge(mix_exp, G + 1)
                    nc.vector.tensor_reduce(total[:, :], logit[:, :, :], AX.X, ALU.add).then_inc(total_ready, 1)
                elif step == 10:
                    dve.wait_ge(total_ready, G + 1)
                    nc.vector.reciprocal(total[:, :], total[:, :]).then_inc(rtotal_ready, 1)
                    dve.wait_ge(rtotal_ready, G + 1)
                    nc.vector.tensor_tensor(total[:, :], total[:, :], flat(rden), ALU.mult).then_inc(norm_ready, 1)
                elif step == 11:
                    dve.wait_ge(norm_ready, G + 1)
                    nc.vector.tensor_tensor(logit[:, :, :], logit[:, :, :], spread(total[:, :], R),
                                            ALU.mult).then_inc(weight_ready, 1)
                elif step in (12, 13, 14, 15):
                    n = step - 12
                    dve.wait_ge(mixed, G + 1)
                    last = nc.vector.tensor_reduce(
                        res.att[:, ds(b, 1), ds(g, 1), 2 * n:2 * n + 2, :].rearrange("p b g e (s d) -> p (b g e s) d", d=HD),
                        product[:, n * TB:(n + 1) * TB, :, :].rearrange("p m r d -> p m d r"), AX.X, ALU.add)
                    if n == 3:
                        last.then_inc(att_done, 1)

            PLAN = {(0, 7): 0, (1, 4): 1, (1, 5): 2, (1, 6): 3, (1, 7): 4, (2, 0): 5, (2, 1): 6, (2, 4): 7,
                    (2, 5): 8, (3, 0): 9, (3, 1): 10, (3, 4): 11}

            def group(G, first, last):
                for s in range(SLOTS):
                    u = G * SLOTS + s
                    before = not (first and s == 0)
                    ahead = not (last and s >= 2)
                    for t in range(TB):
                        if t == 0 and not (last and s == SLOTS - 1):
                            split_max(u + 1, (s + 1) % 2)
                        if ahead:
                            row_max(u + 2, s % 2, t)
                        if t == 1 and not (last and s == SLOTS - 1):
                            if s >= 1 or not first:
                                dve.wait_ge(max_in[(s - 1) % SLOTS], DMA * ((G if s >= 1 else G - 1) + 1))
                            take_rows(u + 1, (s + 1) % 2)
                        if t in (2, 3) and before:
                            quads(u - 1, 1, t - 2, first and s == 1)
                        if t in (6, 7):
                            quads(u, 0, t - 6, first and s == 0)
                        if not first and (s, t) in PLAN:
                            mixing(G - 1, (G - 1) // GPB, (G - 1) % GPB, PLAN[s, t])
                if not first:
                    for step in (12, 13, 14, 15):
                        mixing(G - 1, (G - 1) // GPB, (G - 1) % GPB, step)

            for s in range(SLOTS):
                dve.memset(k_op[s][64:P, :], 1.0).then_inc(ones_set, 1)
            dve.memset(onehot[:, :, :], 0.0).then_inc(onehot_set, 1)
            dve.wait_ge(onehot_set, 1)
            for s in range(SLOTS):
                last = dve.memset(onehot[:, s, s:s + 1], 1.0)
            last.then_inc(onehot_set, 1)
            for t in range(TB):
                row_max(0, 0, t)
            split_max(0, 0)
            for t in range(TB):
                row_max(1, 1, t)
                if t == 4:
                    take_rows(0, 0)
            group(0, True, False)
            with dve.Fori(1, GROUPS - 1) as G:
                group(G, False, False)
            group(GROUPS - 1, False, True)
            quads(U - 1, 1, 0, False)
            quads(U - 1, 1, 1, False)
            for step in range(16):
                mixing(GROUPS - 1, BATCH - 1, GPB - 1, step)

        @block.gpsimd
        def _(pool):
            def pairs(u, k, known_free):
                pool.wait_ge(exp_done, 2 * TB * u + 4 * k + 4)
                if not known_free:
                    pool.wait_ge(quad_done, 4 * u - 2 + 2 * (k // 2))
                pool.tensor_tensor(pair[:, k, :], prob[:, 2 * k, :], prob[:, 2 * k + 1, :],
                                   ALU.add).then_inc(pair_done, 1)

            def values_of(G):
                return mix_in[:, ds(G % 2, 1), :, :, :].rearrange("p g e s w -> p (g e s) w")

            def logit_products(G):
                pool.wait_ge(mix_in_ready, SLOTS * G + SLOTS)
                pool.wait_ge(att_done, G).then_inc(stood, 1)
                pool.tensor_tensor(
                    product[:, :, :, :].rearrange("p m r d -> p (m r) d"),
                    values_of(G).rearrange("p m (r d) -> p (m r) d", d=HD),
                    again(res.rows[:, R_WS + QK:R_WS + QK + HD], TB * SLOTS * R),
                    ALU.mult).then_inc(logit_product, 1)

            def mix(G):
                pool.wait_ge(weight_ready, G + 1).then_inc(stood, 1)
                pool.tensor_tensor(
                    product[:, :, :, :].rearrange("p m r d -> p (m r) d"),
                    values_of(G).rearrange("p m (r d) -> p (m r) d", d=HD),
                    spread(logit[:, :, :].rearrange("p m r -> p (m r)"), HD),
                    ALU.mult).then_inc(mixed, 1)

            def group(G, first):
                for s in range(SLOTS):
                    u = G * SLOTS + s
                    for k in range(TB // 2):
                        pairs(u, k, first and s == 0)
                        if k == 2 and s == 0 and not first:
                            logit_products(G - 1)
                        if k == 2 and s == 3 and not first:
                            mix(G - 1)

            group(0, True)
            with pool.Fori(1, GROUPS) as G:
                group(G, False)
            logit_products(GROUPS - 1)
            mix(GROUPS - 1)


def feed_forward(nc, res, out):
    ctx = ExitStack()
    with ctx:
        def sb(name, shape, dtype=FP32):
            return ctx.enter_context(nc.sbuf_tensor(name, shape, dtype))

        def sem(name):
            return ctx.enter_context(nc.semaphore(name))

        T = HALF // P
        BLOCKS = TILES // T
        att = sb("att", [P, T, DIM])
        attT = sb("attT", [P, HALF])
        x2 = sb("x2", [P, T, DIM])
        stats = sb("ff_stats", [P, T, 6])
        moments = sb("ff_moments", [P, T, 2])
        std = sb("ff_std", [P, T])
        rstd = sb("ff_rstd", [P, T])
        normed = sb("normed", [P, T, DIM])
        onT = sb("onT", [P, HALF])
        hT = sb("hT", [P, HIDDEN // P, HALF])
        x3nT = sb("x3nT", [P, BLOCKS, HALF])
        gT = sb("gT", [P, FF // P, HALF])
        y_out = sb("y_out", [P, 2, T, DIM])
        turn = ctx.enter_context(nc.psum_tensor("ff_turn", [P, HALF], FP32))
        prod = ctx.enter_context(nc.psum_tensor("ff_prod", [P, T, DIM], FP32))
        wide = [ctx.enter_context(nc.psum_tensor(f"ff_wide{n}", [P, HALF], FP32)) for n in range(FF // P)]

        names = ("att_copied att_turned attT_ready projected biased summed x2_ready stats_ready moments_ready "
                 "var_ready std_ready rstd_ready normed_ready normed_turned onT_ready hidden hT_ready reduced "
                 "ff_biased ff_summed x3_ready x3nT_ready wide_done gelu_done down_done down_biased y_ready stood").split()
        S = {n: sem(n) for n in names}
        y_stored = [sem("y_stored0"), sem("y_stored1")]
        block = ctx.enter_context(nc.Block())
        N = BLOCKS
        tiles = lambda r, k: r[:, ds(k * T, T), :]

        @block.gpsimd
        def _(pool):
            with pool.Fori(0, N) as k:
                pool.wait_ge(S["att_turned"], k)
                for g in range(GPB):
                    last = pool.tensor_copy(att[:, :, g * SLOTS * HD:(g + 1) * SLOTS * HD],
                                            res.att[:, ds(k // 2, 1), g, ds((k % 2) * T, T), :]
                                            .rearrange("p b e w -> p (b e) w"))
                last.then_inc(S["att_copied"], 1)

        @block.tensor
        def _(pe):
            def turned(src, done):
                for c in range(T):
                    last = nc.tensor.transpose(turn[:, c * P:(c + 1) * P], src[:, c, :], res.identf[:, :])
                last.then_inc(done, 1)

            with pe.Fori(0, N) as k:
                pe.wait_ge(S["att_copied"], k + 1)
                pe.wait_ge(S["x3nT_ready"], k)
                turned(att, S["att_turned"])
                pe.wait_ge(S["attT_ready"], k + 1)
                pe.wait_ge(S["ff_biased"], k)
                for c in range(T):
                    last = nc.tensor.matmul(prod[:, c, :], attT[:, c * P:(c + 1) * P], res.wfT[:, :],
                                            start=True, stop=True)
                last.then_inc(S["projected"], 1)
                pe.wait_ge(S["normed_ready"], 2 * k + 1)
                turned(normed, S["normed_turned"])
                pe.wait_ge(S["onT_ready"], k + 1)
                for f in range(HIDDEN // P):
                    nc.tensor.matmul(wide[f][:, :], res.wr1T[:, f * P:(f + 1) * P], onT[:, :],
                                     start=True, stop=True).then_inc(S["hidden"], 1)
                pe.wait_ge(S["hT_ready"], 2 * k + 2)
                for c in range(T):
                    for f in range(HIDDEN // P):
                        last = nc.tensor.matmul(prod[:, c, :], hT[:, f, c * P:(c + 1) * P], res.wr2T[:, f, :],
                                                start=(f == 0), stop=(f == HIDDEN // P - 1))
                last.then_inc(S["reduced"], 1)
                pe.wait_ge(S["normed_ready"], 2 * k + 2)
                turned(normed, S["normed_turned"])
            pe.wait_ge(S["ff_biased"], N)
            pe.wait_ge(S["hT_ready"], 2 * N)
            with pe.Fori(0, N) as k:
                pe.wait_ge(S["x3nT_ready"], N)
                for f in range(FF // P):
                    pe.wait_ge(S["gelu_done"], 4 * k)
                    nc.tensor.matmul(wide[f][:, :], res.w1T[:, f * P:(f + 1) * P],
                                     x3nT[:, ds(k, 1), :].rearrange("p k s -> p (k s)"),
                                     start=True, stop=True).then_inc(S["wide_done"], 1)
                pe.wait_ge(S["gelu_done"], 4 * k + 4)
                pe.wait_ge(S["down_biased"], k)
                for c in range(T):
                    for f in range(FF // P):
                        last = nc.tensor.matmul(prod[:, c, :], gT[:, f, c * P:(c + 1) * P], res.w2T[:, f, :],
                                                start=(f == 0), stop=(f == FF // P - 1))
                last.then_inc(S["down_done"], 1)

        @block.scalar
        def _(act):
            with act.Fori(0, N) as k:
                act.wait_ge(S["att_turned"], k + 1)
                act.wait_ge(S["projected"], k)
                nc.scalar.activation(attT[:, :], turn[:, :], ACT.Copy).then_inc(S["attT_ready"], 1)
                act.wait_ge(S["var_ready"], 2 * k + 1)
                nc.scalar.activation(std[:, :], moments[:, :, 1], ACT.Sqrt).then_inc(S["std_ready"], 1)
                act.wait_ge(S["normed_turned"], 2 * k + 1)
                nc.scalar.activation(onT[:, :], turn[:, :], ACT.Identity, bias=res.colsT[:, C_B2:C_B2 + 1],
                                     scale=res.colsT[:, C_G2:C_G2 + 1]).then_inc(S["onT_ready"], 1)
                for f in range(HIDDEN // P):
                    act.wait_ge(S["hidden"], 2 * k + f + 1)
                    nc.scalar.activation(hT[:, f, :], wide[f][:, :], ACT.Relu,
                                         bias=res.colsT[:, C_BR1 + f:C_BR1 + f + 1]).then_inc(S["hT_ready"], 1)
                act.wait_ge(S["var_ready"], 2 * k + 2)
                nc.scalar.activation(std[:, :], moments[:, :, 1], ACT.Sqrt).then_inc(S["std_ready"], 1)
                act.wait_ge(S["normed_turned"], 2 * k + 2)
                nc.scalar.activation(x3nT[:, ds(k, 1), :].rearrange("p k s -> p (k s)"), turn[:, :],
                                     ACT.Copy).then_inc(S["x3nT_ready"], 1)
            with act.Fori(0, N) as k:
                act.wait_ge(S["down_done"], k)
                for f in range(FF // P):
                    act.wait_ge(S["wide_done"], 4 * k + f + 1)
                    nc.scalar.activation(gT[:, f, :], wide[f][:, :], ACT.Gelu,
                                         bias=res.colsT[:, C_FB1 + f:C_FB1 + f + 1]).then_inc(S["gelu_done"], 1)

        @block.vector
        def _(dve):
            def norm(src, at, k):
                for c in range(T):
                    nc.vector.bn_stats(stats[:, c, :], src(c)).then_inc(S["stats_ready"], 1)
                dve.wait_ge(S["stats_ready"], 2 * T * k + T * at + T).then_inc(S["stood"], 1)
                for c in range(T):
                    nc.vector.bn_aggr(moments[:, c, :], stats[:, c, :]).then_inc(S["moments_ready"], 1)
                dve.wait_ge(S["moments_ready"], 2 * T * k + T * at + T)
                nc.vector.tensor_scalar(moments[:, :, 1], moments[:, :, 1], EPS, None,
                                        ALU.add).then_inc(S["var_ready"], 1)
                dve.wait_ge(S["std_ready"], 2 * k + at + 1)
                nc.vector.reciprocal(rstd[:, :], std[:, :]).then_inc(S["rstd_ready"], 1)
                dve.wait_ge(S["rstd_ready"], 2 * k + at + 1)
                dve.wait_ge(S["normed_turned"], 2 * k + at)
                for c in range(T):
                    last = nc.vector.tensor_scalar(normed[:, c, :], src(c), moments[:, c, 0:1], rstd[:, c:c + 1],
                                                   ALU.subtract, ALU.mult)
                last.then_inc(S["normed_ready"], 1)

            with dve.Fori(0, N) as k:
                dve.wait_ge(S["projected"], k + 1)
                nc.vector.tensor_tensor(x2[:, :, :], prod[:, :, :], again(res.rows[:, R_BF:R_BF + DIM], T),
                                        ALU.add).then_inc(S["biased"], 1)
                dve.wait_ge(S["biased"], k + 1)
                nc.vector.tensor_tensor(x2[:, :, :], x2[:, :, :], tiles(res.y, k), ALU.add).then_inc(S["x2_ready"], 1)
                dve.wait_ge(S["x2_ready"], k + 1).then_inc(S["stood"], 1)
                norm(lambda c: x2[:, c, :], 0, k)
                dve.wait_ge(S["reduced"], k + 1)
                nc.vector.tensor_tensor(x2[:, :, :], prod[:, :, :], x2[:, :, :], ALU.add).then_inc(S["ff_biased"], 1)
                dve.wait_ge(S["ff_biased"], k + 1)
                nc.vector.tensor_tensor(x2[:, :, :], x2[:, :, :], again(res.rows[:, R_BR2:R_BR2 + DIM], T),
                                        ALU.add).then_inc(S["ff_summed"], 1)
                dve.wait_ge(S["ff_summed"], k + 1)
                nc.vector.tensor_tensor(tiles(res.x, k), x2[:, :, :], tiles(res.x, k), ALU.add).then_inc(S["x3_ready"], 1)
                dve.wait_ge(S["x3_ready"], k + 1).then_inc(S["stood"], 1)
                norm(lambda c: res.x[:, ds(k * T + c, 1), :].rearrange("p t d -> p (t d)"), 1, k)
            with dve.Fori(0, N // 2) as m:
                for n in range(2):
                    k = 2 * m + n
                    dve.wait_ge(S["down_done"], k + 1)
                    dve.wait_ge(y_stored[n], DMA * m)
                    nc.vector.tensor_tensor(y_out[:, n, :, :], prod[:, :, :], again(res.rows[:, R_FB2:R_FB2 + DIM], T),
                                            ALU.add).then_inc(S["down_biased"], 1)
                    dve.wait_ge(S["down_biased"], k + 1)
                    nc.vector.tensor_tensor(y_out[:, n, :, :], y_out[:, n, :, :], tiles(res.x, k),
                                            ALU.add).then_inc(S["y_ready"], 1)

        @block.sync
        def _(sp):
            rows = out.rearrange("b (t p) d -> (b t) p d", p=P)
            with sp.Fori(0, N // 2) as m:
                for n in range(2):
                    k = 2 * m + n
                    sp.wait_ge(S["y_ready"], k + 1)
                    sp.dma_start(rows[ds(k * T, T)].rearrange("t p d -> p t d"), y_out[:, n, :, :]).then_inc(y_stored[n], DMA)
            for n in range(2):
                sp.wait_ge(y_stored[n], DMA * N // 2)


def build(nc, args, out):
    ctx = ExitStack()
    with ctx:
        res = Resident(nc, ctx)
        prepare(nc, res, args)
        attention(nc, res)
        feed_forward(nc, res, out)


_NAMES = {
    "L0_attn_x": "x", "L0_attn_Wq": "Wq", "L0_attn_bq": "bq", "L0_attn_Wk": "Wk", "L0_attn_bk": "bk",
    "L0_attn_Wv": "Wv", "L0_attn_bv": "bv", "L0_attn_Wqv": "Wqv", "L0_attn_bqv": "bqv", "L0_attn_Ws": "Ws",
    "L0_attn_bs": "bs", "L0_attn_Wf": "Wf", "L0_attn_bf": "bf", "L0_attn_Wr1": "Wr1", "L0_attn_br1": "br1",
    "L0_attn_Wr2": "Wr2", "L0_attn_br2": "br2", "L0_attn_g1": "g1", "L0_attn_b1": "b1", "L0_attn_g2": "g2",
    "L0_attn_b2": "b2", "L0_ffn_W1": "W1", "L0_ffn_b1": "fb1", "L0_ffn_W2": "W2", "L0_ffn_b2": "fb2",
}


def kernel(**inputs):
    import numpy as _np
    import concourse.bacc as _bacc
    from concourse import mybir as _mybir
    from concourse.bass_utils import run_bass_kernel_spmd as _run

    nc = _bacc.Bacc("TRN2", target_bir_lowering=False, num_devices=1)
    arrays, args = {}, {}
    for name, short in _NAMES.items():
        arr = _np.ascontiguousarray(inputs[name])
        arrays[f"in_{name}"] = arr
        args[short] = nc.dram_tensor(f"in_{name}", arr.shape, _mybir.dt.from_np(arr.dtype), kind="ExternalInput").ap()
    out = nc.dram_tensor("out", (BATCH, SEQ, DIM), _mybir.dt.float32, kind="ExternalOutput").ap()
    build(nc, args, out)
    r = _run(nc, [arrays], core_ids=[0])
    return r.results[0]["out"]
```

```python
import numpy as np
import concourse.bass as bass
from concourse import mybir
from contextlib import ExitStack

FP32 = mybir.dt.float32
BF16 = mybir.dt.bfloat16
ALU = mybir.AluOpType
ACT = mybir.ActivationFunctionType
AX = mybir.AxisListType
ds = bass.ds

BATCH, SEQ, DIM = 4, 1024, 128
HEADS, HD, R, QK = 16, 8, 8, 32
HIDDEN, FF = 2 * DIM, 4 * DIM
P = 128
TB = SEQ // P
TILES = BATCH * TB
U = BATCH * HEADS
SLOTS = 4
GROUPS = U // SLOTS
GPB = HEADS // SLOTS
VW = R * HD
HALF = SEQ // 2
PARTS = 3
PROD_ROWS = PARTS * PARTS * HD
MAX_PARTS = 2
ROWS = PROD_ROWS + MAX_PARTS
PAIR = 2
PAIR_COLS = PAIR * P
PAIRS_BEFORE = TB // PAIR + 1
PAIRS_ALONG = TILES // PAIR - PAIRS_BEFORE
EPS = 1e-5
DMA = 16

C_BQ, C_BK, C_G1, C_B1, C_G2, C_B2, C_BR1, C_FB1, C_BQV, N_COLS = 0, 1, 2, 3, 4, 5, 6, 8, 12, 16
R_BV, R_WS, R_BS, R_BF, R_BR2, R_FB2, N_ROWS = 0, 64, 104, 128, 256, 384, 512


def spread(ap, n):
    return ap.unsqueeze(2).to_broadcast([ap.shape[0], ap.shape[1], n])


def again(ap, n):
    return ap.unsqueeze(1).to_broadcast([ap.shape[0], n, ap.shape[1]])


class Resident:

    def __init__(self, nc, ctx):
        def sb(name, shape, dtype=FP32):
            return ctx.enter_context(nc.sbuf_tensor(name, shape, dtype))
        self.x = sb("x_all", [P, TILES, DIM])
        self.y = sb("y_all", [P, TILES, DIM])
        self.v = sb("v_all", [P, TILES, VW])
        self.qs = sb("qs_all", [P, TILES, HEADS])
        self.att = sb("att_all", [P, BATCH, GPB, TB, SLOTS * HD])
        self.identf = sb("identf", [P, P])
        self.identb = sb("identb", [P, P], BF16)
        self.colsT = sb("colsT", [P, N_COLS])
        self.bq_scaled = sb("bq_scaled", [P, 1])
        self.minus_half = sb("minus_half", [P, HALF // P])
        self.qs_bias = sb("qs_bias", [P, HEADS])
        self.rows = sb("rows", [P, N_ROWS])
        self.qkvT = sb("qkvT", [P, 3 * DIM + VW])
        self.proj = sb("proj", [P, P])
        self.q_parts = nc.dram_tensor("q_parts", [PARTS, U, HD, SEQ], BF16, kind="Internal").ap()
        self.k_parts = nc.dram_tensor("k_parts", [PARTS, U, HD, SEQ], BF16, kind="Internal").ap()


class Projections:

    def __init__(self, nc, ctx, res, name, ring, turned, qk, v):
        def sb(what, shape, dtype=FP32):
            return [ctx.enter_context(nc.sbuf_tensor(f"{name}_{what}{r}", shape, dtype)) for r in range(ring)]

        def sem(what):
            return ctx.enter_context(nc.semaphore(f"{name}_{what}"))
        self.nc, self.res, self.ring = nc, res, ring
        self.turned_bank, self.qk_bank, self.v_bank = turned, qk, v
        self.stats_buf = sb("stats", [P, 2, PAIR, 6])
        self.moment = sb("moment", [P, 2, PAIR, 2])
        self.rstd = sb("rstd", [P, 2, PAIR])
        self.z = sb("z", [P, PAIR, DIM])
        self.xnT = sb("xnT", [P, PAIR_COLS])
        self.full = sb("full", [P, 2, PAIR_COLS])
        self.parts = sb("parts", [P, PARTS, 2, PAIR_COLS], BF16)
        self.stats_done, self.var_ready, self.rstd_ready = sem("stats_done"), sem("var_ready"), sem("rstd_ready")
        self.moment_ready = sem("moment_ready")
        self.y_ready, self.z_ready, self.z_turned, self.xnT_ready = (sem("y_ready"), sem("z_ready"),
                                                                     sem("z_turned"), sem("xnT_ready"))
        self.qk_done, self.full_ready, self.v_done, self.v_ready = (sem("qk_done"), sem("full_ready"),
                                                                    sem("v_done"), sem("v_ready"))
        self.part_ready = [sem(f"part{c}_ready") for c in range(PARTS)]
        self.rest_ready, self.biased, self.stored = sem("rest_ready"), sem("biased"), sem("stored")
        self.stood = sem("stood")

    def at(self, n):
        return n % self.ring if isinstance(n, int) else 0

    def wait_left(self, engine, done, n, each=1):
        if not isinstance(n, int) or n >= self.ring:
            engine.wait_ge(done, each * (n - self.ring + 1))

    def stats(self, dve, n, tile, which):
        src = (self.res.x, self.res.y)[which]
        if which == 1:
            dve.wait_ge(self.y_ready, n + 1).then_inc(self.stood, 1)
        for c in range(PAIR):
            last = self.nc.vector.bn_stats(self.stats_buf[self.at(n)][:, which, c, :],
                                           src[:, ds(tile + c, 1), :].rearrange("p t d -> p (t d)"))
        last.then_inc(self.stats_done, 1)

    def moments(self, dve, n, which):
        dve.wait_ge(self.stats_done, 2 * n + which + 1).then_inc(self.stood, 1)
        m = self.moment[self.at(n)]
        for c in range(PAIR):
            last = self.nc.vector.bn_aggr(m[:, which, c, :], self.stats_buf[self.at(n)][:, which, c, :])
        last.then_inc(self.moment_ready, 1)
        dve.wait_ge(self.moment_ready, 2 * n + which + 1)
        self.nc.vector.tensor_scalar(m[:, which, :, 1], m[:, which, :, 1], EPS, None, ALU.add).then_inc(self.var_ready, 1)

    def normalize(self, dve, n, tile, which):
        res, a = self.res, self.at(n)
        dve.wait_ge(self.rstd_ready, 2 * n + which + 1)
        if which == 1:
            self.wait_left(dve, self.z_turned, n)
        for c in range(PAIR):
            src = (res.x, res.y)[which][:, ds(tile + c, 1), :]
            dst = res.y[:, ds(tile + c, 1), :] if which == 0 else self.z[a][:, c:c + 1, :]
            last = self.nc.vector.tensor_scalar(dst, src, self.moment[a][:, which, c, 0:1],
                                                self.rstd[a][:, which, c:c + 1], ALU.subtract, ALU.mult)
        last.then_inc((self.y_ready, self.z_ready)[which], 1)

    def take_values(self, dve, n, tile):
        dve.wait_ge(self.v_done, n + 1)
        tiles = self.v_bank[self.at(n)][:, 0:PAIR_COLS].rearrange("p (c w) -> p c w", w=P)
        self.nc.vector.tensor_tensor(self.res.v[:, ds(tile, PAIR), :], tiles[:, :, 0:VW],
                                     again(self.res.rows[:, R_BV:R_BV + VW], PAIR), ALU.add)
        self.nc.vector.tensor_tensor(self.res.qs[:, ds(tile, PAIR), :], tiles[:, :, VW:VW + HEADS],
                                     again(self.res.qs_bias[:, :], PAIR), ALU.add).then_inc(self.v_ready, 1)

    def rstd_of(self, pool, n, which):
        pool.wait_ge(self.var_ready, 2 * n + which + 1)
        pool.tensor_tensor(self.rstd[self.at(n)][:, which, :], self.moment[self.at(n)][:, which, :, 1],
                           self.res.minus_half[:, 0:PAIR], ALU.pow).then_inc(self.rstd_ready, 1)

    def rest(self, pool, n, c):
        a = self.at(n)
        pool.wait_ge(self.part_ready[c], n + 1)
        done = self.rest_ready if c == 0 else self.part_ready[2]
        dst = self.full[a][:, :, :] if c == 0 else self.parts[a][:, 2, :, :]
        pool.tensor_tensor(dst, self.full[a][:, :, :], self.parts[a][:, c, :, :], ALU.subtract).then_inc(done, 1)

    def add_biases(self, pool, n, tile):
        res = self.res
        pool.wait_ge(self.z_ready, n + 1).then_inc(self.stood, 1)
        for all_, row in ((res.y, R_BF), (res.x, R_BR2)):
            t = all_[:, ds(tile, PAIR), :]
            pool.tensor_tensor(t, t, again(res.rows[:, row:row + DIM], PAIR), ALU.add).then_inc(self.biased, 1)

    def turn(self, pe, n):
        pe.wait_ge(self.z_ready, n + 1)
        self.wait_left(pe, self.xnT_ready, n)
        for c in range(PAIR):
            last = self.nc.tensor.transpose(self.turned_bank[self.at(n)][:, c * P:(c + 1) * P],
                                            self.z[self.at(n)][:, c, :], self.res.identf[:, :])
        last.then_inc(self.z_turned, 1)

    def qk(self, pe, n):
        pe.wait_ge(self.xnT_ready, n + 1)
        self.wait_left(pe, self.full_ready, n, 2)
        for m in range(2):
            last = self.nc.tensor.matmul(self.qk_bank[self.at(n)][:, m * PAIR_COLS:(m + 1) * PAIR_COLS],
                                         self.res.qkvT[:, m * DIM:(m + 1) * DIM], self.xnT[self.at(n)][:, :],
                                         start=True, stop=True)
        last.then_inc(self.qk_done, 1)

    def values(self, pe, n):
        if self.v_bank is self.qk_bank or self.v_bank[0] is self.qk_bank[0]:
            pe.wait_ge(self.full_ready, 2 * n + 2)
        self.wait_left(pe, self.v_ready, n)
        for c in range(PAIR):
            last = self.nc.tensor.matmul(self.v_bank[self.at(n)][:, c * P:(c + 1) * P],
                                         self.xnT[self.at(n)][:, c * P:(c + 1) * P], self.res.proj[:, :],
                                         start=True, stop=True)
        last.then_inc(self.v_done, 1)

    def take_turned(self, act, n):
        act.wait_ge(self.z_turned, n + 1)
        self.wait_left(act, self.v_done, n)
        self.nc.scalar.activation(self.xnT[self.at(n)][:, :], self.turned_bank[self.at(n)][:, 0:PAIR_COLS],
                                  ACT.Identity, bias=self.res.colsT[:, C_B1:C_B1 + 1],
                                  scale=self.res.colsT[:, C_G1:C_G1 + 1]).then_inc(self.xnT_ready, 1)

    def take_qk(self, act, n, m):
        act.wait_ge(self.qk_done, n + 1)
        self.wait_left(act, self.part_ready[2], n)
        self.nc.scalar.activation(self.full[self.at(n)][:, m, :],
                                  self.qk_bank[self.at(n)][:, m * PAIR_COLS:(m + 1) * PAIR_COLS], ACT.Identity,
                                  bias=self.res.bq_scaled[:, :] if m == 0 else self.res.colsT[:, C_BK:C_BK + 1],
                                  scale=HD ** -0.5 if m == 0 else 1.0).then_inc(self.full_ready, 1)

    def part(self, act, n, c):
        if c == 0:
            act.wait_ge(self.full_ready, 2 * n + 2)
            self.wait_left(act, self.stored, n, 2 * PARTS * DMA)
        else:
            act.wait_ge(self.rest_ready, n + 1)
        self.nc.scalar.activation(self.parts[self.at(n)][:, c, :, :], self.full[self.at(n)][:, :, :],
                                  ACT.Copy).then_inc(self.part_ready[c], 1)

    def store(self, sp, n, pair):
        sp.wait_ge(self.part_ready[2], n + 1)
        for m, dram in enumerate((self.res.q_parts, self.res.k_parts)):
            for c in range(PARTS):
                sp.dma_start(dram[PARTS - 1 - c, ds(pair // (TB // PAIR) * HEADS, HEADS), :,
                                  ds(pair % (TB // PAIR) * PAIR_COLS, PAIR_COLS)].rearrange("h d s -> (h d) s"),
                             self.parts[self.at(n)][:, c, m, :]).then_inc(self.stored, DMA)


def prepare(nc, res, a):
    ctx = ExitStack()
    with ctx:
        def sb(name, shape, dtype=FP32):
            return ctx.enter_context(nc.sbuf_tensor(name, shape, dtype))

        def sem(name):
            return ctx.enter_context(nc.semaphore(name))

        wq_n, wk_n, wf_n = sb("wq_n", [P, DIM]), sb("wk_n", [P, DIM]), sb("wf_n", [P, DIM])
        wv_n = sb("wv_n", [VW, DIM])
        wqv_n = sb("wqv_n", [P, QK * HEADS // P, DIM])
        cols_n = sb("cols_n", [N_COLS, P])
        ws_col = sb("ws_col", [P, 1])
        ones = sb("ones", [P, P])
        sel = sb("sel", [P, SLOTS])
        sel_b = sb("sel_b", [P, HEADS])
        bank = [ctx.enter_context(nc.psum_tensor(f"prep{n}", [P, HALF], FP32)) for n in range(8)]
        project = Projections(nc, ctx, res, "first", 2, turned=bank[0:2], qk=bank[2:4], v=bank[4:6])

        x_in = [sem(f"x_in{n}") for n in range(3)]
        weights_in, rows_in, wf_in = sem("weights_in"), sem("rows_in"), sem("wf_in")
        ident_ready, cleared, sel_ready = sem("ident_ready"), sem("cleared"), sem("sel_ready")
        w_turned, cols_turned, w_copied, cols_ready = (sem("w_turned"), sem("cols_turned"), sem("w_copied"),
                                                       sem("cols_ready"))
        ws_summed, selb_ready, qsb_summed, proj_ready = (sem("ws_summed"), sem("selb_ready"), sem("qsb_summed"),
                                                         sem("proj_ready"))
        qsb_ready, wf_turned, wf_copied = sem("qsb_ready"), sem("wf_turned"), sem("wf_copied")

        cuts = [0, PAIR, PAIR * PAIRS_BEFORE, TILES]
        weights = [(wq_n[:, :], a["Wq"]), (wk_n[:, :], a["Wk"]), (wv_n[:, :], a["Wv"]),
                   (wqv_n[:, :, :], a["Wqv"].rearrange("(k p) d -> p k d", p=P))]
        for at, name, n in ((C_BQ, "bq", 1), (C_BK, "bk", 1), (C_G1, "g1", 1), (C_B1, "b1", 1),
                            (C_G2, "g2", 1), (C_B2, "b2", 1), (C_BR1, "br1", HIDDEN // P),
                            (C_FB1, "fb1", FF // P), (C_BQV, "bqv", QK * HEADS // P)):
            weights.append((cols_n[at:at + n, :], a[name].rearrange("(n p) -> n p", p=P)))
        for n in range(P // QK):
            weights.append((ws_col[n * QK:(n + 1) * QK, :], a["Ws"][0, 0:QK].rearrange("(p n) -> p n", n=1)))
        rows = [(res.rows[:, R_WS:R_WS + QK + HD], a["Ws"][0, :].partition_broadcast(P))]
        for at, name, n in ((R_BV, "bv", VW), (R_BS, "bs", 1), (R_BF, "bf", DIM), (R_BR2, "br2", DIM),
                            (R_FB2, "fb2", DIM)):
            rows.append((res.rows[:, at:at + n], a[name].partition_broadcast(P)))

        block = ctx.enter_context(nc.Block())

        @block.sync
        def _(sp):
            x_tiles = a["x"].rearrange("b (t p) d -> p (b t) d", p=P)

            def load_x(n):
                sp.dma_start(res.x[:, cuts[n]:cuts[n + 1], :], x_tiles[:, cuts[n]:cuts[n + 1], :]).then_inc(x_in[n], DMA)

            load_x(0)
            for dst, src in weights[0::2]:
                sp.dma_start(dst, src).then_inc(weights_in, DMA)
            load_x(1)
            sp.dma_start(wf_n[:, :], a["Wf"]).then_inc(wf_in, DMA)
            load_x(2)
            for n in range(PAIRS_BEFORE):
                project.store(sp, n, n)
            sp.wait_ge(x_in[2], DMA)
            sp.wait_ge(project.stored, DMA * 2 * PARTS * PAIRS_BEFORE)

        @block.gpsimd
        def _(pool):
            for dst, src in rows:
                pool.dma_start(dst, src).then_inc(rows_in, DMA)
            pool.memset(res.identf[:, :], 0.0).then_inc(cleared, 1)
            pool.memset(res.identb[:, :], 0.0).then_inc(cleared, 1)
            pool.memset(sel[:, :], 1.0).then_inc(cleared, 1)
            pool.memset(res.minus_half[:, :], -0.5).then_inc(cleared, 1)
            pool.wait_ge(cleared, 4)
            for ident in (res.identf, res.identb):
                pool.affine_select(out=ident[:, :], in_=ident[:, :], compare_op=ALU.not_equal, fill=1.0,
                                   base=0, pattern=[[-1, P]], channel_multiplier=1).then_inc(ident_ready, 1)
            pool.affine_select(out=sel[:, :], in_=sel[:, :], compare_op=ALU.is_ge, fill=0.0,
                               base=0, pattern=[[-QK, SLOTS]], channel_multiplier=1).then_inc(ident_ready, 1)
            pool.wait_ge(ident_ready, 3)
            pool.affine_select(out=sel[:, :], in_=sel[:, :], compare_op=ALU.is_ge, fill=0.0,
                               base=QK - 1, pattern=[[QK, SLOTS]], channel_multiplier=-1).then_inc(ident_ready, 1)
            for n in range(PAIRS_BEFORE):
                project.rstd_of(pool, n, 0)
                if n > 0:
                    project.rstd_of(pool, n - 1, 1)
            project.rstd_of(pool, PAIRS_BEFORE - 1, 1)
            for n in range(PAIRS_BEFORE):
                project.rest(pool, n, 0)
                project.rest(pool, n, 1)
            pool.wait_ge(rows_in, DMA * len(rows))
            for n in range(PAIRS_BEFORE):
                project.add_biases(pool, n, n * PAIR)

        @block.scalar
        def _(act):
            for dst, src in weights[1::2]:
                act.dma_start(dst, src).then_inc(weights_in, DMA)
            act.wait_ge(w_turned, 1)
            nc.scalar.activation(res.qkvT[:, 0:2 * DIM], bank[6][:, 0:2 * DIM], ACT.Copy).then_inc(w_copied, 1)
            nc.scalar.activation(res.proj[:, 0:VW], bank[6][:, 3 * DIM:3 * DIM + VW], ACT.Copy).then_inc(w_copied, 1)
            act.wait_ge(cols_ready, 2)
            for n in range(PAIRS_BEFORE + 1):
                if n < PAIRS_BEFORE:
                    project.take_turned(act, n)
                    for m in range(2):
                        project.take_qk(act, n, m)
                    project.part(act, n, 0)
                if n > 0:
                    project.part(act, n - 1, 1)
            act.wait_ge(wf_turned, 1)
            nc.scalar.activation(res.qkvT[:, 2 * DIM:3 * DIM], bank[6][:, 2 * DIM:3 * DIM], ACT.Copy).then_inc(wf_copied, 1)

        @block.tensor
        def _(pe):
            pe.wait_ge(ident_ready, 4)
            pe.wait_ge(weights_in, DMA * len(weights))
            nc.tensor.transpose(bank[7][:, 0:N_COLS], cols_n[:, :],
                                res.identf[0:N_COLS, 0:N_COLS]).then_inc(cols_turned, 1)
            for n, w in enumerate((wq_n, wk_n)):
                nc.tensor.transpose(bank[6][:, n * DIM:(n + 1) * DIM], w[:, :], res.identf[:, :])
            nc.tensor.transpose(bank[6][:, 3 * DIM:3 * DIM + VW], wv_n[:, :],
                                res.identf[0:VW, 0:VW]).then_inc(w_turned, 1)
            pe.wait_ge(sel_ready, 1)
            for k in range(QK * HEADS // P):
                last = nc.tensor.matmul(bank[5][:, k * SLOTS:(k + 1) * SLOTS], wqv_n[:, k, :], sel[:, :],
                                        start=True, stop=True)
            last.then_inc(ws_summed, 1)
            pe.wait_ge(selb_ready, 1)
            nc.tensor.matmul(bank[7][:, 128:128 + HEADS], ones[:, :], sel_b[:, :],
                             start=True, stop=True).then_inc(qsb_summed, 1)
            pe.wait_ge(w_copied, 2)
            pe.wait_ge(proj_ready, 2)
            for n in range(PAIRS_BEFORE):
                project.turn(pe, n)
                project.qk(pe, n)
                project.values(pe, n)
            pe.wait_ge(wf_in, DMA)
            nc.tensor.transpose(bank[6][:, 2 * DIM:3 * DIM], wf_n[:, :], res.identf[:, :]).then_inc(wf_turned, 1)

        @block.vector
        def _(dve):
            dve.memset(ones[:, :], 1.0)
            dve.memset(res.proj[:, VW + HEADS:P], 0.0).then_inc(proj_ready, 1)
            dve.wait_ge(x_in[0], DMA)
            project.stats(dve, 0, 0, 0)
            project.moments(dve, 0, 0)
            dve.wait_ge(weights_in, DMA * len(weights))
            dve.wait_ge(ident_ready, 4)
            nc.vector.tensor_scalar(sel[:, :], sel[:, :], ws_col[:, 0:1], None, ALU.mult).then_inc(sel_ready, 1)
            dve.wait_ge(cols_turned, 1)
            nc.vector.tensor_copy(res.colsT[:, :], bank[7][:, 0:N_COLS]).then_inc(cols_ready, 1)
            dve.wait_ge(ws_summed, 1)
            nc.vector.tensor_scalar(res.proj[:, VW:VW + HEADS], bank[5][:, 0:HEADS], QK ** -0.5, None,
                                    ALU.mult).then_inc(proj_ready, 1)
            dve.wait_ge(cols_ready, 1)
            nc.vector.tensor_scalar(res.bq_scaled[:, :], res.colsT[:, C_BQ:C_BQ + 1], HD ** -0.5, None,
                                    ALU.mult).then_inc(cols_ready, 1)
            dve.wait_ge(sel_ready, 1)
            for k in range(QK * HEADS // P):
                last = nc.vector.tensor_scalar(sel_b[:, k * SLOTS:(k + 1) * SLOTS], sel[:, :],
                                               res.colsT[:, C_BQV + k:C_BQV + k + 1], None, ALU.mult)
            last.then_inc(selb_ready, 1)
            dve.wait_ge(qsb_summed, 1)
            dve.wait_ge(rows_in, DMA * len(rows))
            nc.vector.tensor_scalar(res.qs_bias[:, :], bank[7][:, 128:128 + HEADS], QK ** -0.5,
                                    res.rows[:, R_BS:R_BS + 1], ALU.mult, ALU.add).then_inc(qsb_ready, 1)
            dve.wait_ge(x_in[1], DMA)
            for n in range(PAIRS_BEFORE + 2):
                if 0 < n < PAIRS_BEFORE:
                    project.stats(dve, n, n * PAIR, 0)
                    project.moments(dve, n, 0)
                if n < PAIRS_BEFORE:
                    project.normalize(dve, n, n * PAIR, 0)
                    project.stats(dve, n, n * PAIR, 1)
                    project.moments(dve, n, 1)
                if 0 < n <= PAIRS_BEFORE:
                    project.normalize(dve, n - 1, (n - 1) * PAIR, 1)
                if n == 2:
                    dve.wait_ge(qsb_ready, 1)
                if n >= 2:
                    project.take_values(dve, n - 2, (n - 2) * PAIR)


def attention(nc, res):
    ctx = ExitStack()
    with ctx:
        def sb(name, shape, dtype=FP32):
            return ctx.enter_context(nc.sbuf_tensor(name, shape, dtype))

        def pb(name, shape):
            return ctx.enter_context(nc.psum_tensor(name, shape, FP32))

        def sem(name):
            return ctx.enter_context(nc.semaphore(name))

        q_op = [sb(f"q_op{s}", [ROWS, SEQ], BF16) for s in range(SLOTS)]
        k_op = [sb(f"k_op{s}", [P, SEQ], BF16) for s in range(SLOTS)]
        v_op = [sb(f"v_op{s}", [P, TB, VW]) for s in range(SLOTS)]
        prob = sb("prob", [P, TB, SEQ])
        pair = sb("pair", [P, TB // 2, SEQ])
        quad = sb("quad", [P, 2, SEQ])
        rowmax = sb("rowmax", [P, 2, TB, 2])
        negmax = sb("negmax", [P, TB])
        max_parts = sb("max_parts", [P, 2, MAX_PARTS, TB], BF16)
        max_rows = [sb(f"max_rows{n}", [MAX_PARTS * TB, P], BF16) for n in range(2)]
        onehot = sb("onehot", [P, SLOTS, 32])
        outT = [sb(f"outT{n}", [P, HALF]) for n in range(2)]
        denT = sb("denT", [P, HALF])
        mix_in = sb("mix_in", [P, 2, TB, SLOTS, VW])
        product = sb("product", [P, TB * SLOTS, R, HD])
        den = sb("den", [P, TB, SLOTS])
        rden = sb("rden", [P, TB, SLOTS])
        logit = sb("logit", [P, TB * SLOTS, R])
        top = sb("top", [P, TB * SLOTS])
        total = sb("total", [P, TB * SLOTS])

        col_bank = [pb(f"col_bank{n}", [P, HALF]) for n in range(2)]
        row_bank = [pb(f"row_bank{n}", [P, HALF]) for n in range(2)]
        out_bank = [pb(f"out_bank{n}", [P, HALF]) for n in range(2)]
        den_bank = pb("den_bank", [P, HALF])
        turn_bank = pb("turn_bank", [P, HALF])
        project = Projections(nc, ctx, res, "along", 1, turned=[turn_bank], qk=[turn_bank], v=[turn_bank])

        operands_in = [sem(f"operands_in{s}") for s in range(SLOTS)]
        max_in = [sem(f"max_in{s}") for s in range(SLOTS)]
        ones_set, onehot_set = sem("ones_set"), sem("onehot_set")
        col_scored, row_scored = sem("col_scored"), sem("row_scored")
        exp_done, max_done, pv_done = sem("exp_done"), sem("max_done"), sem("pv_done")
        negmax_ready, part1_ready, max_split = sem("negmax_ready"), sem("part1_ready"), sem("max_split")
        max_turned, max_rows_ready = sem("max_turned"), sem("max_rows_ready")
        pair_done, quad_done, den_done = sem("pair_done"), sem("quad_done"), sem("den_done")
        outT_ready, out_turned, mix_in_ready = sem("outT_ready"), sem("out_turned"), sem("mix_in_ready")
        denT_ready, den_turned, den_ready, rden_ready = (sem("denT_ready"), sem("den_turned"), sem("den_ready"),
                                                         sem("rden_ready"))
        logit_product, logit_sum, logit_scaled, logit_ready = (sem("logit_product"), sem("logit_sum"),
                                                               sem("logit_scaled"), sem("logit_ready"))
        top_ready, logit_shifted, mix_exp = sem("top_ready"), sem("logit_shifted"), sem("mix_exp")
        total_ready, rtotal_ready, norm_ready, weight_ready = (sem("total_ready"), sem("rtotal_ready"),
                                                               sem("norm_ready"), sem("weight_ready"))
        mixed, att_done = sem("mixed"), sem("att_done")
        stood = sem("stood_pool")

        LOADS = 2 * PARTS + 1
        halves = lambda t: t.rearrange("p (c h i) -> p c h i", c=TB // 2, h=2)

        block = ctx.enter_context(nc.Block())

        @block.sync
        def _(sp):
            def load(u, b, slot):
                for n in range(PARTS):
                    sp.dma_start(k_op[slot][n * PARTS * HD:(n + 1) * PARTS * HD, :],
                                 res.k_parts[:, ds(u, 1)].rearrange("c u d s -> (c u) d s")).then_inc(operands_in[slot], DMA)
                    sp.dma_start(q_op[slot][n * PARTS * HD:(n + 1) * PARTS * HD, :],
                                 res.q_parts[n, ds(u, 1)].to_broadcast([PARTS, HD, SEQ])).then_inc(operands_in[slot], DMA)
                sp.dma_start(v_op[slot][:, :, :], res.v[:, ds(b * TB, TB), :]).then_inc(operands_in[slot], DMA)

            def put_max(w, slot, parity):
                sp.wait_ge(max_rows_ready, w + 1)
                sp.dma_start(q_op[slot][PROD_ROWS:ROWS, :].rearrange("m (t i) -> m t i", t=TB),
                             max_rows[parity][:, :]).then_inc(max_in[slot], DMA)

            def group(G, first, last, along):
                for s in range(SLOTS):
                    u = G * SLOTS + s
                    if s == 1 and not first and not last:
                        sp.wait_ge(project.stored, 2 * PARTS * DMA * (G if along else PAIRS_ALONG))
                        sp.wait_ge(project.v_ready, G if along else PAIRS_ALONG)
                    if not (last and s >= 1):
                        if not (first and s == 0):
                            sp.wait_ge(pv_done, TB * u)
                        nxt = G if s < 1 else G + 1
                        load(nxt * SLOTS + (s + 3) % SLOTS, nxt // GPB, (s + 3) % SLOTS)
                    if not (last and s == SLOTS - 1):
                        put_max(u + 1, (s + 1) % SLOTS, (s + 1) % 2)
                if along:
                    project.store(sp, G, G + PAIRS_BEFORE)

            sp.wait_ge(ones_set, SLOTS)
            for u in range(3):
                load(u, 0, u)
            put_max(0, 0, 0)
            group(0, True, False, True)
            with sp.Fori(1, PAIRS_ALONG) as G:
                group(G, False, False, True)
            with sp.Fori(PAIRS_ALONG, GROUPS - 1) as G:
                group(G, False, False, False)
            group(GROUPS - 1, False, True, False)

        @block.tensor
        def _(pe):
            def row_scores(v, slot, t, known_free):
                for h in range(2):
                    if not known_free:
                        pe.wait_ge(max_done, 2 * TB * v + 2 * t + h - 1)
                    nc.tensor.matmul(row_bank[h][:, :], q_op[slot][0:PROD_ROWS, t * P:(t + 1) * P],
                                     k_op[slot][0:PROD_ROWS, h * HALF:(h + 1) * HALF],
                                     start=True, stop=True).then_inc(row_scored, 1)

            def turn_max(w, parity):
                pe.wait_ge(max_split, w + 1)
                pe.wait_ge(max_rows_ready, w)
                nc.tensor.matmul(turn_bank[0:MAX_PARTS * TB, 0:P],
                                 max_parts[:, parity, :, :].rearrange("p m t -> p (m t)"),
                                 res.identb[:, :], start=True, stop=True).then_inc(max_turned, 1)

            def col_scores(u, slot, t, known_free):
                for h in range(2):
                    if not known_free:
                        pe.wait_ge(exp_done, 2 * TB * u + 2 * t + h - 1)
                    nc.tensor.matmul(col_bank[h][:, :], k_op[slot][0:ROWS, t * P:(t + 1) * P],
                                     q_op[slot][0:ROWS, h * HALF:(h + 1) * HALF],
                                     start=True, stop=True).then_inc(col_scored, 1)

            def values(u, slot, t):
                pe.wait_ge(exp_done, 2 * TB * u + 2 * t + 2)
                for ih in range(2):
                    last = nc.tensor.matmul(out_bank[slot % 2][ih * VW:(ih + 1) * VW, :], v_op[slot][:, t, :],
                                            halves(prob[:, t, :])[:, :, ih, :], start=(t == 0), stop=(t == TB - 1))
                last.then_inc(pv_done, 1)

            def denominators(u, slot):
                pe.wait_ge(quad_done, 4 * u + 4)
                for ih in range(2):
                    for k in range(2):
                        q = 32 * (2 * ih + k)
                        last = nc.tensor.matmul(den_bank[q:q + 32, :], onehot[:, slot, :],
                                                halves(quad[:, k, :])[:, :, ih, :],
                                                start=(slot == 0), stop=(slot == SLOTS - 1))
                last.then_inc(den_done, 1)

            def turn_out(u, parity):
                pe.wait_ge(outT_ready, u + 1)
                for c in range(TB // 2):
                    last = nc.tensor.transpose(out_bank[parity][:, c * P:(c + 1) * P],
                                               outT[parity][:, c * P:(c + 1) * P], res.identf[:, :])
                last.then_inc(out_turned, 1)

            def turn_den(G):
                pe.wait_ge(denT_ready, G + 1)
                for c in range(TB // 2):
                    last = nc.tensor.transpose(turn_bank[:, c * P:(c + 1) * P], denT[:, c * P:(c + 1) * P],
                                               res.identf[:, :])
                last.then_inc(den_turned, 1)

            def group(G, first, last, along):
                for s in range(SLOTS):
                    u = G * SLOTS + s
                    before = not (first and s == 0)
                    ahead = not (last and s >= 2)
                    Gv, sv, sp_ = (G if s < 2 else G + 1), (s + 2) % SLOTS, (s - 1) % SLOTS
                    for t in range(TB):
                        if t == 0:
                            pe.wait_ge(max_in[s], DMA * (G + 1))
                        col_scores(u, s, t, not before and t == 0)
                        if ahead:
                            if t == 0:
                                pe.wait_ge(operands_in[sv], LOADS * DMA * (Gv + 1))
                            row_scores(u + 2, sv, t, False)
                        if t > 0:
                            if t == 1 and not (first and s < 2):
                                pe.wait_ge(mix_in_ready, u - 1)
                            values(u, s, t - 1)
                        elif before:
                            values(u - 1, sp_, TB - 1)
                        if t == 1 and not (last and s == SLOTS - 1):
                            if s == 1 and not first:
                                pe.wait_ge(den_ready, G)
                            if s == 3 and along:
                                pe.wait_ge(project.v_ready, G + 1)
                            turn_max(u + 1, (s + 1) % 2)
                        if t == 2 and before:
                            turn_out(u - 1, sp_ % 2)
                        if t == 4 and before:
                            if s == 1 and not first:
                                pe.wait_ge(denT_ready, G)
                            denominators(u - 1, sp_)
                        if t == 6 and s == 0 and not first:
                            pe.wait_ge(max_rows_ready, u + 2)
                            turn_den(G - 1)
                        if along and (s, t) == (1, 6):
                            pe.wait_ge(max_rows_ready, u + 2)
                            project.turn(pe, G)
                        if along and (s, t) == (2, 4):
                            pe.wait_ge(max_rows_ready, u + 2)
                            project.qk(pe, G)
                        if along and (s, t) == (2, 7):
                            project.values(pe, G)

            pe.wait_ge(operands_in[0], LOADS * DMA)
            for t in range(TB):
                row_scores(0, 0, t, t == 0)
            pe.wait_ge(operands_in[1], LOADS * DMA)
            for t in range(TB):
                row_scores(1, 1, t, False)
                if t == 3:
                    pe.wait_ge(max_split, 1)
                    nc.tensor.matmul(turn_bank[0:MAX_PARTS * TB, 0:P],
                                     max_parts[:, 0, :, :].rearrange("p m t -> p (m t)"),
                                     res.identb[:, :], start=True, stop=True).then_inc(max_turned, 1)
            pe.wait_ge(onehot_set, 2)
            group(0, True, False, True)
            with pe.Fori(1, PAIRS_ALONG) as G:
                group(G, False, False, True)
            with pe.Fori(PAIRS_ALONG, GROUPS - 1) as G:
                group(G, False, False, False)
            group(GROUPS - 1, False, True, False)
            values(U - 1, SLOTS - 1, TB - 1)
            turn_out(U - 1, 1)
            denominators(U - 1, SLOTS - 1)
            turn_den(GROUPS - 1)

        @block.scalar
        def _(act):
            def take_out(u, parity):
                act.wait_ge(pv_done, TB * u + TB)
                nc.scalar.activation(outT[parity][:, :], out_bank[parity][:, :], ACT.Copy).then_inc(outT_ready, 1)

            def take_turned(u, G, slot):
                act.wait_ge(out_turned, u + 1)
                nc.scalar.activation(mix_in[:, ds(G % 2, 1), :, slot, :].rearrange("p g e w -> p (g e) w"),
                                     out_bank[slot % 2][:, :].rearrange("p (e w) -> p e w", w=VW),
                                     ACT.Copy).then_inc(mix_in_ready, 1)

            def take_den(G):
                act.wait_ge(den_done, SLOTS * G + SLOTS)
                nc.scalar.activation(denT[:, :], den_bank[:, :], ACT.Copy).then_inc(denT_ready, 1)

            def mix_exps(G):
                act.wait_ge(logit_shifted, G + 1)
                nc.scalar.activation(logit[:, :, :], logit[:, :, :], ACT.Exp).then_inc(mix_exp, 1)

            def take_rows(w, parity, slot_before, G_before):
                act.wait_ge(max_turned, w + 1)
                if slot_before is not None:
                    act.wait_ge(max_in[slot_before], DMA * (G_before + 1))
                nc.scalar.activation(max_rows[parity][:, :], turn_bank[0:MAX_PARTS * TB, 0:P],
                                     ACT.Copy).then_inc(max_rows_ready, 1)

            def group(G, first, last, along):
                for s in range(SLOTS):
                    u = G * SLOTS + s
                    before = not (first and s == 0)
                    for t in range(TB):
                        for h in range(2):
                            if h == 0 and before:
                                act.wait_ge(pv_done, TB * u - TB + t + 1)
                                act.wait_ge(pair_done, TB // 2 * u - TB // 2 + t // 2 + 1)
                            act.wait_ge(col_scored, 2 * TB * u + 2 * t + h + 1)
                            nc.scalar.activation(prob[:, t, h * HALF:(h + 1) * HALF], col_bank[h][:, :],
                                                 ACT.Exp).then_inc(exp_done, 1)
                        if t == 1 and not (last and s == SLOTS - 1):
                            sent = s >= 1 or not first
                            take_rows(u + 1, (s + 1) % 2, (s - 1) % SLOTS if sent else None, G if s >= 1 else G - 1)
                        if t == 1 and before:
                            take_out(u - 1, (s - 1) % 2)
                        if t == 3 and before:
                            if s == 1 and not first:
                                act.wait_ge(att_done, G)
                            take_turned(u - 1, G if s > 0 else G - 1, (s - 1) % SLOTS)
                        if t == 5 and s == 0 and not first:
                            take_den(G - 1)
                        if t == 3 and s == 2 and not first:
                            mix_exps(G - 1)
                        if along and (s, t) == (1, 7):
                            project.take_turned(act, G)
                        if along and (s, t) in ((2, 5), (2, 6)):
                            project.take_qk(act, G, t - 5)
                        if along and (s, t) == (3, 0):
                            project.part(act, G, 0)
                        if along and (s, t) == (3, 4):
                            project.part(act, G, 1)

            take_rows(0, 0, None, 0)
            group(0, True, False, True)
            with act.Fori(1, PAIRS_ALONG) as G:
                group(G, False, False, True)
            with act.Fori(PAIRS_ALONG, GROUPS - 1) as G:
                group(G, False, False, False)
            group(GROUPS - 1, False, True, False)
            take_out(U - 1, 1)
            take_turned(U - 1, GROUPS - 1, SLOTS - 1)
            take_den(GROUPS - 1)
            mix_exps(GROUPS - 1)

        @block.vector
        def _(dve):
            def row_max(v, parity, t):
                for h in range(2):
                    dve.wait_ge(row_scored, 2 * TB * v + 2 * t + h + 1)
                    nc.vector.tensor_reduce(rowmax[:, parity, t, h:h + 1], row_bank[h][:, :], AX.X,
                                            ALU.max).then_inc(max_done, 1)

            def split_max(w, parity):
                dve.wait_ge(max_done, 2 * TB * w + 2 * TB)
                nc.vector.tensor_reduce(negmax[:, :], rowmax[:, parity, :, :], AX.X, ALU.max,
                                        negate=True).then_inc(negmax_ready, 1)
                dve.wait_ge(negmax_ready, w + 1)
                nc.vector.tensor_copy(max_parts[:, parity, 0, :], negmax[:, :]).then_inc(part1_ready, 1)
                dve.wait_ge(part1_ready, w + 1)
                nc.vector.tensor_tensor(max_parts[:, parity, 1, :], negmax[:, :], max_parts[:, parity, 0, :],
                                        ALU.subtract).then_inc(max_split, 1)

            def quads(u, k, h, known_free):
                dve.wait_ge(pair_done, TB // 2 * u + 2 * k + 2)
                if not known_free:
                    dve.wait_ge(den_done, u)
                part = slice(h * HALF, (h + 1) * HALF)
                nc.vector.tensor_tensor(quad[:, k, part], pair[:, 2 * k, part], pair[:, 2 * k + 1, part],
                                        ALU.add).then_inc(quad_done, 1)

            def mixing(G, b, g, step):
                E = TB * SLOTS
                flat = lambda x: x[:, :, :].rearrange("p e s -> p (e s)")
                if step == 0:
                    dve.wait_ge(den_turned, G + 1)
                    nc.vector.tensor_reduce(den[:, :, :], turn_bank[:, :].rearrange("p (e k s) -> p e s k", k=2, s=32)
                                            [:, :, 0:SLOTS, :], AX.X, ALU.add).then_inc(den_ready, 1)
                    dve.wait_ge(den_ready, G + 1)
                    nc.vector.reciprocal(flat(rden), flat(den)).then_inc(rden_ready, 1)
                elif step in (1, 2, 3, 4):
                    n, part = step - 1, slice((step - 1) * TB, step * TB)
                    dve.wait_ge(logit_product, G + 1)
                    nc.vector.tensor_reduce(logit[:, part, :], product[:, part, :, :], AX.X,
                                            ALU.add).then_inc(logit_sum, 1)
                elif step == 5:
                    dve.wait_ge(logit_sum, 4 * G + 4)
                    dve.wait_ge(rden_ready, G + 1)
                    nc.vector.tensor_tensor(logit[:, :, :], logit[:, :, :], spread(flat(rden), R),
                                            ALU.mult).then_inc(logit_scaled, 1)
                elif step == 6:
                    dve.wait_ge(logit_scaled, G + 1)
                    nc.vector.tensor_tensor(
                        logit[:, :, :].rearrange("p (e s) r -> p e s r", s=SLOTS),
                        logit[:, :, :].rearrange("p (e s) r -> p e s r", s=SLOTS),
                        res.qs[:, ds(b * TB, TB), ds(g * SLOTS, SLOTS)].unsqueeze(3)
                        .to_broadcast([P, TB, SLOTS, R]), ALU.add).then_inc(logit_ready, 1)
                elif step == 7:
                    dve.wait_ge(logit_ready, G + 1)
                    nc.vector.tensor_reduce(top[:, :], logit[:, :, :], AX.X, ALU.max).then_inc(top_ready, 1)
                elif step == 8:
                    dve.wait_ge(top_ready, G + 1)
                    nc.vector.tensor_tensor(logit[:, :, :], logit[:, :, :], spread(top[:, :], R),
                                            ALU.subtract).then_inc(logit_shifted, 1)
                elif step == 9:
                    dve.wait_ge(mix_exp, G + 1)
                    nc.vector.tensor_reduce(total[:, :], logit[:, :, :], AX.X, ALU.add).then_inc(total_ready, 1)
                elif step == 10:
                    dve.wait_ge(total_ready, G + 1)
                    nc.vector.reciprocal(total[:, :], total[:, :]).then_inc(rtotal_ready, 1)
                    dve.wait_ge(rtotal_ready, G + 1)
                    nc.vector.tensor_tensor(total[:, :], total[:, :], flat(rden), ALU.mult).then_inc(norm_ready, 1)
                elif step == 11:
                    dve.wait_ge(norm_ready, G + 1)
                    nc.vector.tensor_tensor(logit[:, :, :], logit[:, :, :], spread(total[:, :], R),
                                            ALU.mult).then_inc(weight_ready, 1)
                elif step in (12, 13, 14, 15):
                    n = step - 12
                    dve.wait_ge(mixed, G + 1)
                    last = nc.vector.tensor_reduce(
                        res.att[:, ds(b, 1), ds(g, 1), 2 * n:2 * n + 2, :].rearrange("p b g e (s d) -> p (b g e s) d", d=HD),
                        product[:, n * TB:(n + 1) * TB, :, :].rearrange("p m r d -> p m d r"), AX.X, ALU.add)
                    if n == 3:
                        last.then_inc(att_done, 1)

            PLAN = {(0, 7): [0], (1, 0): [1], (1, 1): [2], (1, 4): [3], (1, 5): [4], (2, 0): [5], (2, 1): [6, 7],
                    (2, 2): [8], (2, 4): [9, 10], (2, 5): [11], (3, 0): [12], (3, 1): [13], (3, 4): [14], (3, 5): [15]}

            def group(G, first, last, along):
                for s in range(SLOTS):
                    u = G * SLOTS + s
                    before = not (first and s == 0)
                    ahead = not (last and s >= 2)
                    for t in range(TB):
                        if t == 0 and not (last and s == SLOTS - 1):
                            split_max(u + 1, (s + 1) % 2)
                        if ahead:
                            row_max(u + 2, s % 2, t)
                        if t in (2, 3) and before:
                            quads(u - 1, 1, t - 2, first and s == 1)
                        if t in (6, 7):
                            quads(u, 0, t - 6, first and s == 0)
                        if not first:
                            for step in PLAN.get((s, t), ()):
                                mixing(G - 1, (G - 1) // GPB, (G - 1) % GPB, step)
                        if along:
                            tile = (G + PAIRS_BEFORE) * PAIR
                            if (s, t) == (0, 0):
                                project.stats(dve, G, tile, 0)
                            elif (s, t) == (0, 1):
                                project.moments(dve, G, 0)
                            elif (s, t) == (0, 4):
                                project.normalize(dve, G, tile, 0)
                            elif (s, t) == (0, 5):
                                project.stats(dve, G, tile, 1)
                                project.moments(dve, G, 1)
                            elif (s, t) == (1, 3):
                                project.normalize(dve, G, tile, 1)
                            elif (s, t) == (3, 0):
                                project.take_values(dve, G, tile)

            dve.sem_inc(att_done, 1)
            for s in range(SLOTS):
                dve.memset(k_op[s][64:P, :], 1.0).then_inc(ones_set, 1)
            dve.memset(onehot[:, :, :], 0.0).then_inc(onehot_set, 1)
            dve.wait_ge(onehot_set, 1)
            for s in range(SLOTS):
                last = dve.memset(onehot[:, s, s:s + 1], 1.0)
            last.then_inc(onehot_set, 1)
            for t in range(TB):
                row_max(0, 0, t)
            split_max(0, 0)
            for t in range(TB):
                row_max(1, 1, t)
            group(0, True, False, True)
            with dve.Fori(1, PAIRS_ALONG) as G:
                group(G, False, False, True)
            with dve.Fori(PAIRS_ALONG, GROUPS - 1) as G:
                group(G, False, False, False)
            group(GROUPS - 1, False, True, False)
            quads(U - 1, 1, 0, False)
            quads(U - 1, 1, 1, False)
            for step in range(16):
                mixing(GROUPS - 1, BATCH - 1, GPB - 1, step)

        @block.gpsimd
        def _(pool):
            def pairs(u, k, known_free):
                pool.wait_ge(exp_done, 2 * TB * u + 4 * k + 4)
                if not known_free:
                    pool.wait_ge(quad_done, 4 * u - 2 + 2 * (k // 2))
                pool.tensor_tensor(pair[:, k, :], prob[:, 2 * k, :], prob[:, 2 * k + 1, :],
                                   ALU.add).then_inc(pair_done, 1)

            def values_of(G):
                return mix_in[:, ds(G % 2, 1), :, :, :].rearrange("p g e s w -> p (g e s) w")

            def logit_products(G):
                pool.wait_ge(mix_in_ready, SLOTS * G + SLOTS)
                pool.wait_ge(att_done, G + 1).then_inc(stood, 1)
                pool.tensor_tensor(
                    product[:, :, :, :].rearrange("p m r d -> p (m r) d"),
                    values_of(G).rearrange("p m (r d) -> p (m r) d", d=HD),
                    again(res.rows[:, R_WS + QK:R_WS + QK + HD], TB * SLOTS * R),
                    ALU.mult).then_inc(logit_product, 1)

            def mix(G):
                pool.wait_ge(weight_ready, G + 1).then_inc(stood, 1)
                pool.tensor_tensor(
                    product[:, :, :, :].rearrange("p m r d -> p (m r) d"),
                    values_of(G).rearrange("p m (r d) -> p (m r) d", d=HD),
                    spread(logit[:, :, :].rearrange("p m r -> p (m r)"), HD),
                    ALU.mult).then_inc(mixed, 1)

            def group(G, first, along):
                for s in range(SLOTS):
                    u = G * SLOTS + s
                    for k in range(TB // 2):
                        pairs(u, k, first and s == 0)
                        if along and s == 0 and k == 0:
                            project.rstd_of(pool, G, 0)
                        if k == 1 and s == 0 and not first:
                            logit_products(G - 1)
                        if along and s == 0 and k == 2:
                            project.rstd_of(pool, G, 1)
                        if along and s == 1 and k == 2:
                            project.add_biases(pool, G, (G + PAIRS_BEFORE) * PAIR)
                        if k == 2 and s == 2 and not first:
                            mix(G - 1)
                        if along and s == 3 and k in (0, 2):
                            project.rest(pool, G, k // 2)

            group(0, True, True)
            with pool.Fori(1, PAIRS_ALONG) as G:
                group(G, False, True)
            with pool.Fori(PAIRS_ALONG, GROUPS) as G:
                group(G, False, False)
            logit_products(GROUPS - 1)
            mix(GROUPS - 1)


def feed_forward(nc, res, a, out):
    ctx = ExitStack()
    with ctx:
        def sb(name, shape, dtype=FP32):
            return ctx.enter_context(nc.sbuf_tensor(name, shape, dtype))

        def sem(name):
            return ctx.enter_context(nc.semaphore(name))

        CREDIT = 2
        events = lambda n: n + CREDIT
        T = HALF // P
        N = TILES // T
        HT, FT = HIDDEN // P, FF // P
        pair = lambda name, shape, dtype=FP32: [sb(f"{name}{n}", shape, dtype) for n in range(2)]
        att, attT, normed = pair("att", [P, T, DIM]), pair("attT", [P, HALF]), pair("normed", [P, T, DIM])
        stats, moments, rstd = pair("ff_stats", [P, T, 6]), pair("ff_moments", [P, T, 2]), pair("ff_rstd", [P, T])
        onT = sb("onT", [P, N, HALF])
        hT = pair("hT", [P, HT, HALF])
        x3nT = sb("x3nT", [P, N, HALF])
        gT = pair("gT", [P, FT, HALF])
        y_out = pair("y_out", [P, T, DIM])
        wr1_n, wr2_n = sb("wr1_n", [P, HT, DIM]), sb("wr2_n", [P, HIDDEN])
        w1_n, w2_n = sb("w1_n", [P, FT, DIM]), sb("w2_n", [P, FF])
        wr1T, wr2T = sb("wr1T", [P, HIDDEN]), sb("wr2T", [P, HT, DIM])
        w1T, w2T = sb("w1T", [P, FF]), sb("w2T", [P, FT, DIM])
        ones = sb("ff_ones", [P, P])
        absum = sb("absum", [P, 2])
        scale = sb("scale", [P, 2, 2])
        above, below = sb("above", [P, FF]), sb("below", [P, FF])

        psum = lambda name: ctx.enter_context(nc.psum_tensor(name, [P, HALF], FP32))
        turn = [psum(f"ff_turn{n}") for n in range(2)]
        prod = [psum(f"ff_prod{n}") for n in range(2)]
        wide = [psum(f"ff_wide{n}") for n in range(FT)]

        by_engine = {
            "pool": "att_copied rstd_ready fb2_added",
            "pe": "att_turned projected normed_turned hidden reduced wide_done down_done",
            "act": "attT_ready onT_ready hT_ready x3nT_ready gelu_done",
            "dve": "x2_ready stats_ready moments_ready var_ready normed_ready x3_part x3_ready y_ready",
        }
        S = {n: sem(n) for names in by_engine.values() for n in names.split()}
        stood = sem("ff_stood")
        weights_in, weights_turned, weights_copied = sem("ff_weights_in"), sem("ff_weights_turned"), sem("ff_weights_copied")
        ones_set, absum_ready, absum_total = sem("ff_ones_set"), sem("absum_ready"), sem("absum_total")
        scale_ready, tern_step = sem("scale_ready"), sem("tern_step")
        y_stored = [sem(f"y_stored{n}") for n in range(2)]
        block = ctx.enter_context(nc.Block())

        def start(engine, name):
            for s in by_engine[name].split():
                engine.sem_inc(S[s], CREDIT)

        def tiles(r, k):
            return r[:, ds(k * T, T), :]

        def flat(t):
            return t[:, :, :].rearrange("p t d -> p (t d)")

        def blocks(engine, body, before=None, after=None):
            if before:
                before()
            for k in range(2):
                body(k, k, k == 0, False)
            with engine.Fori(1, N // 2 - 1) as m:
                for n in range(2):
                    body(2 * m + n, n, False, False)
            for k in range(N - 2, N):
                body(k, k % 2, False, k == N - 1)
            if after:
                after()

        weights = [(wr1_n[:, :, :], a["Wr1"].rearrange("(k p) d -> p k d", p=P)), (wr2_n[:, :], a["Wr2"]),
                   (w1_n[:, :, :], a["W1"].rearrange("(k p) d -> p k d", p=P)), (w2_n[:, :], a["W2"])]

        @block.sync
        def _(sp):
            for dst, src in weights:
                sp.dma_start(dst, src).then_inc(weights_in, DMA)
            rows = out.rearrange("b (t p) d -> (b t) p d", p=P)

            def store(k, n, first, last):
                sp.wait_ge(S["y_ready"], events(k + 1))
                sp.dma_start(rows[ds(k * T, T)].rearrange("t p d -> p t d"), y_out[n][:, :, :]).then_inc(y_stored[n], DMA)

            blocks(sp, store)
            for n in range(2):
                sp.wait_ge(y_stored[n], DMA * N // 2)

        @block.gpsimd
        def _(pool):
            start(pool, "pool")

            def copy_att(k, n):
                if not isinstance(k, int) or k >= 2:
                    pool.wait_ge(S["att_turned"], events(k - 1)).then_inc(stood, 1)
                for g in range(GPB):
                    last = pool.tensor_copy(att[n][:, :, g * SLOTS * HD:(g + 1) * SLOTS * HD],
                                            res.att[:, ds(k // 2, 1), g, ds((k % 2) * T, T), :]
                                            .rearrange("p b e w -> p (b e) w"))
                last.then_inc(S["att_copied"], 1)

            def root(k, n, at):
                pool.wait_ge(S["var_ready"], events(N * at + k + 1))
                pool.tensor_tensor(rstd[n][:, :], moments[n][:, :, 1], res.minus_half[:, :],
                                   ALU.pow).then_inc(S["rstd_ready"], 1)

            def norm2(k, n, first, last):
                root(k, n, 0)
                if not last:
                    copy_att(k + 1, 1 - n)

            def norm3(k, n, first, last):
                root(k, n, 1)
                if not first:
                    add_fb2(k - 1)

            def add_fb2(k):
                pool.wait_ge(S["normed_ready"], events(N + k + 1)).then_inc(stood, 1)
                pool.tensor_tensor(tiles(res.x, k), tiles(res.x, k), again(res.rows[:, R_FB2:R_FB2 + DIM], T),
                                   ALU.add).then_inc(S["fb2_added"], 1)

            blocks(pool, norm2, before=lambda: copy_att(0, 0))
            pool.wait_ge(scale_ready, 3)
            for n, w in enumerate((w1T[:, :], flat(w2T))):
                if n > 0:
                    pool.wait_ge(tern_step, 5 * n)
                pool.tensor_scalar(above[:, :], w, scale[:, n, 0:1], None, ALU.is_gt).then_inc(tern_step, 1)
                pool.tensor_scalar(below[:, :], w, scale[:, n, 1:2], None, ALU.is_lt).then_inc(tern_step, 1)
                pool.wait_ge(tern_step, 5 * n + 2)
                pool.tensor_tensor(above[:, :], above[:, :], below[:, :], ALU.subtract).then_inc(tern_step, 1)
                pool.wait_ge(tern_step, 5 * n + 3)
                pool.tensor_tensor(above[:, :], above[:, :], w, ALU.subtract).then_inc(tern_step, 1)
                pool.wait_ge(tern_step, 5 * n + 4)
                pool.tensor_tensor(w, w, above[:, :], ALU.add).then_inc(tern_step, 1)
            blocks(pool, norm3, after=lambda: add_fb2(N - 1))

        @block.tensor
        def _(pe):
            start(pe, "pe")

            def turned(bank, src, done):
                for c in range(T):
                    last = nc.tensor.transpose(bank[:, c * P:(c + 1) * P], src[:, c, :], res.identf[:, :])
                last.then_inc(done, 1)

            def project(k, n):
                pe.wait_ge(S["att_copied"], events(k + 1))
                if not isinstance(k, int) or k >= 1:
                    pe.wait_ge(S["attT_ready"], events(k))
                turned(turn[0], att[n], S["att_turned"])
                pe.wait_ge(S["attT_ready"], events(k + 1))
                if not isinstance(k, int) or k >= 2:
                    pe.wait_ge(S["x2_ready"], events(k - 1))
                for c in range(T):
                    last = nc.tensor.matmul(prod[n][:, c * P:(c + 1) * P], attT[n][:, c * P:(c + 1) * P],
                                            res.qkvT[:, 2 * DIM:3 * DIM], start=True, stop=True)
                last.then_inc(S["projected"], 1)

            def norm2(k, n, first, last):
                if not last:
                    project(k + 1, 1 - n)
                pe.wait_ge(S["normed_ready"], events(k + 1))
                if not first:
                    pe.wait_ge(S["onT_ready"], events(k))
                turned(turn[1], normed[n], S["normed_turned"])

            def hidden(k, n):
                for f in range(HT):
                    if not isinstance(k, int) or k >= 2:
                        pe.wait_ge(S["hT_ready"], events(2 * k - 2))
                    nc.tensor.matmul(wide[HT * n + f][:, :], wr1T[:, f * P:(f + 1) * P], onT[:, ds(k, 1), :]
                                     .rearrange("p k s -> p (k s)"), start=True, stop=True).then_inc(S["hidden"], 1)

            def turn_x3(k, n):
                pe.wait_ge(S["normed_ready"], events(N + k + 1))
                if not isinstance(k, int) or k >= 2:
                    pe.wait_ge(S["x3nT_ready"], events(k - 1))
                turned(turn[n], normed[n], S["normed_turned"])

            def relu_layer(k, n, first, last):
                if not last:
                    hidden(k + 1, 1 - n)
                pe.wait_ge(S["hT_ready"], events(2 * k + 2))
                if not isinstance(k, int) or k >= 2:
                    pe.wait_ge(S["x3_part"], events(k - 1))
                for c in range(T):
                    for f in range(HT):
                        last_mm = nc.tensor.matmul(prod[n][:, c * P:(c + 1) * P], hT[n][:, f, c * P:(c + 1) * P],
                                                   wr2T[:, f, :], start=(f == 0), stop=(f == HT - 1))
                last_mm.then_inc(S["reduced"], 1)
                if not first:
                    turn_x3(k - 1, 1 - n)

            def ternary_up(k):
                for f in range(FT):
                    if not isinstance(k, int) or k >= 1:
                        pe.wait_ge(S["gelu_done"], events(FT * k - FT + f + 1))
                    nc.tensor.matmul(wide[f][:, :], w1T[:, f * P:(f + 1) * P], x3nT[:, ds(k, 1), :]
                                     .rearrange("p k s -> p (k s)"), start=True, stop=True).then_inc(S["wide_done"], 1)

            def gelu_layer(k, n, first, last):
                if not last:
                    ternary_up(k + 1)
                pe.wait_ge(S["gelu_done"], events(FT * k + FT))
                if not isinstance(k, int) or k >= 2:
                    pe.wait_ge(S["y_ready"], events(k - 1))
                for c in range(T):
                    for f in range(FT):
                        last_mm = nc.tensor.matmul(prod[n][:, c * P:(c + 1) * P], gT[n][:, f, c * P:(c + 1) * P],
                                                   w2T[:, f, :], start=(f == 0), stop=(f == FT - 1))
                last_mm.then_inc(S["down_done"], 1)

            project(0, 0)
            pe.wait_ge(weights_in, DMA * len(weights))
            for k in range(HT):
                nc.tensor.transpose(wide[0][:, k * P:(k + 1) * P], wr1_n[:, k, :], res.identf[:, :])
            for k in range(HT):
                last = nc.tensor.transpose(wide[1][:, k * P:(k + 1) * P], wr2_n[:, k * P:(k + 1) * P], res.identf[:, :])
            last.then_inc(weights_turned, 1)
            for k in range(FT):
                nc.tensor.transpose(wide[2][:, k * P:(k + 1) * P], w1_n[:, k, :], res.identf[:, :])
            for k in range(FT):
                last = nc.tensor.transpose(wide[3][:, k * P:(k + 1) * P], w2_n[:, k * P:(k + 1) * P], res.identf[:, :])
            last.then_inc(weights_turned, 1)
            blocks(pe, norm2)
            pe.wait_ge(weights_copied, 4)
            pe.wait_ge(absum_ready, 2)
            nc.tensor.matmul(wide[3][:, 0:2], ones[:, :], absum[:, :], start=True, stop=True).then_inc(absum_total, 1)
            pe.wait_ge(S["onT_ready"], events(N))
            pe.wait_ge(S["x2_ready"], events(N))
            pe.wait_ge(scale_ready, 1)
            blocks(pe, relu_layer, before=lambda: hidden(0, 0), after=lambda: turn_x3(N - 1, 1))
            pe.wait_ge(S["hT_ready"], events(2 * N))
            pe.wait_ge(S["x3nT_ready"], events(N))
            pe.wait_ge(S["x3_part"], events(N))
            pe.wait_ge(tern_step, 10)
            blocks(pe, gelu_layer, before=lambda: ternary_up(0))

        @block.scalar
        def _(act):
            start(act, "act")

            def take_att(k, n):
                act.wait_ge(S["att_turned"], events(k + 1))
                if not isinstance(k, int) or k >= 2:
                    act.wait_ge(S["projected"], events(k - 1))
                nc.scalar.activation(attT[n][:, :], turn[0][:, :], ACT.Copy).then_inc(S["attT_ready"], 1)

            def norm2(k, n, first, last):
                if not last:
                    take_att(k + 1, 1 - n)
                act.wait_ge(S["normed_turned"], events(k + 1)).then_inc(stood, 1)
                nc.scalar.activation(onT[:, ds(k, 1), :].rearrange("p k s -> p (k s)"), turn[1][:, :], ACT.Identity,
                                     bias=res.colsT[:, C_B2:C_B2 + 1],
                                     scale=res.colsT[:, C_G2:C_G2 + 1]).then_inc(S["onT_ready"], 1)

            def relu(k, n):
                for f in range(HT):
                    act.wait_ge(S["hidden"], events(HT * k + f + 1))
                    if f == 0 and (not isinstance(k, int) or k >= 2):
                        act.wait_ge(S["reduced"], events(k - 1))
                    nc.scalar.activation(hT[n][:, f, :], wide[HT * n + f][:, :], ACT.Relu,
                                         bias=res.colsT[:, C_BR1 + f:C_BR1 + f + 1]).then_inc(S["hT_ready"], 1)

            def take_x3(k, n):
                act.wait_ge(S["normed_turned"], events(N + k + 1)).then_inc(stood, 1)
                nc.scalar.activation(x3nT[:, ds(k, 1), :].rearrange("p k s -> p (k s)"), turn[n][:, :],
                                     ACT.Copy).then_inc(S["x3nT_ready"], 1)

            def relu_layer(k, n, first, last):
                if not last:
                    relu(k + 1, 1 - n)
                if not first:
                    take_x3(k - 1, 1 - n)

            def gelu(k, n, first, last):
                for f in range(FT):
                    act.wait_ge(S["wide_done"], events(FT * k + f + 1))
                    if f == 0 and (not isinstance(k, int) or k >= 2):
                        act.wait_ge(S["down_done"], events(k - 1))
                    nc.scalar.activation(gT[n][:, f, :], wide[f][:, :], ACT.Gelu,
                                         bias=res.colsT[:, C_FB1 + f:C_FB1 + f + 1]).then_inc(S["gelu_done"], 1)

            take_att(0, 0)
            act.wait_ge(weights_turned, 1)
            nc.scalar.activation(wr1T[:, :], wide[0][:, 0:HIDDEN], ACT.Copy).then_inc(weights_copied, 1)
            nc.scalar.activation(flat(wr2T), wide[1][:, 0:HIDDEN], ACT.Copy).then_inc(weights_copied, 1)
            act.wait_ge(weights_turned, 2)
            nc.scalar.activation(w1T[:, :], wide[2][:, :], ACT.Copy).then_inc(weights_copied, 1)
            nc.scalar.activation(flat(w2T), wide[3][:, :], ACT.Copy).then_inc(weights_copied, 1)
            blocks(act, norm2)
            blocks(act, relu_layer, before=lambda: relu(0, 0), after=lambda: take_x3(N - 1, 1))
            blocks(act, gelu)

        @block.vector
        def _(dve):
            start(dve, "dve")
            dve.memset(ones[:, :], 1.0).then_inc(ones_set, 1)

            def moments_of(src, k, n, at):
                for c in range(T):
                    last = nc.vector.bn_stats(stats[n][:, c, :], src[:, ds(k * T + c, 1), :]
                                              .rearrange("p t d -> p (t d)"))
                last.then_inc(S["stats_ready"], 1)
                dve.wait_ge(S["stats_ready"], events(N * at + k + 1)).then_inc(stood, 1)
                for c in range(T):
                    last = nc.vector.bn_aggr(moments[n][:, c, :], stats[n][:, c, :])
                last.then_inc(S["moments_ready"], 1)
                dve.wait_ge(S["moments_ready"], events(N * at + k + 1))
                nc.vector.tensor_scalar(moments[n][:, :, 1], moments[n][:, :, 1], EPS, None,
                                        ALU.add).then_inc(S["var_ready"], 1)

            def normalize(src, k, n, at):
                dve.wait_ge(S["rstd_ready"], events(N * at + k + 1))
                if at or not isinstance(k, int) or k >= 2:
                    dve.wait_ge(S["normed_turned"], events(N * at + k - 1))
                for c in range(T):
                    last = nc.vector.tensor_scalar(normed[n][:, c:c + 1, :], src[:, ds(k * T + c, 1), :],
                                                   moments[n][:, c, 0:1], rstd[n][:, c:c + 1],
                                                   ALU.subtract, ALU.mult)
                last.then_inc(S["normed_ready"], 1)

            def attended(k, n):
                dve.wait_ge(S["projected"], events(k + 1))
                nc.vector.tensor_tensor(tiles(res.y, k), prod[n][:, :].rearrange("p (t d) -> p t d", t=T),
                                        tiles(res.y, k), ALU.add).then_inc(S["x2_ready"], 1)
                dve.wait_ge(S["x2_ready"], events(k + 1)).then_inc(stood, 1)
                moments_of(res.y, k, n, 0)

            def norm2(k, n, first, last):
                if not last:
                    attended(k + 1, 1 - n)
                normalize(res.y, k, n, 0)

            def fed(k, n):
                dve.wait_ge(S["reduced"], events(k + 1))
                nc.vector.tensor_tensor(tiles(res.y, k), prod[n][:, :].rearrange("p (t d) -> p t d", t=T),
                                        tiles(res.y, k), ALU.add).then_inc(S["x3_part"], 1)
                dve.wait_ge(S["x3_part"], events(k + 1))
                nc.vector.tensor_tensor(tiles(res.x, k), tiles(res.x, k), tiles(res.y, k),
                                        ALU.add).then_inc(S["x3_ready"], 1)
                dve.wait_ge(S["x3_ready"], events(k + 1)).then_inc(stood, 1)
                moments_of(res.x, k, n, 1)

            def relu_layer(k, n, first, last):
                if not first:
                    fed(k, n)
                    normalize(res.x, k - 1, 1 - n, 1)
                else:
                    fed(k, n)

            def gelu_layer(k, n, first, last):
                dve.wait_ge(S["down_done"], events(k + 1))
                if not isinstance(k, int) or k >= 2:
                    dve.wait_ge(y_stored[n], DMA * (k // 2))
                nc.vector.tensor_tensor(y_out[n][:, :, :], prod[n][:, :].rearrange("p (t d) -> p t d", t=T),
                                        tiles(res.x, k), ALU.add).then_inc(S["y_ready"], 1)

            attended(0, 0)
            blocks(dve, norm2)
            dve.wait_ge(weights_copied, 4)
            for n, w in enumerate((w1T[:, :], flat(w2T))):
                nc.vector.tensor_reduce(absum[:, n:n + 1], w, AX.X, ALU.add,
                                        apply_absolute_value=True).then_inc(absum_ready, 1)
            dve.wait_ge(absum_total, 1)
            nc.vector.tensor_scalar(scale[:, :, 0], wide[3][:, 0:2], 1.0 / (FF * DIM), 1e-8,
                                    ALU.mult, ALU.max).then_inc(scale_ready, 1)
            dve.wait_ge(scale_ready, 1)
            nc.vector.tensor_scalar(scale[:, :, 1], scale[:, :, 0], -0.5, None, ALU.mult).then_inc(scale_ready, 1)
            dve.wait_ge(scale_ready, 2)
            nc.vector.tensor_scalar(scale[:, :, 0], scale[:, :, 0], 0.5, None, ALU.mult).then_inc(scale_ready, 1)
            blocks(dve, relu_layer, after=lambda: normalize(res.x, N - 1, 1, 1))
            dve.wait_ge(S["fb2_added"], events(N))
            blocks(dve, gelu_layer)


def build(nc, args, out):
    ctx = ExitStack()
    with ctx:
        res = Resident(nc, ctx)
        prepare(nc, res, args)
        attention(nc, res)
        feed_forward(nc, res, args, out)


_NAMES = {
    "L0_attn_x": "x", "L0_attn_Wq": "Wq", "L0_attn_bq": "bq", "L0_attn_Wk": "Wk", "L0_attn_bk": "bk",
    "L0_attn_Wv": "Wv", "L0_attn_bv": "bv", "L0_attn_Wqv": "Wqv", "L0_attn_bqv": "bqv", "L0_attn_Ws": "Ws",
    "L0_attn_bs": "bs", "L0_attn_Wf": "Wf", "L0_attn_bf": "bf", "L0_attn_Wr1": "Wr1", "L0_attn_br1": "br1",
    "L0_attn_Wr2": "Wr2", "L0_attn_br2": "br2", "L0_attn_g1": "g1", "L0_attn_b1": "b1", "L0_attn_g2": "g2",
    "L0_attn_b2": "b2", "L0_ffn_W1": "W1", "L0_ffn_b1": "fb1", "L0_ffn_W2": "W2", "L0_ffn_b2": "fb2",
}


def kernel(**inputs):
    import numpy as _np
    import concourse.bacc as _bacc
    from concourse import mybir as _mybir
    from concourse.bass_utils import run_bass_kernel_spmd as _run

    nc = _bacc.Bacc("TRN2", target_bir_lowering=False, num_devices=1)
    arrays, args = {}, {}
    for name, short in _NAMES.items():
        arr = _np.ascontiguousarray(inputs[name])
        arrays[f"in_{name}"] = arr
        args[short] = nc.dram_tensor(f"in_{name}", arr.shape, _mybir.dt.from_np(arr.dtype), kind="ExternalInput").ap()
    out = nc.dram_tensor("out", (BATCH, SEQ, DIM), _mybir.dt.float32, kind="ExternalOutput").ap()
    build(nc, args, out)
    r = _run(nc, [arrays], core_ids=[0])
    return r.results[0]["out"]
```

```python
import numpy as np
import concourse.bass as bass
from concourse import mybir
from contextlib import ExitStack

FP32 = mybir.dt.float32
BF16 = mybir.dt.bfloat16
ALU = mybir.AluOpType
ACT = mybir.ActivationFunctionType
AX = mybir.AxisListType
ds = bass.ds

BATCH, SEQ, DIM = 4, 1024, 128
HEADS, HD, R, QK = 16, 8, 8, 32
HIDDEN, FF = 2 * DIM, 4 * DIM
P = 128
TB = SEQ // P
TILES = BATCH * TB
U = BATCH * HEADS
SLOTS = 4
GROUPS = U // SLOTS
GPB = HEADS // SLOTS
VW = R * HD
HALF = SEQ // 2
PARTS = 3
PROD_ROWS = PARTS * PARTS * HD
MAX_PARTS = 2
ROWS = PROD_ROWS + MAX_PARTS
PAIR = 2
PAIR_COLS = PAIR * P
PAIRS_BEFORE = TB // PAIR + 1
PAIRS_ALONG = TILES // PAIR - PAIRS_BEFORE
BLOCK_TILES = HALF // P
BLOCKS = TILES // BLOCK_TILES
EPS = 1e-5
LOADS = 2 + PARTS
STORES = 1 + PARTS
DMA = 16

C_BQ, C_BK, C_G1, C_B1, C_G2, C_B2, C_BR1, C_FB1, C_BQV, N_COLS = 0, 1, 2, 3, 4, 5, 6, 8, 12, 16
R_BV, R_WS, R_BS, R_BF, R_BR2, R_FB2, N_ROWS = 0, 64, 104, 128, 256, 384, 512


def spread(ap, n):
    return ap.unsqueeze(2).to_broadcast([ap.shape[0], ap.shape[1], n])


def again(ap, n):
    return ap.unsqueeze(1).to_broadcast([ap.shape[0], n, ap.shape[1]])


class Resident:

    def __init__(self, nc, ctx):
        def sb(name, shape, dtype=FP32):
            return ctx.enter_context(nc.sbuf_tensor(name, shape, dtype))
        self.x = sb("x_all", [P, TILES, DIM])
        self.y = sb("y_all", [P, TILES, DIM])
        self.v = sb("v_all", [P, TILES, VW])
        self.qs = sb("qs_all", [P, TILES, HEADS])
        self.att = sb("att_all", [P, TILES, DIM])
        self.identf = sb("identf", [P, P])
        self.identb = sb("identb", [P, P], BF16)
        self.colsT = sb("colsT", [P, N_COLS])
        self.bq_scaled = sb("bq_scaled", [P, 1])
        self.minus_half = sb("minus_half", [P, PAIR * PAIRS_BEFORE])
        self.qs_bias = sb("qs_bias", [P, HEADS])
        self.rows = sb("rows", [P, N_ROWS])
        self.qkvT = sb("qkvT", [P, 3 * DIM + VW])
        self.proj = sb("proj", [P, P])
        self.q_op = [sb(f"q_op{s}", [ROWS, SEQ], BF16) for s in range(SLOTS)]
        self.k_op = [sb(f"k_op{s}", [P, SEQ], BF16) for s in range(SLOTS)]
        self.v_op = [sb(f"v_op{s}", [P, TB, VW]) for s in range(SLOTS)]
        self.operands_in = [ctx.enter_context(nc.semaphore(f"operands_in{s}")) for s in range(SLOTS)]
        self.q_parts = nc.dram_tensor("q_parts", [PARTS, U, HD, SEQ], BF16, kind="Internal").ap()
        self.k_parts = nc.dram_tensor("k_parts", [U, PARTS, HD, SEQ], BF16, kind="Internal").ap()

    def load(self, sp, u, b, slot):
        sp.dma_start(self.k_op[slot][0:PROD_ROWS, :], self.k_parts[ds(u, 1)].rearrange("u c d s -> u (c d) s")
                     .to_broadcast([PARTS, PARTS * HD, SEQ])).then_inc(self.operands_in[slot], DMA)
        for m in range(PARTS):
            sp.dma_start(self.q_op[slot][m * PARTS * HD:(m + 1) * PARTS * HD, :],
                         self.q_parts[m, ds(u, 1)].to_broadcast([PARTS, HD, SEQ])).then_inc(self.operands_in[slot], DMA)
        sp.dma_start(self.v_op[slot][:, :, :], self.v[:, ds(b * TB, TB), :]).then_inc(self.operands_in[slot], DMA)


class Projections:

    def __init__(self, nc, ctx, res, name, ring, turned, qk, v):
        def sb(what, shape, dtype=FP32):
            return [ctx.enter_context(nc.sbuf_tensor(f"{name}_{what}{r}", shape, dtype)) for r in range(ring)]
        self.banks = len(turned)

        def sem(what):
            return ctx.enter_context(nc.semaphore(f"{name}_{what}"))
        self.nc, self.res, self.ring = nc, res, ring
        self.turned_bank, self.qk_bank, self.v_bank = turned, qk, v
        self.stats_buf = sb("stats", [P, 2, PAIR, 6])
        self.moment = sb("moment", [P, 2, PAIR, 2])
        self.rstd = sb("rstd", [P, 2, PAIR])
        self.z = sb("z", [P, PAIR, DIM])
        self.xnT = sb("xnT", [P, PAIR_COLS])
        self.full = sb("full", [P, 2, PAIR_COLS])
        self.parts = sb("parts", [P, PARTS, 2, PAIR_COLS], BF16)
        self.stats_done, self.var_ready, self.rstd_ready = sem("stats_done"), sem("var_ready"), sem("rstd_ready")
        self.moment_ready = sem("moment_ready")
        self.y_ready, self.z_ready, self.z_turned, self.xnT_ready = (sem("y_ready"), sem("z_ready"),
                                                                     sem("z_turned"), sem("xnT_ready"))
        self.qk_done, self.full_ready, self.v_done, self.v_ready = (sem("qk_done"), sem("full_ready"),
                                                                    sem("v_done"), sem("v_ready"))
        self.part_ready = [sem(f"part{c}_ready") for c in range(PARTS)]
        self.rest_ready, self.biased = sem("rest_ready"), sem("biased")
        self.stored = sem("stored")
        self.stood = sem("stood")

    def at(self, n):
        return n % self.ring if isinstance(n, int) else 0

    def bank_at(self, n):
        return n % self.banks if isinstance(n, int) else 0

    def wait_left(self, engine, done, n, each=1, of=None):
        of = of or self.ring
        if not isinstance(n, int) or n >= of:
            engine.wait_ge(done, each * (n - of + 1))

    def stats(self, dve, n, tile, which):
        src = (self.res.x, self.res.y)[which]
        if which == 1:
            dve.wait_ge(self.y_ready, n + 1).then_inc(self.stood, 1)
        for c in range(PAIR):
            last = self.nc.vector.bn_stats(self.stats_buf[self.at(n)][:, which, c, :],
                                           src[:, ds(tile + c, 1), :].rearrange("p t d -> p (t d)"))
        last.then_inc(self.stats_done, 1)

    def moments(self, dve, n, which):
        dve.wait_ge(self.stats_done, 2 * n + which + 1).then_inc(self.stood, 1)
        m = self.moment[self.at(n)]
        for c in range(PAIR):
            last = self.nc.vector.bn_aggr(m[:, which, c, :], self.stats_buf[self.at(n)][:, which, c, :])
        last.then_inc(self.moment_ready, 1)
        dve.wait_ge(self.moment_ready, 2 * n + which + 1)
        self.nc.vector.tensor_scalar(m[:, which, :, 1], m[:, which, :, 1], EPS, None,
                                     ALU.add).then_inc(self.var_ready, 1)

    def normalize(self, dve, n, tile, which):
        res, a = self.res, self.at(n)
        dve.wait_ge(self.rstd_ready, 2 * n + which + 1)
        if which == 1:
            self.wait_left(dve, self.z_turned, n)
        for c in range(PAIR):
            src = (res.x, res.y)[which][:, ds(tile + c, 1), :]
            dst = res.y[:, ds(tile + c, 1), :] if which == 0 else self.z[a][:, c:c + 1, :]
            last = self.nc.vector.tensor_scalar(dst, src, self.moment[a][:, which, c, 0:1],
                                                self.rstd[a][:, which, c:c + 1], ALU.subtract, ALU.mult)
        last.then_inc((self.y_ready, self.z_ready)[which], 1)

    def take_values(self, dve, n, tile):
        dve.wait_ge(self.v_done, n + 1)
        tiles = self.v_bank[self.bank_at(n)][:, 0:PAIR_COLS].rearrange("p (c w) -> p c w", w=P)
        self.nc.vector.tensor_tensor(self.res.v[:, ds(tile, PAIR), :], tiles[:, :, 0:VW],
                                     again(self.res.rows[:, R_BV:R_BV + VW], PAIR), ALU.add)
        self.nc.vector.tensor_tensor(self.res.qs[:, ds(tile, PAIR), :], tiles[:, :, VW:VW + HEADS],
                                     again(self.res.qs_bias[:, :], PAIR), ALU.add).then_inc(self.v_ready, 1)

    def rest(self, engine, n, c):
        a = self.at(n)
        engine.wait_ge(self.part_ready[c], n + 1)
        done = self.rest_ready if c == 0 else self.part_ready[2]
        dst = self.full[a][:, :, :] if c == 0 else self.parts[a][:, 0, :, :]
        engine.tensor_tensor(dst, self.full[a][:, :, :], self.parts[a][:, 2 - c, :, :], ALU.subtract).then_inc(done, 1)

    def rstd_of(self, pool, n, which):
        pool.wait_ge(self.var_ready, 2 * n + which + 1)
        pool.tensor_tensor(self.rstd[self.at(n)][:, which, :], self.moment[self.at(n)][:, which, :, 1],
                           self.res.minus_half[:, 0:PAIR], ALU.pow).then_inc(self.rstd_ready, 1)

    def add_biases(self, pool, n, tile):
        res = self.res
        pool.wait_ge(self.z_ready, n + 1).then_inc(self.stood, 1)
        for all_, row in ((res.y, R_BF), (res.x, R_BR2)):
            t = all_[:, ds(tile, PAIR), :]
            pool.tensor_tensor(t, t, again(res.rows[:, row:row + DIM], PAIR), ALU.add).then_inc(self.biased, 1)

    def turn(self, pe, n):
        pe.wait_ge(self.z_ready, n + 1)
        self.wait_left(pe, self.xnT_ready, n, of=self.banks)
        for c in range(PAIR):
            last = self.nc.tensor.transpose(self.turned_bank[self.bank_at(n)][:, c * P:(c + 1) * P],
                                            self.z[self.at(n)][:, c, :], self.res.identf[:, :])
        last.then_inc(self.z_turned, 1)

    def qk(self, pe, n):
        pe.wait_ge(self.xnT_ready, n + 1)
        self.wait_left(pe, self.full_ready, n, 2, of=self.banks)
        for m in range(2):
            last = self.nc.tensor.matmul(self.qk_bank[self.bank_at(n)][:, m * PAIR_COLS:(m + 1) * PAIR_COLS],
                                         self.res.qkvT[:, m * DIM:(m + 1) * DIM], self.xnT[self.at(n)][:, :],
                                         start=True, stop=True)
        last.then_inc(self.qk_done, 1)

    def values(self, pe, n):
        if self.v_bank is self.qk_bank or self.v_bank[0] is self.qk_bank[0]:
            pe.wait_ge(self.full_ready, 2 * n + 2)
        self.wait_left(pe, self.v_ready, n, of=self.banks)
        for c in range(PAIR):
            last = self.nc.tensor.matmul(self.v_bank[self.bank_at(n)][:, c * P:(c + 1) * P],
                                         self.xnT[self.at(n)][:, c * P:(c + 1) * P], self.res.proj[:, :],
                                         start=True, stop=True)
        last.then_inc(self.v_done, 1)

    def take_turned(self, act, n):
        act.wait_ge(self.z_turned, n + 1)
        self.wait_left(act, self.v_done, n)
        self.nc.scalar.activation(self.xnT[self.at(n)][:, :], self.turned_bank[self.bank_at(n)][:, 0:PAIR_COLS],
                                  ACT.Identity, bias=self.res.colsT[:, C_B1:C_B1 + 1],
                                  scale=self.res.colsT[:, C_G1:C_G1 + 1]).then_inc(self.xnT_ready, 1)

    def take_qk(self, act, n, m):
        act.wait_ge(self.qk_done, n + 1)
        self.wait_left(act, self.part_ready[2], n)
        self.nc.scalar.activation(self.full[self.at(n)][:, m, :],
                                  self.qk_bank[self.bank_at(n)][:, m * PAIR_COLS:(m + 1) * PAIR_COLS], ACT.Identity,
                                  bias=self.res.bq_scaled[:, :] if m == 0 else self.res.colsT[:, C_BK:C_BK + 1],
                                  scale=HD ** -0.5 if m == 0 else 1.0).then_inc(self.full_ready, 1)

    def part(self, act, n, c):
        if c == 0:
            act.wait_ge(self.full_ready, 2 * n + 2)
            self.wait_left(act, self.stored, n, STORES * DMA)
        else:
            act.wait_ge(self.rest_ready, n + 1)
        self.nc.scalar.activation(self.parts[self.at(n)][:, 2 - c, :, :], self.full[self.at(n)][:, :, :],
                                  ACT.Copy).then_inc(self.part_ready[c], 1)

    def store(self, queue, n, pair, q, k, stored):
        queue.wait_ge(self.part_ready[2], n + 1)
        heads, cols = ds(pair // (TB // PAIR) * HEADS, HEADS), ds(pair % (TB // PAIR) * PAIR_COLS, PAIR_COLS)
        parts = self.parts[self.at(n)]
        if q:
            queue.dma_start(self.res.q_parts[:, heads, :, cols].rearrange("c h d s -> (h d) c s"),
                            parts[:, :, 0, :]).then_inc(stored, DMA)
        for c in k:
            queue.dma_start(self.res.k_parts[heads, c, :, cols], parts[:, c, 1, :]).then_inc(stored, DMA)


class Mixing:

    def __init__(self, nc, ctx, res):
        def sb(name, shape, dtype=FP32):
            return ctx.enter_context(nc.sbuf_tensor(name, shape, dtype))

        def sem(name):
            return ctx.enter_context(nc.semaphore(name))
        self.nc, self.res = nc, res
        self.mix_in = sb("mix_in", [P, 2, TB, SLOTS, VW])
        self.product = sb("product", [P, TB * SLOTS, R, HD])
        self.den = sb("den", [P, TB, SLOTS])
        self.rden = sb("rden", [P, TB, SLOTS])
        self.logit = sb("logit", [P, TB * SLOTS, R])
        self.top = sb("top", [P, TB * SLOTS])
        self.total = sb("total", [P, TB * SLOTS])
        self.turn_bank = None
        self.mix_in_ready, self.den_turned = sem("mix_in_ready"), sem("den_turned")
        self.den_ready, self.rden_ready = sem("den_ready"), sem("rden_ready")
        self.logit_product, self.logit_sum, self.logit_scaled, self.logit_ready = (
            sem("logit_product"), sem("logit_sum"), sem("logit_scaled"), sem("logit_ready"))
        self.top_ready, self.logit_shifted, self.mix_exp = sem("top_ready"), sem("logit_shifted"), sem("mix_exp")
        self.total_ready, self.rtotal_ready, self.norm_ready, self.weight_ready = (
            sem("total_ready"), sem("rtotal_ready"), sem("norm_ready"), sem("weight_ready"))
        self.mixed, self.att_done = sem("mixed"), sem("att_done")
        self.stood = sem("stood_pool")

    def step(self, dve, G, b, g, what, first=0, end=TB):
        part = slice(first * SLOTS, end * SLOTS)
        flat = lambda x: x[:, :, :].rearrange("p e s -> p (e s)")
        if what == "denominators":
            dve.wait_ge(self.den_turned, G + 1)
            sums = self.turn_bank[:, :].rearrange("p (e k s) -> p e s k", k=2, s=32)[:, :, 0:SLOTS, :]
            self.nc.vector.tensor_reduce(self.den[:, :, :], sums, AX.X, ALU.add).then_inc(self.den_ready, 1)
            dve.wait_ge(self.den_ready, G + 1)
            self.nc.vector.reciprocal(flat(self.rden), flat(self.den)).then_inc(self.rden_ready, 1)
        elif what == "logit sums":
            dve.wait_ge(self.logit_product, G + 1)
            self.nc.vector.tensor_reduce(self.logit[:, part, :], self.product[:, part, :, :], AX.X,
                                         ALU.add).then_inc(self.logit_sum, end - first)
        elif what == "logits over denominators":
            dve.wait_ge(self.logit_sum, TB * G + TB)
            dve.wait_ge(self.rden_ready, G + 1)
            self.nc.vector.tensor_tensor(self.logit[:, :, :], self.logit[:, :, :], spread(flat(self.rden), R),
                                    ALU.mult).then_inc(self.logit_scaled, 1)
        elif what == "query part":
            dve.wait_ge(self.logit_scaled, G + 1)
            self.nc.vector.tensor_tensor(
                self.logit[:, :, :].rearrange("p (e s) r -> p e s r", s=SLOTS),
                self.logit[:, :, :].rearrange("p (e s) r -> p e s r", s=SLOTS),
                self.res.qs[:, ds(b * TB, TB), ds(g * SLOTS, SLOTS)].unsqueeze(3)
                .to_broadcast([P, TB, SLOTS, R]), ALU.add).then_inc(self.logit_ready, 1)
        elif what == "maxima":
            dve.wait_ge(self.logit_ready, G + 1)
            self.nc.vector.tensor_reduce(self.top[:, :], self.logit[:, :, :], AX.X, ALU.max).then_inc(self.top_ready, 1)
        elif what == "shift":
            dve.wait_ge(self.top_ready, G + 1)
            self.nc.vector.tensor_tensor(self.logit[:, :, :], self.logit[:, :, :], spread(self.top[:, :], R),
                                    ALU.subtract).then_inc(self.logit_shifted, 1)
        elif what == "totals":
            dve.wait_ge(self.mix_exp, G + 1)
            self.nc.vector.tensor_reduce(self.total[:, :], self.logit[:, :, :], AX.X,
                                         ALU.add).then_inc(self.total_ready, 1)
        elif what == "normalizers":
            dve.wait_ge(self.total_ready, G + 1)
            self.nc.vector.reciprocal(self.total[:, :], self.total[:, :]).then_inc(self.rtotal_ready, 1)
            dve.wait_ge(self.rtotal_ready, G + 1)
            self.nc.vector.tensor_tensor(self.total[:, :], self.total[:, :], flat(self.rden),
                                         ALU.mult).then_inc(self.norm_ready, 1)
        elif what == "weights":
            dve.wait_ge(self.norm_ready, G + 1)
            self.nc.vector.tensor_tensor(self.logit[:, :, :], self.logit[:, :, :], spread(self.total[:, :], R),
                                    ALU.mult).then_inc(self.weight_ready, 1)
        elif what == "output":
            dve.wait_ge(self.mixed, G + 1)
            last = self.nc.vector.tensor_reduce(
                self.res.att[:, ds(b * TB + first, end - first), ds(g * SLOTS * HD, SLOTS * HD)]
                .rearrange("p e (s d) -> p e s d", d=HD),
                self.product[:, part, :, :].rearrange("p (e s) r d -> p e s d r", s=SLOTS), AX.X, ALU.add)
            if end == TB:
                last.then_inc(self.att_done, 1)

    def values_of(self, G):
        return self.mix_in[:, ds(G % 2, 1), :, :, :].rearrange("p g e s (r d) -> p (g e s r) d", d=HD)

    def logit_products(self, pool, G):
        pool.wait_ge(self.mix_in_ready, SLOTS * G + SLOTS)
        pool.wait_ge(self.att_done, G + 1).then_inc(self.stood, 1)
        pool.tensor_tensor(
            self.product[:, :, :, :].rearrange("p m r d -> p (m r) d"), self.values_of(G),
            again(self.res.rows[:, R_WS + QK:R_WS + QK + HD], TB * SLOTS * R),
            ALU.mult).then_inc(self.logit_product, 1)

    def mix(self, pool, G):
        pool.wait_ge(self.weight_ready, G + 1).then_inc(self.stood, 1)
        pool.tensor_tensor(
            self.product[:, :, :, :].rearrange("p m r d -> p (m r) d"), self.values_of(G),
            spread(self.logit[:, :, :].rearrange("p m r -> p (m r)"), HD),
            ALU.mult).then_inc(self.mixed, 1)

    def exps(self, act, G):
        act.wait_ge(self.logit_shifted, G + 1)
        self.nc.scalar.activation(self.logit[:, :, :], self.logit[:, :, :], ACT.Exp).then_inc(self.mix_exp, 1)


class FeedForwardWeights:

    def __init__(self, nc, ctx, res):
        def sb(name, shape, dtype=FP32):
            return ctx.enter_context(nc.sbuf_tensor(name, shape, dtype))

        def sem(name):
            return ctx.enter_context(nc.semaphore(name))
        self.nc, self.res = nc, res
        self.wr1_n, self.wr2_n = sb("wr1_n", [P, HIDDEN // P, DIM]), sb("wr2_n", [P, HIDDEN])
        self.w1_n, self.w2_n = sb("w1_n", [P, FF // P, DIM]), sb("w2_n", [P, FF])
        self.wr1T, self.wr2T = sb("wr1T", [P, HIDDEN]), sb("wr2T", [P, HIDDEN])
        self.w1T, self.w2T = sb("w1T", [P, FF]), sb("w2T", [P, FF])
        self.ones = sb("ff_ones", [P, P])
        self.absum = sb("absum", [P, 2])
        self.scale = sb("scale", [P, 2, 2])
        self.above, self.below = sb("above", [P, FF]), sb("below", [P, FF])
        self.loaded, self.turned, self.copied = sem("ff_loaded"), sem("ff_turned"), sem("ff_copied")
        self.absum_ready, self.absum_total = sem("absum_ready"), sem("absum_total")
        self.scale_ready, self.tern_step = sem("scale_ready"), sem("tern_step")

    def load(self, sp, a):
        for dst, src in ((self.w1_n[:, :, :], a["W1"].rearrange("(k p) d -> p k d", p=P)),
                         (self.w2_n[:, :], a["W2"]),
                         (self.wr1_n[:, :, :], a["Wr1"].rearrange("(k p) d -> p k d", p=P)),
                         (self.wr2_n[:, :], a["Wr2"])):
            sp.dma_start(dst, src).then_inc(self.loaded, DMA)

    def turn_ternary(self, pe, bank):
        pe.wait_ge(self.loaded, DMA * 4)
        for k in range(FF // P):
            self.nc.tensor.transpose(bank[0][:, k * P:(k + 1) * P], self.w1_n[:, k, :], self.res.identf[:, :])
        for k in range(FF // P):
            last = self.nc.tensor.transpose(bank[1][:, k * P:(k + 1) * P], self.w2_n[:, k * P:(k + 1) * P],
                                            self.res.identf[:, :])
        last.then_inc(self.turned, 1)

    def take_ternary(self, act, bank):
        act.wait_ge(self.turned, 1)
        for n, w in enumerate((self.w1T, self.w2T)):
            self.nc.scalar.activation(w[:, :], bank[n][:, :], ACT.Copy).then_inc(self.copied, 1)

    def turn_relu(self, pe, bank):
        pe.wait_ge(self.copied, 2)
        for k in range(HIDDEN // P):
            self.nc.tensor.transpose(bank[0][:, k * P:(k + 1) * P], self.wr1_n[:, k, :], self.res.identf[:, :])
        for k in range(HIDDEN // P):
            last = self.nc.tensor.transpose(bank[0][:, HIDDEN + k * P:HIDDEN + (k + 1) * P],
                                            self.wr2_n[:, k * P:(k + 1) * P], self.res.identf[:, :])
        last.then_inc(self.turned, 1)

    def take_relu(self, act, bank):
        act.wait_ge(self.turned, 2)
        for n, w in enumerate((self.wr1T, self.wr2T)):
            self.nc.scalar.activation(w[:, :], bank[0][:, n * HIDDEN:(n + 1) * HIDDEN],
                                      ACT.Copy).then_inc(self.copied, 1)

    def sum_rows(self, dve):
        dve.wait_ge(self.copied, 2)
        for n, w in enumerate((self.w1T, self.w2T)):
            self.nc.vector.tensor_reduce(self.absum[:, n:n + 1], w[:, :], AX.X, ALU.add,
                                         apply_absolute_value=True).then_inc(self.absum_ready, 1)

    def sum_all(self, pe, bank):
        pe.wait_ge(self.absum_ready, 2)
        self.nc.tensor.matmul(bank[1][:, 0:2], self.ones[:, :], self.absum[:, :], start=True,
                              stop=True).then_inc(self.absum_total, 1)

    def scales(self, dve, bank):
        dve.wait_ge(self.absum_total, 1)
        v, scale = self.nc.vector, self.scale
        v.tensor_scalar(scale[:, :, 0], bank[1][:, 0:2], 1.0 / (FF * DIM), 1e-8, ALU.mult,
                        ALU.max).then_inc(self.scale_ready, 1)
        dve.wait_ge(self.scale_ready, 1)
        v.tensor_scalar(scale[:, :, 1], scale[:, :, 0], -0.5, None, ALU.mult).then_inc(self.scale_ready, 1)
        dve.wait_ge(self.scale_ready, 2)
        v.tensor_scalar(scale[:, :, 0], scale[:, :, 0], 0.5, None, ALU.mult).then_inc(self.scale_ready, 1)

    def ternary(self, dve, n):
        w, above, below = (self.w1T, self.w2T)[n][:, :], self.above[:, :], self.below[:, :]
        v, done = self.nc.vector, self.tern_step
        dve.wait_ge(self.scale_ready, 3)
        if n > 0:
            dve.wait_ge(done, 5 * n)
        v.tensor_scalar(above, w, self.scale[:, n, 0:1], None, ALU.is_gt).then_inc(done, 1)
        v.tensor_scalar(below, w, self.scale[:, n, 1:2], None, ALU.is_lt).then_inc(done, 1)
        dve.wait_ge(done, 5 * n + 2)
        v.tensor_tensor(above, above, below, ALU.subtract).then_inc(done, 1)
        dve.wait_ge(done, 5 * n + 3)
        v.tensor_tensor(above, above, w, ALU.subtract).then_inc(done, 1)
        dve.wait_ge(done, 5 * n + 4)
        v.tensor_tensor(w, w, above, ALU.add).then_inc(done, 1)


def block_tiles(r, j):
    return r[:, ds(j * BLOCK_TILES, BLOCK_TILES), :]


def block_tile(r, j, c):
    return r[:, ds(j * BLOCK_TILES + c, 1), :].rearrange("p t d -> p (t d)")


def split(bank):
    return bank[:, :].rearrange("p (t d) -> p t d", t=BLOCK_TILES)


def turn_tiles(nc, bank, src, identity, done):
    for c in range(BLOCK_TILES):
        last = nc.tensor.transpose(bank[:, c * P:(c + 1) * P], src[:, c, :], identity[:, :])
    last.then_inc(done, 1)


class BlockNorm:

    def __init__(self, nc, ctx, res, name, src):
        def sb(what, shape):
            return ctx.enter_context(nc.sbuf_tensor(f"{name}_{what}", shape, FP32))

        def sem(what):
            return ctx.enter_context(nc.semaphore(f"{name}_{what}"))
        self.nc, self.res, self.src = nc, res, src
        self.stats, self.moment, self.rstd = (sb("stats", [P, BLOCK_TILES, 6]), sb("moment", [P, BLOCK_TILES, 2]),
                                              sb("rstd", [P, BLOCK_TILES]))
        self.normed = sb("normed", [P, BLOCK_TILES, DIM])
        self.stats_ready, self.moments_ready = sem("stats_ready"), sem("moments_ready")
        self.var_ready = sem("var_ready")
        self.rstd_ready, self.ready, self.turned = sem("rstd_ready"), sem("ready"), sem("turned")
        self.stood = sem("stood")

    def moments(self, dve, j):
        v = self.nc.vector
        for c in range(BLOCK_TILES):
            last = v.bn_stats(self.stats[:, c, :], block_tile(self.src, j, c))
        last.then_inc(self.stats_ready, 1)
        dve.wait_ge(self.stats_ready, j + 1).then_inc(self.stood, 1)
        for c in range(BLOCK_TILES):
            last = v.bn_aggr(self.moment[:, c, :], self.stats[:, c, :])
        last.then_inc(self.moments_ready, 1)
        dve.wait_ge(self.moments_ready, j + 1)
        v.tensor_scalar(self.moment[:, :, 1], self.moment[:, :, 1], EPS, None, ALU.add).then_inc(self.var_ready, 1)

    def root(self, pool, j):
        pool.wait_ge(self.var_ready, j + 1)
        pool.tensor_tensor(self.rstd[:, :], self.moment[:, :, 1], self.res.minus_half[:, 0:BLOCK_TILES],
                           ALU.pow).then_inc(self.rstd_ready, 1)

    def normalize(self, dve, j):
        dve.wait_ge(self.rstd_ready, j + 1)
        if not isinstance(j, int) or j > 0:
            dve.wait_ge(self.turned, j)
        for c in range(BLOCK_TILES):
            last = self.nc.vector.tensor_scalar(self.normed[:, c, :], block_tile(self.src, j, c),
                                                self.moment[:, c, 0:1], self.rstd[:, c:c + 1],
                                                ALU.subtract, ALU.mult)
        last.then_inc(self.ready, 1)

    def turn(self, pe, j, bank):
        pe.wait_ge(self.ready, j + 1)
        turn_tiles(self.nc, bank, self.normed, self.res.identf, self.turned)


class AttentionOutput:

    def __init__(self, nc, ctx, res, mix):
        def sem(name):
            return ctx.enter_context(nc.semaphore(name))
        self.nc, self.res, self.mix = nc, res, mix
        self.att = ctx.enter_context(nc.sbuf_tensor("att", [P, BLOCK_TILES, DIM], FP32))
        self.attT = ctx.enter_context(nc.sbuf_tensor("attT", [P, HALF], FP32))
        self.norm = BlockNorm(nc, ctx, res, "norm2", res.y)
        self.copied, self.turned, self.attT_ready = sem("att_copied"), sem("att_turned"), sem("attT_ready")
        self.projected, self.x2_ready, self.stood = sem("projected"), sem("x2_ready"), sem("ff_stood")

    def copy(self, act, j):
        if not isinstance(j, int) or j > 0:
            act.wait_ge(self.turned, j).then_inc(self.stood, 1)
        if not isinstance(j, int):
            act.wait_ge(self.mix.att_done, GROUPS + (j + SEQ // HALF) // BLOCKS).then_inc(self.stood, 1)
        self.nc.scalar.activation(self.att[:, :, :], block_tiles(self.res.att, j), ACT.Copy).then_inc(self.copied, 1)

    def turn(self, pe, j, bank):
        pe.wait_ge(self.copied, j + 1)
        turn_tiles(self.nc, bank, self.att, self.res.identf, self.turned)

    def take(self, act, j, bank):
        act.wait_ge(self.turned, j + 1)
        self.nc.scalar.activation(self.attT[:, :], bank[:, :], ACT.Copy).then_inc(self.attT_ready, 1)

    def project(self, pe, j, bank):
        pe.wait_ge(self.attT_ready, j + 1)
        for c in range(BLOCK_TILES):
            last = self.nc.tensor.matmul(bank[:, c * P:(c + 1) * P], self.attT[:, c * P:(c + 1) * P],
                                         self.res.qkvT[:, 2 * DIM:3 * DIM], start=True, stop=True)
        last.then_inc(self.projected, 1)

    def add(self, dve, j, bank):
        dve.wait_ge(self.projected, j + 1)
        y = block_tiles(self.res.y, j)
        self.nc.vector.tensor_tensor(y, split(bank), y, ALU.add).then_inc(self.x2_ready, 1)
        dve.wait_ge(self.x2_ready, j + 1).then_inc(self.stood, 1)
        self.norm.moments(dve, j)


def prepare(nc, res, a):
    ctx = ExitStack()
    with ctx:
        def sb(name, shape, dtype=FP32):
            return ctx.enter_context(nc.sbuf_tensor(name, shape, dtype))

        def sem(name):
            return ctx.enter_context(nc.semaphore(name))

        wq_n, wk_n, wf_n = sb("wq_n", [P, DIM]), sb("wk_n", [P, DIM]), sb("wf_n", [P, DIM])
        wv_n = sb("wv_n", [VW, DIM])
        wqv_n = sb("wqv_n", [P, QK * HEADS // P, DIM])
        cols_n = sb("cols_n", [N_COLS, P])
        ws_col = sb("ws_col", [P, 1])
        ones = sb("ones", [P, P])
        sel = sb("sel", [P, SLOTS])
        sel_b = sb("sel_b", [P, HEADS])
        bank = [ctx.enter_context(nc.psum_tensor(f"prep{n}", [P, HALF], FP32)) for n in range(8)]
        project = Projections(nc, ctx, res, "first", PAIRS_BEFORE, turned=bank[0:2], qk=bank[2:4], v=bank[4:6])
        tiles_before = PAIR * PAIRS_BEFORE
        stats, moment, rstd = (sb("ln_stats", [P, tiles_before, 6]), sb("ln_moment", [P, tiles_before, 2]),
                               sb("ln_rstd", [P, tiles_before]))

        x_in = [sem(f"x_in{n}") for n in range(3)]
        weights_in, rows_in, wf_in = sem("weights_in"), sem("rows_in"), sem("wf_in")
        ident_ready, cleared, sel_ready = sem("ident_ready"), sem("cleared"), sem("sel_ready")
        w_turned, cols_turned, w_copied, cols_ready = (sem("w_turned"), sem("cols_turned"), sem("w_copied"),
                                                       sem("cols_ready"))
        ws_summed, selb_ready, qsb_summed, proj_ready = (sem("ws_summed"), sem("selb_ready"), sem("qsb_summed"),
                                                         sem("proj_ready"))
        qsb_ready, wf_turned, wf_copied = sem("qsb_ready"), sem("wf_turned"), sem("wf_copied")
        k_stored, last_stored, last_k_stored = sem("k_stored"), sem("last_stored"), sem("last_k_stored")
        ones_set, stats_done, moments_done, var_ready, rstd_ready, y_ready = (
            sem("ones_set"), sem("ln_stats_done"), sem("ln_moments_done"), sem("ln_var_ready"),
            sem("ln_rstd_ready"), sem("ln_y_ready"))

        cuts = [0, TB // 2, tiles_before, TILES]
        weights = [(wq_n[:, :], a["Wq"]), (wk_n[:, :], a["Wk"]), (wv_n[:, :], a["Wv"]),
                   (wqv_n[:, :, :], a["Wqv"].rearrange("(k p) d -> p k d", p=P))]
        for at, name, n in ((C_BQ, "bq", 1), (C_BK, "bk", 1), (C_G1, "g1", 1), (C_B1, "b1", 1),
                            (C_G2, "g2", 1), (C_B2, "b2", 1), (C_BR1, "br1", HIDDEN // P),
                            (C_FB1, "fb1", FF // P), (C_BQV, "bqv", QK * HEADS // P)):
            weights.append((cols_n[at:at + n, :], a[name].rearrange("(n p) -> n p", p=P)))
        for n in range(P // QK):
            weights.append((ws_col[n * QK:(n + 1) * QK, :], a["Ws"][0, 0:QK].rearrange("(p n) -> p n", n=1)))
        rows = [(res.rows[:, R_WS:R_WS + QK + HD], a["Ws"][0, :].partition_broadcast(P))]
        for at, name, n in ((R_BV, "bv", VW), (R_BS, "bs", 1), (R_BF, "bf", DIM), (R_BR2, "br2", DIM),
                            (R_FB2, "fb2", DIM)):
            rows.append((res.rows[:, at:at + n], a[name].partition_broadcast(P)))

        block = ctx.enter_context(nc.Block())

        @block.sync
        def _(sp):
            x_tiles = a["x"].rearrange("b (t p) d -> p (b t) d", p=P)

            def load_x(n):
                piece = slice(cuts[n], cuts[n + 1])
                sp.dma_start(res.x[:, piece, :], x_tiles[:, piece, :]).then_inc(x_in[n], DMA)

            load_x(0)
            load_x(1)
            for dst, src in weights[0::2]:
                sp.dma_start(dst, src).then_inc(weights_in, DMA)
            sp.dma_start(wf_n[:, :], a["Wf"]).then_inc(wf_in, DMA)
            load_x(2)
            for n in range(PAIRS_BEFORE):
                project.store(sp, n, n, True, [0, 1], project.stored if n < PAIRS_BEFORE - 1 else last_stored)
            sp.wait_ge(ones_set, 1)
            sp.wait_ge(project.v_ready, TB // PAIR)
            sp.wait_ge(project.stored, DMA * 3 * (PAIRS_BEFORE - 1))
            sp.wait_ge(k_stored, DMA * (PAIRS_BEFORE - 1))
            res.load(sp, 0, 0, 0)
            sp.wait_ge(x_in[2], DMA)
            sp.wait_ge(last_stored, DMA * 3)
            sp.wait_ge(last_k_stored, DMA)

        @block.gpsimd
        def _(pool):
            pool.memset(res.identf[:, :], 0.0).then_inc(cleared, 1)
            pool.memset(res.identb[:, :], 0.0).then_inc(cleared, 1)
            pool.memset(sel[:, :], 1.0).then_inc(cleared, 1)
            pool.memset(res.minus_half[:, :], -0.5).then_inc(cleared, 1)
            pool.wait_ge(cleared, 4)
            for ident in (res.identf, res.identb):
                pool.affine_select(out=ident[:, :], in_=ident[:, :], compare_op=ALU.not_equal, fill=1.0,
                                   base=0, pattern=[[-1, P]], channel_multiplier=1).then_inc(ident_ready, 1)
            pool.affine_select(out=sel[:, :], in_=sel[:, :], compare_op=ALU.is_ge, fill=0.0,
                               base=0, pattern=[[-QK, SLOTS]], channel_multiplier=1).then_inc(ident_ready, 1)
            pool.wait_ge(ident_ready, 3)
            pool.affine_select(out=sel[:, :], in_=sel[:, :], compare_op=ALU.is_ge, fill=0.0,
                               base=QK - 1, pattern=[[QK, SLOTS]], channel_multiplier=-1).then_inc(ident_ready, 1)
            for n in range(4):
                a_, b_ = cuts[n % 2], cuts[n % 2 + 1]
                pool.wait_ge(var_ready, n + 1)
                pool.tensor_tensor(rstd[:, a_:b_], moment[:, a_:b_, 1], res.minus_half[:, 0:b_ - a_],
                                   ALU.pow).then_inc(rstd_ready, 1)
            for dst, src in rows:
                pool.dma_start(dst, src).then_inc(rows_in, DMA)
            pool.wait_ge(rstd_ready, 4)
            for s in range(SLOTS):
                last = pool.memset(res.k_op[s][64:P, :], 1.0)
            last.then_inc(ones_set, 1)
            for n in range(PAIRS_BEFORE):
                project.store(pool, n, n, False, [2], k_stored if n < PAIRS_BEFORE - 1 else last_k_stored)
            pool.wait_ge(rows_in, DMA * len(rows))

        @block.scalar
        def _(act):
            for dst, src in weights[1::2]:
                act.dma_start(dst, src).then_inc(weights_in, DMA)
            act.wait_ge(cols_turned, 1)
            nc.scalar.activation(res.colsT[:, :], bank[7][:, 0:N_COLS], ACT.Copy).then_inc(cols_ready, 1)
            nc.scalar.activation(res.bq_scaled[:, :], bank[7][:, C_BQ:C_BQ + 1], ACT.Copy,
                                 scale=HD ** -0.5).then_inc(cols_ready, 1)
            act.wait_ge(w_turned, 1)
            nc.scalar.activation(res.qkvT[:, 0:2 * DIM], bank[6][:, 0:2 * DIM], ACT.Copy).then_inc(w_copied, 1)
            nc.scalar.activation(res.proj[:, 0:VW], bank[6][:, 3 * DIM:3 * DIM + VW], ACT.Copy).then_inc(w_copied, 1)
            act.wait_ge(cols_ready, 2)
            project.take_turned(act, 0)
            for n in range(PAIRS_BEFORE + 1):
                if n + 1 < PAIRS_BEFORE:
                    project.take_turned(act, n + 1)
                if n < PAIRS_BEFORE:
                    for m in range(2):
                        project.take_qk(act, n, m)
                    project.part(act, n, 0)
                if n > 0:
                    project.part(act, n - 1, 1)
            act.wait_ge(wf_turned, 1)
            nc.scalar.activation(res.qkvT[:, 2 * DIM:3 * DIM], bank[6][:, 2 * DIM:3 * DIM],
                                 ACT.Copy).then_inc(wf_copied, 1)

        @block.tensor
        def _(pe):
            pe.wait_ge(ident_ready, 4)
            pe.wait_ge(weights_in, DMA * len(weights))
            nc.tensor.transpose(bank[7][:, 0:N_COLS], cols_n[:, :],
                                res.identf[0:N_COLS, 0:N_COLS]).then_inc(cols_turned, 1)
            for n, w in enumerate((wq_n, wk_n)):
                nc.tensor.transpose(bank[6][:, n * DIM:(n + 1) * DIM], w[:, :], res.identf[:, :])
            nc.tensor.transpose(bank[6][:, 3 * DIM:3 * DIM + VW], wv_n[:, :],
                                res.identf[0:VW, 0:VW]).then_inc(w_turned, 1)
            project.turn(pe, 0)
            project.turn(pe, 1)
            pe.wait_ge(w_copied, 2)
            project.qk(pe, 0)
            pe.wait_ge(sel_ready, 1)
            for k in range(QK * HEADS // P):
                last = nc.tensor.matmul(bank[5][:, k * SLOTS:(k + 1) * SLOTS], wqv_n[:, k, :], sel[:, :],
                                        start=True, stop=True)
            last.then_inc(ws_summed, 1)
            pe.wait_ge(selb_ready, 1)
            nc.tensor.matmul(bank[7][:, 128:128 + HEADS], ones[:, :], sel_b[:, :],
                             start=True, stop=True).then_inc(qsb_summed, 1)
            for n in range(1, PAIRS_BEFORE):
                if n + 1 < PAIRS_BEFORE:
                    project.turn(pe, n + 1)
                project.qk(pe, n)
                if n == 1:
                    pe.wait_ge(proj_ready, 2)
                project.values(pe, n - 1)
            project.values(pe, PAIRS_BEFORE - 1)
            pe.wait_ge(wf_in, DMA)
            nc.tensor.transpose(bank[6][:, 2 * DIM:3 * DIM], wf_n[:, :], res.identf[:, :]).then_inc(wf_turned, 1)

        @block.vector
        def _(dve):
            dve.memset(ones[:, :], 1.0)
            dve.memset(res.proj[:, VW + HEADS:P], 0.0).then_inc(proj_ready, 1)
            def moments(n, which):
                src, done = (res.x, res.y)[which], 2 * which + n + 1
                if which == 0:
                    dve.wait_ge(x_in[n], DMA)
                else:
                    dve.wait_ge(y_ready, n + 1)
                for t in range(cuts[n], cuts[n + 1]):
                    last = nc.vector.bn_stats(stats[:, t, :], src[:, t, :])
                last.then_inc(stats_done, 1)
                dve.wait_ge(stats_done, done)
                for t in range(cuts[n], cuts[n + 1]):
                    last = nc.vector.bn_aggr(moment[:, t, :], stats[:, t, :])
                last.then_inc(moments_done, 1)
                dve.wait_ge(moments_done, done)
                part = moment[:, cuts[n]:cuts[n + 1], 1]
                nc.vector.tensor_scalar(part, part, EPS, None, ALU.add).then_inc(var_ready, 1)

            def normalize(n, which):
                dve.wait_ge(rstd_ready, 2 * which + n + 1)
                for t in range(cuts[n], cuts[n + 1]):
                    dst = res.y[:, t, :] if which == 0 else project.z[t // PAIR][:, t % PAIR, :]
                    last = nc.vector.tensor_scalar(dst, (res.x, res.y)[which][:, t, :], moment[:, t, 0:1],
                                                   rstd[:, t:t + 1], ALU.subtract, ALU.mult)
                    if which == 1 and t % PAIR == PAIR - 1:
                        last.then_inc(project.z_ready, 1)
                if which == 0:
                    last.then_inc(y_ready, 1)

            for n in range(2):
                moments(n, 0)
            for n in range(2):
                normalize(n, 0)
                moments(n, 1)
            normalize(0, 1)
            dve.wait_ge(weights_in, DMA * len(weights))
            dve.wait_ge(ident_ready, 4)
            nc.vector.tensor_scalar(sel[:, :], sel[:, :], ws_col[:, 0:1], None, ALU.mult).then_inc(sel_ready, 1)
            normalize(1, 1)
            dve.wait_ge(cols_ready, 1)
            dve.wait_ge(sel_ready, 1)
            for k in range(QK * HEADS // P):
                last = nc.vector.tensor_scalar(sel_b[:, k * SLOTS:(k + 1) * SLOTS], sel[:, :],
                                               res.colsT[:, C_BQV + k:C_BQV + k + 1], None, ALU.mult)
            last.then_inc(selb_ready, 1)
            dve.wait_ge(ws_summed, 1)
            nc.vector.tensor_scalar(res.proj[:, VW:VW + HEADS], bank[5][:, 0:HEADS], QK ** -0.5, None,
                                    ALU.mult).then_inc(proj_ready, 1)
            project.rest(dve, 0, 0)
            dve.wait_ge(qsb_summed, 1)
            dve.wait_ge(rows_in, DMA * len(rows))
            nc.vector.tensor_scalar(res.qs_bias[:, :], bank[7][:, 128:128 + HEADS], QK ** -0.5,
                                    res.rows[:, R_BS:R_BS + 1], ALU.mult, ALU.add).then_inc(qsb_ready, 1)
            dve.wait_ge(qsb_ready, 1)
            for n in range(PAIRS_BEFORE):
                if n + 1 < PAIRS_BEFORE:
                    project.rest(dve, n + 1, 0)
                project.rest(dve, n, 1)
                project.take_values(dve, n, n * PAIR)


def attention(nc, res, mix, joined, ffw, a):
    ctx = ExitStack()
    with ctx:
        def sb(name, shape, dtype=FP32):
            return ctx.enter_context(nc.sbuf_tensor(name, shape, dtype))

        def pb(name, shape):
            return ctx.enter_context(nc.psum_tensor(name, shape, FP32))

        def sem(name):
            return ctx.enter_context(nc.semaphore(name))

        q_op, k_op, v_op, operands_in = res.q_op, res.k_op, res.v_op, res.operands_in
        prob = sb("prob", [P, TB, SEQ])
        pair = sb("pair", [P, TB // 2, SEQ])
        quad = sb("quad", [P, 2, SEQ])
        rowmax = sb("rowmax", [P, 2, TB, 2])
        negmax = sb("negmax", [P, TB])
        max_parts = sb("max_parts", [P, 2, MAX_PARTS, TB], BF16)
        max_rows = [sb(f"max_rows{n}", [MAX_PARTS * TB, P], BF16) for n in range(2)]
        onehot = sb("onehot", [P, SLOTS, 32])
        outT = [sb(f"outT{n}", [P, HALF]) for n in range(2)]
        denT = sb("denT", [P, HALF])

        col_bank = [pb(f"col_bank{n}", [P, HALF]) for n in range(2)]
        row_bank = [pb(f"row_bank{n}", [P, HALF]) for n in range(2)]
        out_bank = [pb(f"out_bank{n}", [P, HALF]) for n in range(2)]
        den_bank = pb("den_bank", [P, HALF])
        turn_bank = pb("turn_bank", [P, HALF])
        project = Projections(nc, ctx, res, "along", 1, turned=[turn_bank], qk=[turn_bank], v=[turn_bank])

        max_in = [sem(f"max_in{s}") for s in range(SLOTS)]
        onehot_set = sem("onehot_set")
        col_scored, row_scored = sem("col_scored"), sem("row_scored")
        exp_done, max_done, pv_done = sem("exp_done"), sem("max_done"), sem("pv_done")
        negmax_ready, part1_ready, max_split = sem("negmax_ready"), sem("part1_ready"), sem("max_split")
        max_turned, max_rows_ready = sem("max_turned"), sem("max_rows_ready")
        pair_done, quad_done, den_done = sem("pair_done"), sem("quad_done"), sem("den_done")
        outT_ready, out_turned, denT_ready = sem("outT_ready"), sem("out_turned"), sem("denT_ready")
        mix_in, mix_in_ready, att_done = mix.mix_in, mix.mix_in_ready, mix.att_done
        mix.turn_bank = turn_bank

        halves = lambda t: t.rearrange("p (c h i) -> p c h i", c=TB // 2, h=2)

        block = ctx.enter_context(nc.Block())

        @block.sync
        def _(sp):
            def put_max(w, slot, parity):
                sp.wait_ge(max_rows_ready, w + 1)
                sp.dma_start(q_op[slot][PROD_ROWS:ROWS, :].rearrange("m (t i) -> m t i", t=TB),
                             max_rows[parity][:, :]).then_inc(max_in[slot], DMA)

            def group(G, first, last, along):
                for s in range(SLOTS):
                    u = G * SLOTS + s
                    if s == 1 and not first and not last:
                        sp.wait_ge(project.stored, STORES * DMA * (G if along else PAIRS_ALONG))
                        sp.wait_ge(project.v_ready, G if along else PAIRS_ALONG)
                    if not (last and s >= 1):
                        if not (first and s == 0):
                            sp.wait_ge(pv_done, TB * u)
                        nxt = G if s < 1 else G + 1
                        res.load(sp, nxt * SLOTS + (s + 3) % SLOTS, nxt // GPB, (s + 3) % SLOTS)
                    if not (last and s == SLOTS - 1):
                        put_max(u + 1, (s + 1) % SLOTS, (s + 1) % 2)
                if along:
                    project.store(sp, G, G + PAIRS_BEFORE, True, range(PARTS), project.stored)

            for u in (1, 2):
                res.load(sp, u, 0, u)
            ffw.load(sp, a)
            put_max(0, 0, 0)
            group(0, True, False, True)
            with sp.Fori(1, PAIRS_ALONG) as G:
                group(G, False, False, True)
            with sp.Fori(PAIRS_ALONG, GROUPS - 1) as G:
                group(G, False, False, False)
            group(GROUPS - 1, False, True, False)

        @block.tensor
        def _(pe):
            def row_scores(v, slot, t, known_free):
                for h in range(2):
                    if not known_free:
                        pe.wait_ge(max_done, 2 * TB * v + 2 * t + h - 1)
                    nc.tensor.matmul(row_bank[h][:, :], q_op[slot][0:PROD_ROWS, t * P:(t + 1) * P],
                                     k_op[slot][0:PROD_ROWS, h * HALF:(h + 1) * HALF],
                                     start=True, stop=True).then_inc(row_scored, 1)

            def turn_max(w, parity):
                pe.wait_ge(max_split, w + 1)
                pe.wait_ge(max_rows_ready, w)
                nc.tensor.matmul(turn_bank[0:MAX_PARTS * TB, 0:P],
                                 max_parts[:, parity, :, :].rearrange("p m t -> p (m t)"),
                                 res.identb[:, :], start=True, stop=True).then_inc(max_turned, 1)

            def col_scores(u, slot, t, known_free):
                for h in range(2):
                    if not known_free:
                        pe.wait_ge(exp_done, 2 * TB * u + 2 * t + h - 1)
                    nc.tensor.matmul(col_bank[h][:, :], k_op[slot][0:ROWS, t * P:(t + 1) * P],
                                     q_op[slot][0:ROWS, h * HALF:(h + 1) * HALF],
                                     start=True, stop=True).then_inc(col_scored, 1)

            def values(u, slot, t):
                pe.wait_ge(exp_done, 2 * TB * u + 2 * t + 2)
                for ih in range(2):
                    last = nc.tensor.matmul(out_bank[slot % 2][ih * VW:(ih + 1) * VW, :], v_op[slot][:, t, :],
                                            halves(prob[:, t, :])[:, :, ih, :], start=(t == 0), stop=(t == TB - 1))
                last.then_inc(pv_done, 1)

            def denominators(u, slot):
                pe.wait_ge(quad_done, 4 * u + 4)
                for ih in range(2):
                    for k in range(2):
                        q = 32 * (2 * ih + k)
                        last = nc.tensor.matmul(den_bank[q:q + 32, :], onehot[:, slot, :],
                                                halves(quad[:, k, :])[:, :, ih, :],
                                                start=(slot == 0), stop=(slot == SLOTS - 1))
                last.then_inc(den_done, 1)

            def turn_out(u, parity):
                pe.wait_ge(outT_ready, u + 1)
                for c in range(TB // 2):
                    last = nc.tensor.transpose(out_bank[parity][:, c * P:(c + 1) * P],
                                               outT[parity][:, c * P:(c + 1) * P], res.identf[:, :])
                last.then_inc(out_turned, 1)

            def turn_den(G):
                pe.wait_ge(denT_ready, G + 1)
                for c in range(TB // 2):
                    last = nc.tensor.transpose(turn_bank[:, c * P:(c + 1) * P], denT[:, c * P:(c + 1) * P],
                                               res.identf[:, :])
                last.then_inc(mix.den_turned, 1)

            def group(G, first, last, along):
                for s in range(SLOTS):
                    u = G * SLOTS + s
                    before = not (first and s == 0)
                    ahead = not (last and s >= 2)
                    Gv, sv, sp_ = (G if s < 2 else G + 1), (s + 2) % SLOTS, (s - 1) % SLOTS
                    for t in range(TB):
                        if t == 0:
                            pe.wait_ge(max_in[s], DMA * (G + 1))
                        col_scores(u, s, t, not before and t == 0)
                        if ahead:
                            if t == 0:
                                pe.wait_ge(operands_in[sv], LOADS * DMA * (Gv + 1))
                            row_scores(u + 2, sv, t, False)
                        if t > 0:
                            if t == 1 and not (first and s < 2):
                                pe.wait_ge(mix_in_ready, u - 1)
                            values(u, s, t - 1)
                        elif before:
                            values(u - 1, sp_, TB - 1)
                        if t == 2 and not (last and s == SLOTS - 1):
                            if s == 1 and not first:
                                pe.wait_ge(mix.den_ready, G)
                            if s == 3 and along:
                                pe.wait_ge(project.v_ready, G + 1)
                            turn_max(u + 1, (s + 1) % 2)
                        if t == 2 and before:
                            turn_out(u - 1, sp_ % 2)
                        if t == 4 and before:
                            if s == 1 and not first:
                                pe.wait_ge(denT_ready, G)
                            denominators(u - 1, sp_)
                        if t == 6 and s == 0 and not first:
                            pe.wait_ge(max_rows_ready, u + 2)
                            turn_den(G - 1)
                        if along and (s, t) == (1, 6):
                            pe.wait_ge(max_rows_ready, u + 2)
                            project.turn(pe, G)
                        if last and (s, t) == (2, 0):
                            pe.wait_ge(max_done, 2 * TB * U)
                            ffw.turn_ternary(pe, row_bank)
                        if last and (s, t) == (2, 4):
                            ffw.sum_all(pe, row_bank)
                        if last and (s, t) == (2, 5):
                            ffw.turn_relu(pe, row_bank)
                        if last and (s, t) == (3, 3):
                            pe.wait_ge(ffw.scale_ready, 1)
                            joined.turn(pe, 0, row_bank[1])
                        if last and (s, t) == (3, 5):
                            pe.wait_ge(ffw.copied, 4)
                            joined.project(pe, 0, row_bank[0])
                        if along and (s, t) == (2, 4):
                            pe.wait_ge(max_rows_ready, u + 2)
                            project.qk(pe, G)
                        if along and (s, t) == (2, 6):
                            project.values(pe, G)

            pe.wait_ge(operands_in[0], LOADS * DMA)
            for t in range(TB):
                row_scores(0, 0, t, t == 0)
            pe.wait_ge(operands_in[1], LOADS * DMA)
            for t in range(TB):
                row_scores(1, 1, t, False)
                if t == 3:
                    pe.wait_ge(max_split, 1)
                    nc.tensor.matmul(turn_bank[0:MAX_PARTS * TB, 0:P],
                                     max_parts[:, 0, :, :].rearrange("p m t -> p (m t)"),
                                     res.identb[:, :], start=True, stop=True).then_inc(max_turned, 1)
            pe.wait_ge(onehot_set, 2)
            group(0, True, False, True)
            with pe.Fori(1, PAIRS_ALONG) as G:
                group(G, False, False, True)
            with pe.Fori(PAIRS_ALONG, GROUPS - 1) as G:
                group(G, False, False, False)
            group(GROUPS - 1, False, True, False)
            values(U - 1, SLOTS - 1, TB - 1)
            turn_out(U - 1, 1)
            denominators(U - 1, SLOTS - 1)
            turn_den(GROUPS - 1)

        @block.scalar
        def _(act):
            def take_out(u, parity):
                act.wait_ge(pv_done, TB * u + TB)
                nc.scalar.activation(outT[parity][:, :], out_bank[parity][:, :], ACT.Copy).then_inc(outT_ready, 1)

            def take_turned(u, G, slot):
                act.wait_ge(out_turned, u + 1)
                nc.scalar.activation(mix_in[:, ds(G % 2, 1), :, slot, :].rearrange("p g e w -> p (g e) w"),
                                     out_bank[slot % 2][:, :].rearrange("p (e w) -> p e w", w=VW),
                                     ACT.Copy).then_inc(mix_in_ready, 1)

            def take_den(G):
                act.wait_ge(den_done, SLOTS * G + SLOTS)
                nc.scalar.activation(denT[:, :], den_bank[:, :], ACT.Copy).then_inc(denT_ready, 1)

            def take_rows(w, parity, slot_before, G_before):
                act.wait_ge(max_turned, w + 1)
                if slot_before is not None:
                    act.wait_ge(max_in[slot_before], DMA * (G_before + 1))
                nc.scalar.activation(max_rows[parity][:, :], turn_bank[0:MAX_PARTS * TB, 0:P],
                                     ACT.Copy).then_inc(max_rows_ready, 1)

            def group(G, first, last, along):
                for s in range(SLOTS):
                    u = G * SLOTS + s
                    before = not (first and s == 0)
                    for t in range(TB):
                        for h in range(2):
                            if h == 0 and before:
                                act.wait_ge(pv_done, TB * u - TB + t + 1)
                                act.wait_ge(pair_done, TB // 2 * u - TB // 2 + t // 2 + 1)
                            act.wait_ge(col_scored, 2 * TB * u + 2 * t + h + 1)
                            nc.scalar.activation(prob[:, t, h * HALF:(h + 1) * HALF], col_bank[h][:, :],
                                                 ACT.Exp).then_inc(exp_done, 1)
                        if t == 2 and not (last and s == SLOTS - 1):
                            sent = s >= 1 or not first
                            take_rows(u + 1, (s + 1) % 2, (s - 1) % SLOTS if sent else None, G if s >= 1 else G - 1)
                        if t == 1 and before:
                            take_out(u - 1, (s - 1) % 2)
                        if t == 3 and before:
                            if s == 1 and not first:
                                act.wait_ge(att_done, G)
                            take_turned(u - 1, G if s > 0 else G - 1, (s - 1) % SLOTS)
                        if t == 5 and s == 0 and not first:
                            take_den(G - 1)
                        if t == 3 and s == 2 and not first:
                            mix.exps(act, G - 1)
                        if along and (s, t) == (1, 7):
                            project.take_turned(act, G)
                        if last and (s, t) == (2, 1):
                            ffw.take_ternary(act, row_bank)
                        if last and (s, t) == (2, 6):
                            ffw.take_relu(act, row_bank)
                        if last and (s, t) == (3, 2):
                            joined.copy(act, 0)
                        if last and (s, t) == (3, 4):
                            joined.take(act, 0, row_bank[1])
                        if along and (s, t) == (2, 5):
                            for m in range(2):
                                project.take_qk(act, G, m)
                        if along and (s, t) == (3, 0):
                            project.part(act, G, 0)
                        if along and (s, t) == (3, 4):
                            project.part(act, G, 1)

            take_rows(0, 0, None, 0)
            group(0, True, False, True)
            with act.Fori(1, PAIRS_ALONG) as G:
                group(G, False, False, True)
            with act.Fori(PAIRS_ALONG, GROUPS - 1) as G:
                group(G, False, False, False)
            group(GROUPS - 1, False, True, False)
            take_out(U - 1, 1)
            take_turned(U - 1, GROUPS - 1, SLOTS - 1)
            take_den(GROUPS - 1)

        @block.vector
        def _(dve):
            def row_max(v, parity, t, h):
                dve.wait_ge(row_scored, 2 * TB * v + 2 * t + h + 1)
                nc.vector.tensor_reduce(rowmax[:, parity, t, h:h + 1], row_bank[h][:, :], AX.X,
                                        ALU.max).then_inc(max_done, 1)

            def split_max(w, parity, step):
                if step == 0:
                    dve.wait_ge(max_done, 2 * TB * w + 2 * TB)
                    nc.vector.tensor_reduce(negmax[:, :], rowmax[:, parity, :, :], AX.X, ALU.max,
                                            negate=True).then_inc(negmax_ready, 1)
                elif step == 1:
                    dve.wait_ge(negmax_ready, w + 1)
                    nc.vector.tensor_copy(max_parts[:, parity, 0, :], negmax[:, :]).then_inc(part1_ready, 1)
                else:
                    dve.wait_ge(part1_ready, w + 1)
                    nc.vector.tensor_tensor(max_parts[:, parity, 1, :], negmax[:, :], max_parts[:, parity, 0, :],
                                            ALU.subtract).then_inc(max_split, 1)

            def quads(u, k, h, known_free):
                dve.wait_ge(pair_done, TB // 2 * u + 2 * k + 2)
                if not known_free:
                    dve.wait_ge(den_done, u)
                part = slice(h * HALF, (h + 1) * HALF)
                nc.vector.tensor_tensor(quad[:, k, part], pair[:, 2 * k, part], pair[:, 2 * k + 1, part],
                                        ALU.add).then_inc(quad_done, 1)

            PLAN = {
                (1, 0): [("denominators",)],
                (1, 1): [("logit sums", 0, 1)],
                (1, 2): [("logit sums", 1, 2)],
                (1, 4): [("logit sums", 2, 6)],
                (1, 6): [("logit sums", 6, 8)],
                (2, 0): [("logits over denominators",)],
                (2, 1): [("query part",)],
                (2, 2): [("maxima",)],
                (2, 3): [("shift",)],
                (2, 4): [("totals",), ("normalizers",)],
                (2, 5): [("weights",)],
                (3, 1): [("output", 0, 1)],
                (3, 2): [("output", 1, 2)],
                (3, 4): [("output", 2, 6)],
                (3, 6): [("output", 6, 8)],
            }

            def group(G, first, last, along):
                for s in range(SLOTS):
                    u = G * SLOTS + s
                    before = not (first and s == 0)
                    ahead = not (last and s >= 2)
                    for t in range(TB):
                        for h in range(2):
                            if ahead:
                                row_max(u + 2, s % 2, t, h)
                            if 2 * t + h < 3 and not (last and s == SLOTS - 1):
                                split_max(u + 1, (s + 1) % 2, 2 * t + h)
                        if t in (2, 3) and before:
                            quads(u - 1, 1, t - 2, first and s == 1)
                        if t in (5, 7):
                            quads(u, 0, (t - 5) // 2, first and s == 0)
                        if not first:
                            for step in PLAN.get((s, t), ()):
                                mix.step(dve, G - 1, (G - 1) // GPB, (G - 1) % GPB, *step)
                        if last and (s, t) == (2, 2):
                            ffw.sum_rows(dve)
                        if last and (s, t) == (2, 5):
                            ffw.scales(dve, row_bank)
                        if last and (s, t) in ((2, 6), (2, 7)):
                            ffw.ternary(dve, t - 6)
                        if last and (s, t) == (3, 7):
                            joined.add(dve, 0, row_bank[0])
                        if along:
                            tile = (G + PAIRS_BEFORE) * PAIR
                            if (s, t) == (0, 0):
                                project.stats(dve, G, tile, 0)
                            elif (s, t) == (0, 1):
                                project.moments(dve, G, 0)
                            elif (s, t) == (0, 4):
                                project.normalize(dve, G, tile, 0)
                            elif (s, t) == (0, 5):
                                project.stats(dve, G, tile, 1)
                            elif (s, t) == (0, 6):
                                project.moments(dve, G, 1)
                            elif (s, t) == (1, 3):
                                project.normalize(dve, G, tile, 1)
                            elif (s, t) == (3, 0):
                                project.take_values(dve, G, tile)

            dve.memset(ffw.ones[:, :], 1.0)
            dve.sem_inc(att_done, 1)
            dve.memset(onehot[:, :, :], 0.0).then_inc(onehot_set, 1)
            dve.wait_ge(onehot_set, 1)
            for s in range(SLOTS):
                last = dve.memset(onehot[:, s, s:s + 1], 1.0)
            last.then_inc(onehot_set, 1)
            for v in range(2):
                for t in range(TB):
                    for h in range(2):
                        row_max(v, v, t, h)
                if v == 0:
                    for step in range(3):
                        split_max(0, 0, step)
            group(0, True, False, True)
            with dve.Fori(1, PAIRS_ALONG) as G:
                group(G, False, False, True)
            with dve.Fori(PAIRS_ALONG, GROUPS - 1) as G:
                group(G, False, False, False)
            group(GROUPS - 1, False, True, False)
            quads(U - 1, 1, 0, False)
            quads(U - 1, 1, 1, False)
            joined.norm.normalize(dve, 0)
            mix.step(dve, GROUPS - 1, BATCH - 1, GPB - 1, "denominators")

        @block.gpsimd
        def _(pool):
            def pairs(u, k, known_free):
                pool.wait_ge(exp_done, 2 * TB * u + 4 * k + 4)
                if not known_free:
                    pool.wait_ge(quad_done, 4 * u - 2 + 2 * (k // 2))
                pool.tensor_tensor(pair[:, k, :], prob[:, 2 * k, :], prob[:, 2 * k + 1, :],
                                   ALU.add).then_inc(pair_done, 1)

            def group(G, first, along):
                for s in range(SLOTS):
                    u = G * SLOTS + s
                    for k in range(TB // 2):
                        pairs(u, k, first and s == 0)
                        if along and s == 0 and k == 0:
                            project.rstd_of(pool, G, 0)
                        if k == 1 and s == 0 and not first:
                            mix.logit_products(pool, G - 1)
                        if along and s == 0 and k == 2:
                            project.rstd_of(pool, G, 1)
                        if along and s == 1 and k == 2:
                            project.add_biases(pool, G, (G + PAIRS_BEFORE) * PAIR)
                        if k == 2 and s == 2 and not first:
                            mix.mix(pool, G - 1)
                        if along and s == 3 and k in (0, 2):
                            project.rest(pool, G, k // 2)

            for all_, row in ((res.y, R_BF), (res.x, R_BR2)):
                t = all_[:, 0:PAIR * PAIRS_BEFORE, :]
                pool.tensor_tensor(t, t, again(res.rows[:, row:row + DIM], PAIR * PAIRS_BEFORE), ALU.add)
            group(0, True, True)
            with pool.Fori(1, PAIRS_ALONG) as G:
                group(G, False, True)
            with pool.Fori(PAIRS_ALONG, GROUPS) as G:
                group(G, False, False)
            joined.norm.root(pool, 0)


def feed_forward(nc, res, mix, joined, ffw, out):
    ctx = ExitStack()
    with ctx:
        def sb(name, shape, dtype=FP32):
            return ctx.enter_context(nc.sbuf_tensor(name, shape, dtype))

        def sem(name):
            return ctx.enter_context(nc.semaphore(name))

        T, N = BLOCK_TILES, BLOCKS
        HT, FT = HIDDEN // P, FF // P
        LAG = 3
        G = GROUPS - 1
        norm2, norm3 = joined.norm, BlockNorm(nc, ctx, res, "norm3", res.x)
        onT, hT = sb("onT", [P, HALF]), sb("hT", [P, HT, HALF])
        x3nT, gT = sb("x3nT", [P, HALF]), sb("gT", [P, FT, HALF])
        y_out = sb("y_out", [P, T, DIM])

        psum = lambda name: ctx.enter_context(nc.psum_tensor(name, [P, HALF], FP32))
        turn_bank, turn2_bank = psum("ff_turn_bank"), psum("ff_turn2_bank")
        mid_bank, down_bank = psum("mid_bank"), psum("down_bank")
        wide = [psum(f"wide{n}") for n in range(FT)]

        hidden_done, reduced, up_done, down_done = (sem("hidden_done"), sem("reduced"), sem("up_done"),
                                                    sem("down_done"))
        onT_ready, hT_ready, x3nT_ready, gelu_done = (sem("onT_ready"), sem("hT_ready"), sem("x3nT_ready"),
                                                      sem("gelu_done"))
        x3_part, x3_ready, fb2_added = sem("x3_part"), sem("x3_ready"), sem("fb2_added")
        y_ready, y_stored = sem("y_ready"), sem("y_stored")
        stood = sem("fed_stood")
        block = ctx.enter_context(nc.Block())

        def live(j):
            return not isinstance(j, int) or 0 <= j < N

        def steps(engine, step, extra=None):
            for k in range(1, LAG + 1):
                step(k)
                if extra:
                    extra(k)
            with engine.Fori(LAG + 1, N) as k:
                step(k)
            for k in range(N, N + LAG):
                step(k)

        @block.sync
        def _(sp):
            rows = out.rearrange("b (t p) d -> (b t) p d", p=P)

            def step(k):
                if live(k - 3):
                    sp.wait_ge(y_ready, k - 2)
                    sp.dma_start(rows[ds((k - 3) * T, T)].rearrange("t p d -> p t d"),
                                 y_out[:, :, :]).then_inc(y_stored, DMA)

            steps(sp, step)
            sp.wait_ge(y_stored, DMA * N)

        @block.gpsimd
        def _(pool):
            def add_fb2(j):
                pool.wait_ge(norm3.ready, j + 1).then_inc(stood, 1)
                x = block_tiles(res.x, j)
                pool.tensor_tensor(x, x, again(res.rows[:, R_FB2:R_FB2 + DIM], T), ALU.add).then_inc(fb2_added, 1)

            def step(k):
                if live(k - 2):
                    norm3.root(pool, k - 2)
                if live(k):
                    norm2.root(pool, k)
                if live(k - 2):
                    add_fb2(k - 2)

            def extra(k):
                if k == 3:
                    mix.mix(pool, G)

            mix.logit_products(pool, G)
            steps(pool, step, extra)

        @block.tensor
        def _(pe):
            def up(j):
                for f in range(FT):
                    if f == 0:
                        pe.wait_ge(x3nT_ready, j + 1)
                    nc.tensor.matmul(wide[f][:, :], ffw.w1T[:, f * P:(f + 1) * P], x3nT[:, :],
                                     start=True, stop=True).then_inc(up_done, 1)

            def down(j):
                pe.wait_ge(gelu_done, FT * j + FT)
                if not isinstance(j, int) or j > 0:
                    pe.wait_ge(y_ready, j)
                for c in range(T):
                    for f in range(FT):
                        last = nc.tensor.matmul(down_bank[:, c * P:(c + 1) * P], gT[:, f, c * P:(c + 1) * P],
                                                ffw.w2T[:, f * P:(f + 1) * P], start=(f == 0), stop=(f == FT - 1))
                last.then_inc(down_done, 1)

            def hidden(j):
                pe.wait_ge(onT_ready, j + 1)
                for f in range(HT):
                    nc.tensor.matmul(wide[f][:, :], ffw.wr1T[:, f * P:(f + 1) * P], onT[:, :],
                                     start=True, stop=True).then_inc(hidden_done, 1)

            def reduce(j):
                pe.wait_ge(hT_ready, HT * j + HT)
                if live(j + 1):
                    pe.wait_ge(joined.x2_ready, j + 2)
                for c in range(T):
                    for f in range(HT):
                        last = nc.tensor.matmul(mid_bank[:, c * P:(c + 1) * P], hT[:, f, c * P:(c + 1) * P],
                                                ffw.wr2T[:, f * P:(f + 1) * P], start=(f == 0), stop=(f == HT - 1))
                last.then_inc(reduced, 1)

            def step(k):
                if live(k - 3):
                    up(k - 3)
                if live(k):
                    if not isinstance(k, int) or k > 2:
                        pe.wait_ge(x3nT_ready, k - 2)
                    joined.turn(pe, k, turn_bank)
                if live(k - 1):
                    norm2.turn(pe, k - 1, turn2_bank)
                if live(k):
                    if not isinstance(k, int) or k > 1:
                        pe.wait_ge(x3_part, k - 1)
                    joined.project(pe, k, mid_bank)
                if live(k - 3):
                    down(k - 3)
                if live(k - 1):
                    hidden(k - 1)
                if live(k - 2):
                    norm3.turn(pe, k - 2, turn_bank)
                if live(k - 1):
                    reduce(k - 1)

            steps(pe, step)

        @block.scalar
        def _(act):
            def gelu(j):
                for f in range(FT):
                    act.wait_ge(up_done, FT * j + f + 1)
                    nc.scalar.activation(gT[:, f, :], wide[f][:, :], ACT.Gelu,
                                         bias=res.colsT[:, C_FB1 + f:C_FB1 + f + 1]).then_inc(gelu_done, 1)

            def relu(j):
                for f in range(HT):
                    act.wait_ge(hidden_done, HT * j + f + 1)
                    nc.scalar.activation(hT[:, f, :], wide[f][:, :], ACT.Relu,
                                         bias=res.colsT[:, C_BR1 + f:C_BR1 + f + 1]).then_inc(hT_ready, 1)

            def step(k):
                if live(k):
                    joined.copy(act, k)
                if live(k - 3):
                    gelu(k - 3)
                if live(k):
                    joined.take(act, k, turn_bank)
                if live(k - 1):
                    act.wait_ge(norm2.turned, k)
                    nc.scalar.activation(onT[:, :], turn2_bank[:, :], ACT.Identity,
                                         bias=res.colsT[:, C_B2:C_B2 + 1],
                                         scale=res.colsT[:, C_G2:C_G2 + 1]).then_inc(onT_ready, 1)
                    relu(k - 1)
                if live(k - 2):
                    act.wait_ge(norm3.turned, k - 1)
                    nc.scalar.activation(x3nT[:, :], turn_bank[:, :], ACT.Copy).then_inc(x3nT_ready, 1)

            def extra(k):
                if k == 2:
                    mix.exps(act, G)

            steps(act, step, extra)

        @block.vector
        def _(dve):
            def fed(j):
                dve.wait_ge(reduced, j + 1)
                x, y = block_tiles(res.x, j), block_tiles(res.y, j)
                nc.vector.tensor_tensor(y, split(mid_bank), y, ALU.add).then_inc(x3_part, 1)
                dve.wait_ge(x3_part, j + 1)
                nc.vector.tensor_tensor(x, x, y, ALU.add).then_inc(x3_ready, 1)
                dve.wait_ge(x3_ready, j + 1).then_inc(stood, 1)
                norm3.moments(dve, j)

            def result(j):
                dve.wait_ge(down_done, j + 1)
                dve.wait_ge(fb2_added, j + 1)
                if not isinstance(j, int) or j > 0:
                    dve.wait_ge(y_stored, DMA * j)
                nc.vector.tensor_tensor(y_out[:, :, :], split(down_bank), block_tiles(res.x, j),
                                        ALU.add).then_inc(y_ready, 1)

            MIXING = {(1, "end"): ["logit sums"],
                      (2, 3): ["logits over denominators", "query part"],
                      (2, 2): ["maxima", "shift"],
                      (3, 3): ["totals", "normalizers"],
                      (3, 2): ["weights"],
                      (3, "end"): ["output"]}

            def mixing(k, place):
                if isinstance(k, int):
                    for what in MIXING.get((k, place), ()):
                        mix.step(dve, G, BATCH - 1, GPB - 1, what)

            def step(k):
                if live(k - 2):
                    fed(k - 2)
                    mixing(k, 3)
                    norm3.normalize(dve, k - 2)
                if live(k):
                    joined.add(dve, k, mid_bank)
                    mixing(k, 2)
                if live(k - 3):
                    result(k - 3)
                if live(k):
                    norm2.normalize(dve, k)
                mixing(k, "end")

            steps(dve, step)


def build(nc, args, out):
    ctx = ExitStack()
    with ctx:
        res = Resident(nc, ctx)
        prepare(nc, res, args)
        mix = Mixing(nc, ctx, res)
        ffw = FeedForwardWeights(nc, ctx, res)
        joined = AttentionOutput(nc, ctx, res, mix)
        attention(nc, res, mix, joined, ffw, args)
        feed_forward(nc, res, mix, joined, ffw, out)


_NAMES = {
    "L0_attn_x": "x", "L0_attn_Wq": "Wq", "L0_attn_bq": "bq", "L0_attn_Wk": "Wk", "L0_attn_bk": "bk",
    "L0_attn_Wv": "Wv", "L0_attn_bv": "bv", "L0_attn_Wqv": "Wqv", "L0_attn_bqv": "bqv", "L0_attn_Ws": "Ws",
    "L0_attn_bs": "bs", "L0_attn_Wf": "Wf", "L0_attn_bf": "bf", "L0_attn_Wr1": "Wr1", "L0_attn_br1": "br1",
    "L0_attn_Wr2": "Wr2", "L0_attn_br2": "br2", "L0_attn_g1": "g1", "L0_attn_b1": "b1", "L0_attn_g2": "g2",
    "L0_attn_b2": "b2", "L0_ffn_W1": "W1", "L0_ffn_b1": "fb1", "L0_ffn_W2": "W2", "L0_ffn_b2": "fb2",
}


def kernel(**inputs):
    import numpy as _np
    import concourse.bacc as _bacc
    from concourse import mybir as _mybir
    from concourse.bass_utils import run_bass_kernel_spmd as _run

    nc = _bacc.Bacc("TRN2", target_bir_lowering=False, num_devices=1)
    arrays, args = {}, {}
    for name, short in _NAMES.items():
        arr = _np.ascontiguousarray(inputs[name])
        arrays[f"in_{name}"] = arr
        args[short] = nc.dram_tensor(f"in_{name}", arr.shape, _mybir.dt.from_np(arr.dtype), kind="ExternalInput").ap()
    out = nc.dram_tensor("out", (BATCH, SEQ, DIM), _mybir.dt.float32, kind="ExternalOutput").ap()
    build(nc, args, out)
    r = _run(nc, [arrays], core_ids=[0])
    return r.results[0]["out"]
```
